# Optimizing a Trainium2 kernel written in Bass

```python
import numpy as np
import jax
import jax.numpy as jnp

def _softmax(x, axis=-1):
    return jax.nn.softmax(x, axis=axis)
def _gelu(x):
    return jax.nn.gelu(x, approximate=True)
def _silu(x):
    return jax.nn.silu(x)
def _sigmoid(x):
    return jax.nn.sigmoid(x)
def _layernorm(x, axis=-1, eps=1e-5):
    m = jnp.mean(x, axis=axis, keepdims=True)
    v = jnp.var(x, axis=axis, keepdims=True)
    return (x - m) / jnp.sqrt(v + eps)
def _scatter_add(tgt, idx, src, axis=0):
    return tgt.at[idx].add(src)
def _segment_sum(src, seg, n):
    return jax.ops.segment_sum(src, seg, n)

kernel_name = 'mk_adj_ffn_d1_adj_256_cbff4e'

def setup_inputs(seed: int = 0):
    np.random.seed(seed)
    _w = jnp.asarray
    def _rec_inputs():
        import jax
        import jax.numpy as jnp
        _gk = jax.random.key(seed)
        x = -0.000929 + 1 * jax.random.normal(jax.random.fold_in(_gk, 1), (8192, 256), jnp.float32)
        _a = jax.random.bernoulli(jax.random.fold_in(_gk, 2), 0.000488281, (8192, 8192))
        _a = jnp.logical_or(_a, jnp.swapaxes(_a, -1, -2))
        _a = jnp.logical_or(_a, jnp.eye(8192, dtype=bool))
        _af = _a.astype(jnp.float32)
        _af = _af * jax.random.uniform(jax.random.fold_in(_gk, 3), (8192, 8192), jnp.float32, 0.05, 1)
        adj = _af
        return x, adj
    x, adj = _rec_inputs()
    def _L0_gnn_setup():
        import jax, jax.numpy as jnp
        import numpy as np
        N = 4096
        IN = 256
        H = 8
        D = 32
        ALPHA = 0.2
        key = jax.random.key(seed)
        ks = jax.random.split(key, 9)
        xav = lambda k, sh: jax.random.normal(k, sh, jnp.float32) * np.float32(np.sqrt(2.0 / (sh[0] + sh[-1])))
        return {'x': jax.random.normal(ks[0], (N, IN), jnp.float32), 'adj_matrix': jax.random.uniform(ks[1], (N, N), jnp.float32), 'W': xav(ks[2], (H * D, IN)), 'We': xav(ks[3], (H, 1)), 'be': jnp.zeros((H,), jnp.float32), 'a_src': xav(ks[4], (H, D)), 'a_dst': xav(ks[5], (H, D)), 'Wr': xav(ks[6], (H * D, IN)), 'br': jnp.zeros((H * D,), jnp.float32)}
    _L0_gnn_all = _L0_gnn_setup()
    _L0_gnn_in = {k: v for k, v in _L0_gnn_all.items() if k in ('W', 'We', 'be', 'a_src', 'a_dst', 'Wr', 'br', )}
    del _L0_gnn_all

    def _L0_ffn_setup():
        import jax, jax.numpy as jnp
        import numpy as np
        H, P, G, NS, K = (8, 64, 64, 64, 3)
        D_INNER = H * P
        CONV_DIM = D_INNER + 2 * NS
        D_IN_PROJ = 2 * D_INNER + 2 * NS + 2 * H

        def _hydra(u, in_w, conv_w, conv_b, dt_bias, A_log, Dp, fcD_w, norm_w, out_w):
            Bt, L, _ = u.shape
            zxbcdt = u @ in_w.T
            z = zxbcdt[..., :D_INNER]
            xBC = zxbcdt[..., D_INNER:D_INNER + CONV_DIM]
            dt = zxbcdt[..., -2 * H:]
            dt = jnp.concatenate([dt[..., :H], jnp.flip(dt[..., H:], axis=1)], axis=0)
            dt = jax.nn.softplus(dt + dt_bias)
            xp = jnp.pad(xBC, ((0, 0), (K - 1, 0), (0, 0)))
            xBC = sum((xp[:, k:k + L, :] * conv_w[:, k] for k in range(K))) + conv_b
            xBC = jax.nn.silu(xBC)
            x = xBC[..., :D_INNER]
            Bm = xBC[..., D_INNER:D_INNER + NS]
            Cm = xBC[..., D_INNER + NS:]
            x_og = x
            x2 = jnp.concatenate([x, jnp.flip(x, 1)], 0).reshape(2 * Bt, L, H, P)
            B2 = jnp.concatenate([Bm, jnp.flip(Bm, 1)], 0)
            C2 = jnp.concatenate([Cm, jnp.flip(Cm, 1)], 0)
            dA = jnp.exp(dt * -jnp.exp(A_log))
            dBx = jnp.einsum('blh,bln,blhp->blhpn', dt, B2, x2)

            def step(h, inp):
                dA_t, dBx_t, C_t = inp
                h = h * dA_t[:, :, None, None] + dBx_t
                return (h, jnp.einsum('bhpn,bn->bhp', h, C_t))
            h0 = jnp.zeros((2 * Bt, H, P, NS), u.dtype)
            _, ys = jax.lax.scan(step, h0, (dA.transpose(1, 0, 2), dBx.transpose(1, 0, 2, 3, 4), C2.transpose(1, 0, 2)))
            y = ys.transpose(1, 0, 2, 3).reshape(2 * Bt, L, D_INNER)
            y_fw, y_bw = (y[:Bt], jnp.flip(y[Bt:], 1))
            y = jnp.pad(y_fw[:, :-1], ((0, 0), (1, 0), (0, 0))) + jnp.pad(y_bw[:, 1:], ((0, 0), (0, 1), (0, 0)))
            y = y + x_og * jnp.repeat(x_og @ fcD_w.T + Dp, P, axis=-1)
            yg = y * jax.nn.silu(z)
            yg = yg * jax.lax.rsqrt(jnp.mean(jnp.square(yg), -1, keepdims=True) + 1e-05) * norm_w
            return yg @ out_w.T
        key = jax.random.key(seed)
        ks = jax.random.split(key, 10)
        dim, Bsz, N = (256, 4, 8192)
        s = 0.02
        return {'x': jax.random.normal(ks[0], (Bsz, N, dim), jnp.float32), 'W_fx': jax.random.normal(ks[1], (D_INNER, dim), jnp.float32) * s, 'b_fx': jnp.zeros((D_INNER,), jnp.float32), 'W_x': jax.random.normal(ks[2], (D_INNER, dim), jnp.float32) * s, 'b_x': jnp.zeros((D_INNER,), jnp.float32), 'W_slice': jax.random.normal(ks[3], (G, P), jnp.float32) * s, 'b_slice': jnp.zeros((G,), jnp.float32), 'temperature': jnp.full((1, H, 1, 1), 0.5, jnp.float32), 'hy_in_w': jax.random.normal(ks[4], (D_IN_PROJ, D_INNER), jnp.float32) * s, 'hy_conv_w': jax.random.normal(ks[5], (CONV_DIM, K), jnp.float32) * s, 'hy_conv_b': jnp.zeros((CONV_DIM,), jnp.float32), 'hy_dt_bias': jnp.log(jnp.expm1(jnp.full((H,), 0.01, jnp.float32))), 'hy_A_log': jnp.log(jnp.linspace(1.0, 16.0, H)).astype(jnp.float32), 'hy_D': jnp.ones((H,), jnp.float32), 'hy_fcD_w': jax.random.normal(ks[6], (H, D_INNER), jnp.float32) * s, 'hy_norm_w': jnp.ones((D_INNER,), jnp.float32), 'hy_out_w': jax.random.normal(ks[7], (D_INNER, D_INNER), jnp.float32) * s, 'out_w': jax.random.normal(ks[8], (dim, D_INNER), jnp.float32) * s, 'out_b': jnp.zeros((dim,), jnp.float32)}
    _L0_ffn_all = _L0_ffn_setup()
    _L0_ffn_in = {k: v for k, v in _L0_ffn_all.items() if k in ('W_fx', 'b_fx', 'W_x', 'b_x', 'W_slice', 'b_slice', 'temperature', 'hy_in_w', 'hy_conv_w', 'hy_conv_b', 'hy_dt_bias', 'hy_A_log', 'hy_D', 'hy_fcD_w', 'hy_norm_w', 'hy_out_w', 'out_w', 'out_b', )}
    del _L0_ffn_all

    return {
        "x": x,
        "adj": adj,
        "L0_gnn_W": _L0_gnn_in["W"],
        "L0_gnn_We": _L0_gnn_in["We"],
        "L0_gnn_be": _L0_gnn_in["be"],
        "L0_gnn_a_src": _L0_gnn_in["a_src"],
        "L0_gnn_a_dst": _L0_gnn_in["a_dst"],
        "L0_gnn_Wr": _L0_gnn_in["Wr"],
        "L0_gnn_br": _L0_gnn_in["br"],
        "L0_ffn_W_fx": _L0_ffn_in["W_fx"],
        "L0_ffn_b_fx": _L0_ffn_in["b_fx"],
        "L0_ffn_W_x": _L0_ffn_in["W_x"],
        "L0_ffn_b_x": _L0_ffn_in["b_x"],
        "L0_ffn_W_slice": _L0_ffn_in["W_slice"],
        "L0_ffn_b_slice": _L0_ffn_in["b_slice"],
        "L0_ffn_temperature": _L0_ffn_in["temperature"],
        "L0_ffn_hy_in_w": _L0_ffn_in["hy_in_w"],
        "L0_ffn_hy_conv_w": _L0_ffn_in["hy_conv_w"],
        "L0_ffn_hy_conv_b": _L0_ffn_in["hy_conv_b"],
        "L0_ffn_hy_dt_bias": _L0_ffn_in["hy_dt_bias"],
        "L0_ffn_hy_A_log": _L0_ffn_in["hy_A_log"],
        "L0_ffn_hy_D": _L0_ffn_in["hy_D"],
        "L0_ffn_hy_fcD_w": _L0_ffn_in["hy_fcD_w"],
        "L0_ffn_hy_norm_w": _L0_ffn_in["hy_norm_w"],
        "L0_ffn_hy_out_w": _L0_ffn_in["hy_out_w"],
        "L0_ffn_out_w": _L0_ffn_in["out_w"],
        "L0_ffn_out_b": _L0_ffn_in["out_b"],
    }

def reference(x, adj, L0_gnn_W, L0_gnn_We, L0_gnn_be, L0_gnn_a_src, L0_gnn_a_dst, L0_gnn_Wr, L0_gnn_br, L0_ffn_W_fx, L0_ffn_b_fx, L0_ffn_W_x, L0_ffn_b_x, L0_ffn_W_slice, L0_ffn_b_slice, L0_ffn_temperature, L0_ffn_hy_in_w, L0_ffn_hy_conv_w, L0_ffn_hy_conv_b, L0_ffn_hy_dt_bias, L0_ffn_hy_A_log, L0_ffn_hy_D, L0_ffn_hy_fcD_w, L0_ffn_hy_norm_w, L0_ffn_hy_out_w, L0_ffn_out_w, L0_ffn_out_b):
    import jax
    import jax.numpy as jnp
    def _L0_gnn_ref(x, adj_matrix, W, We, be, a_src, a_dst, Wr, br):
        import jax, jax.numpy as jnp
        import numpy as np
        N = 4096
        IN = 256
        H = 8
        D = 32
        ALPHA = 0.2
        n = x.shape[0]
        h = (x @ W.T).reshape(n, H, D)
        s_src = jnp.einsum('nhd,hd->nh', h, a_src)
        s_dst = jnp.einsum('nhd,hd->nh', h, a_dst)
        attn = s_src[:, None, :] + s_dst[None, :, :]
        attn = attn + adj_matrix[:, :, None] * We[:, 0] + be
        mask = (adj_matrix > 0)[:, :, None]
        attn = jnp.where(mask, attn, -jnp.inf)
        attn = jax.nn.leaky_relu(attn, ALPHA)
        attn = jax.nn.softmax(attn, axis=1)
        h_out = jnp.einsum('ijh,jhd->ihd', attn, h).reshape(n, H * D)
        return h_out + x @ Wr.T + br

    def _L0_ffn_ref(x, W_fx, b_fx, W_x, b_x, W_slice, b_slice, temperature, hy_in_w, hy_conv_w, hy_conv_b, hy_dt_bias, hy_A_log, hy_D, hy_fcD_w, hy_norm_w, hy_out_w, out_w, out_b):
        import jax, jax.numpy as jnp
        import numpy as np
        H, P, G, NS, K = (8, 64, 64, 64, 3)
        D_INNER = H * P
        CONV_DIM = D_INNER + 2 * NS
        D_IN_PROJ = 2 * D_INNER + 2 * NS + 2 * H

        def _hydra(u, in_w, conv_w, conv_b, dt_bias, A_log, Dp, fcD_w, norm_w, out_w):
            Bt, L, _ = u.shape
            zxbcdt = u @ in_w.T
            z = zxbcdt[..., :D_INNER]
            xBC = zxbcdt[..., D_INNER:D_INNER + CONV_DIM]
            dt = zxbcdt[..., -2 * H:]
            dt = jnp.concatenate([dt[..., :H], jnp.flip(dt[..., H:], axis=1)], axis=0)
            dt = jax.nn.softplus(dt + dt_bias)
            xp = jnp.pad(xBC, ((0, 0), (K - 1, 0), (0, 0)))
            xBC = sum((xp[:, k:k + L, :] * conv_w[:, k] for k in range(K))) + conv_b
            xBC = jax.nn.silu(xBC)
            x = xBC[..., :D_INNER]
            Bm = xBC[..., D_INNER:D_INNER + NS]
            Cm = xBC[..., D_INNER + NS:]
            x_og = x
            x2 = jnp.concatenate([x, jnp.flip(x, 1)], 0).reshape(2 * Bt, L, H, P)
            B2 = jnp.concatenate([Bm, jnp.flip(Bm, 1)], 0)
            C2 = jnp.concatenate([Cm, jnp.flip(Cm, 1)], 0)
            dA = jnp.exp(dt * -jnp.exp(A_log))
            dBx = jnp.einsum('blh,bln,blhp->blhpn', dt, B2, x2)

            def step(h, inp):
                dA_t, dBx_t, C_t = inp
                h = h * dA_t[:, :, None, None] + dBx_t
                return (h, jnp.einsum('bhpn,bn->bhp', h, C_t))
            h0 = jnp.zeros((2 * Bt, H, P, NS), u.dtype)
            _, ys = jax.lax.scan(step, h0, (dA.transpose(1, 0, 2), dBx.transpose(1, 0, 2, 3, 4), C2.transpose(1, 0, 2)))
            y = ys.transpose(1, 0, 2, 3).reshape(2 * Bt, L, D_INNER)
            y_fw, y_bw = (y[:Bt], jnp.flip(y[Bt:], 1))
            y = jnp.pad(y_fw[:, :-1], ((0, 0), (1, 0), (0, 0))) + jnp.pad(y_bw[:, 1:], ((0, 0), (0, 1), (0, 0)))
            y = y + x_og * jnp.repeat(x_og @ fcD_w.T + Dp, P, axis=-1)
            yg = y * jax.nn.silu(z)
            yg = yg * jax.lax.rsqrt(jnp.mean(jnp.square(yg), -1, keepdims=True) + 1e-05) * norm_w
            return yg @ out_w.T
        B, N, _ = x.shape
        fx = (x @ W_fx.T + b_fx).reshape(B, N, H, P).transpose(0, 2, 1, 3)
        xm = (x @ W_x.T + b_x).reshape(B, N, H, P).transpose(0, 2, 1, 3)
        temp = jnp.maximum(temperature, 1e-06)
        sw = jax.nn.softmax((xm @ W_slice.T + b_slice) / temp, axis=-1)
        snorm = sw.sum(2)
        st = jnp.einsum('bhnc,bhng->bhgc', fx, sw) / (snorm + 1e-05)[..., None]
        st = st.transpose(0, 2, 1, 3).reshape(B, G, D_INNER)
        ot = _hydra(st, hy_in_w, hy_conv_w, hy_conv_b, hy_dt_bias, hy_A_log, hy_D, hy_fcD_w, hy_norm_w, hy_out_w)
        ot = ot.reshape(B, G, H, P).transpose(0, 2, 1, 3)
        out = jnp.einsum('bhgc,bhng->bhnc', ot, sw).transpose(0, 2, 1, 3).reshape(B, N, D_INNER)
        return out @ out_w.T + out_b

    x = x + _L0_gnn_ref(_layernorm(x, axis=-1), adj, L0_gnn_W, L0_gnn_We, L0_gnn_be, L0_gnn_a_src, L0_gnn_a_dst, L0_gnn_Wr, L0_gnn_br)
    x = x + _L0_ffn_ref((_layernorm(x, axis=-1))[None], L0_ffn_W_fx, L0_ffn_b_fx, L0_ffn_W_x, L0_ffn_b_x, L0_ffn_W_slice, L0_ffn_b_slice, L0_ffn_temperature, L0_ffn_hy_in_w, L0_ffn_hy_conv_w, L0_ffn_hy_conv_b, L0_ffn_hy_dt_bias, L0_ffn_hy_A_log, L0_ffn_hy_D, L0_ffn_hy_fcD_w, L0_ffn_hy_norm_w, L0_ffn_hy_out_w, L0_ffn_out_w, L0_ffn_out_b)[0]
    return x


_drawn_inputs = setup_inputs


def setup_inputs(seed=0):
    import zlib

    import numpy as np

    out = dict(_drawn_inputs(seed))
    spreads = {'L0_gnn_be': (0.0, 0.8),
     'L0_gnn_br': (0.0, 0.1),
     'L0_ffn_b_fx': (0.0, 0.1),
     'L0_ffn_b_x': (0.0, 0.8),
     'L0_ffn_b_slice': (0.0, 0.8),
     'L0_ffn_temperature': (0.5, 0.6),
     'L0_ffn_hy_conv_b': (0.0, 0.1),
     'L0_ffn_hy_dt_bias': (-4.600166320800781, 0.6),
     'L0_ffn_hy_D': (1.0, 0.6),
     'L0_ffn_hy_norm_w': (1.0, 0.6),
     'L0_ffn_out_b': (0.0, 0.1)}
    factors = {'L0_ffn_W_fx': 3.008,
     'L0_ffn_W_x': 8.0,
     'L0_ffn_W_slice': 8.0,
     'L0_ffn_hy_conv_w': 8.0,
     'L0_ffn_hy_A_log': 8.0,
     'L0_ffn_hy_fcD_w': 8.0}
    for name, (base, spread) in spreads.items():
        noise = np.random.default_rng([zlib.crc32(name.encode()), seed]).standard_normal(out[name].shape)
        drawn = base * np.exp(spread * noise) if base else spread * noise
        out[name] = jnp.asarray(drawn.astype(out[name].dtype))
    for name, factor in factors.items():
        out[name] = (out[name] * factor).astype(out[name].dtype)
    return out
```

```python
from contextlib import ExitStack

import numpy as np

import concourse.bass as bass
from concourse import mybir

P = 128
H = 8
D = 32
C = 256
G = 64
S = H * G
NS = 64
KC = 3
ROW = C + H
NCH = 12
CAND = 8 * NCH
K = 24
GR = 4
GROUPS = K // GR
BY_VECTOR, BY_POOL, BY_SCALAR = (0, 1), (2, 3), (4, 5)
EPS = 1e-5
BIG = 1e30

NV_ABS = 7
NV_DA = 16
NV_CONV = 30
NV_ACT = 36
NV_DECAY = 40
NV_MIX = 50
NV_MS = 60
NV_Y = 64
NA_YT = 11

ALU = mybir.AluOpType
ACT = mybir.ActivationFunctionType
F32 = mybir.dt.float32
U32 = mybir.dt.uint32
I32 = mybir.dt.int32
AX = mybir.AxisListType
ds = bass.ds


class Steps:

    def __init__(self, eng, sem, gate=None):
        self.eng, self.sem, self.n, self.base, self.gate = eng, sem, 0, 0, gate

    def __call__(self, ins):
        self.n += 1
        ins.then_inc(self.sem, 1)
        self.eng.wait_ge(self.sem, self.base + self.n)
        if self.gate is not None:
            self.eng.sem_inc(self.gate, 1)


def wait(eng, sem, value):
    if isinstance(value, int) and value <= 0:
        return
    eng.wait_ge(sem, value)


def loop(eng, n, body):
    body(0)
    if n > 1:
        with eng.Fori(1, n) as i:
            body(i)


def pipeline(eng, n, body):
    for t in range(4):
        body(t, t, 0)
    if n > 8:
        with eng.Fori(1, n // 4 - 1) as i:
            for j in range(4):
                body(i * 4 + j, j, i)
    for t in range(n - 4, n + 1):
        body(t, t % 4, t // 4)


def has(t, n):
    return not isinstance(t, int) or 0 <= t < n


def flat(ap):
    return ap.rearrange("p a c -> p (a c)")


def chunk_bounds(n):
    return [n * c // NCH for c in range(NCH + 1)]


def build(nc, t):
    N = t["x"].shape[0]
    NT = N // P
    XQ = 8
    TQ = NT // XQ
    node_table = nc.dram_tensor("node_table", [N, ROW], F32, kind="Internal").ap()
    residual_rows = nc.dram_tensor("residual_rows", [N, C], F32, kind="Internal").ap()
    weights_t = nc.dram_tensor("slice_weights_t", [NT, P, S], F32, kind="Internal").ap()
    bounds = chunk_bounds(N)

    with ExitStack() as ctx:
        def sb(name, shape, dt=F32, c=ctx):
            return c.enter_context(nc.sbuf_tensor(name, shape, dt))

        def sem(name):
            return ctx.enter_context(nc.semaphore(name))

        def ps(name, shape, c):
            return c.enter_context(nc.psum_tensor(name, [P, 512], F32))[:, 0:shape[1]]

        x_sb = sb("x_sb", [P, NT, C])
        src_score = sb("src_score", [P, NT, H])
        ident = sb("ident", [P, P])
        ones = sb("ones", [P, P])
        wct = sb("wct", [P, 2, S])
        bc = sb("bc", [P, S])
        stat6 = sb("stat6", [P, 2, 6])
        stat2 = sb("stat2", [P, 2, 2])
        mean = sb("mean", [P, NT])
        var = sb("var", [P, NT])
        rstd = sb("rstd", [P, NT])

        def norm_stats(dve, name, pieces):
            done = sem(f"{name}_stats")
            step = Steps(dve, done, sem(f"{name}_gate"))
            for q in range(XQ):
                if pieces is not None:
                    dve.wait_ge(pieces[q], 16)
                with dve.Fori(q * TQ, (q + 1) * TQ) as i:
                    step.base, step.n = i * 3, 0
                    step(nc.vector.bn_stats(stat6[:, 0, :], flat(x_sb[:, ds(i, 1), :])))
                    step(nc.vector.bn_aggr(stat2[:, 0, :], stat6[:, 0, :]))
                    nc.vector.tensor_copy(mean[:, ds(i, 1)], stat2[:, 0, 0:1])
                    step(nc.vector.tensor_scalar(var[:, ds(i, 1)], stat2[:, 0, 1:2], EPS, None, ALU.add))

        with ExitStack() as c1:
            w_nat = sb("w_nat", [P, 2, C], c=c1)
            a_bd = sb("a_bd", [P, 2, 2 * H], c=c1)
            w_cat = sb("w_cat", [P, 2, ROW + H], c=c1)
            wr_t = sb("wr_t", [P, 2, C], c=c1)
            br = sb("br", [P, C], c=c1)
            be = sb("be", [P, H], c=c1)
            wx = sb("wx", [G, H, C], c=c1)
            ws_t = sb("ws_t", [G, G], c=c1)
            bx = sb("bx", [G, H], c=c1)
            bx_wide = sb("bx_wide", [G, H, P], c=c1)
            bs = sb("bs", [P, G], c=c1)
            temp = sb("temp", [P, H], c=c1)
            xn = sb("xn", [P, 2, C], c=c1)
            xn_t = sb("xn_t", [P, 2, C], c=c1)
            row_out = sb("row_out", [P, 2, ROW], c=c1)
            p_t = [ps(f"p_t{u}", [P, C], c1) for u in range(2)]
            p_h = [ps(f"p_h{u}", [P, ROW + H], c1) for u in range(2)]
            p_r = [ps(f"p_r{u}", [P, C], c1) for u in range(2)]
            p_w = ps("p_w", [P, S], c1)
            p_v = ps("p_v", [P, S], c1)

            weights_in = sem("weights_in")
            x_in = [sem(f"x_in{q}") for q in range(XQ)]
            prep_pe, prep_dve = sem("prep_pe"), sem("prep_dve")
            var_done, std_done, rstd_done = sem("var_done"), sem("std_done"), sem("rstd_done")
            xn_done, xt_done, xt_copied = sem("xn_done"), sem("xt_done"), sem("xt_copied")
            h_done, h_copied = sem("h_done"), sem("h_copied")
            r_done, r_added, br_added = sem("r_done"), sem("r_added"), sem("br_added")
            row_stored = [sem(f"row_stored{u}") for u in range(2)]
            residual_stored = sem("residual_stored")
            loads = [
                (ident[:], t["ident"]), (ones[:], t["ones"]),
                (w_nat[:], t["W"].rearrange("(b p) i -> p b i", p=P)),
                (a_bd[:], t["a_bd"].rearrange("(b p) i -> p b i", p=P)),
                (w_cat[:, :, 0:C], t["W_t"].rearrange("(b p) i -> p b i", p=P)),
                (wr_t[:], t["Wr_t"].rearrange("(b p) i -> p b i", p=P)),
                (br[:], t["br"]), (be[:], t["be"]),
                (wx[:], t["W_x"].rearrange("(h p) i -> p h i", p=G)),
                (ws_t[:], t["W_slice_t"]), (bx[:], t["b_x_t"]), (bs[:], t["b_slice"]), (temp[:], t["temp"]),
            ]
            with nc.Block() as block:
                @block.sync
                def _(sp):
                    for dst, src in loads:
                        sp.dma_start(dst, src).then_inc(weights_in, 16)
                    xr = t["x"].rearrange("(t p) c -> p t c", p=P)
                    for q in range(XQ):
                        sp.dma_start(x_sb[:, q * TQ:(q + 1) * TQ, :], xr[:, q * TQ:(q + 1) * TQ, :]).then_inc(x_in[q], 16)
                    with sp.Fori(0, NT // 2) as i:
                        for u in range(2):
                            rows = sp.snap((i * 2 + u) * P)
                            sp.wait_ge(h_copied, (i * 2 + u) + 1)
                            sp.dma_start(node_table[ds(rows, P), :], row_out[:, u, :]).then_inc(row_stored[u], 16)
                    rr = residual_rows.rearrange("(t p) c -> p t c", p=P)
                    sp.wait_ge(r_added, NT)
                    for q in range(XQ):
                        sp.dma_start(rr[:, q * TQ:(q + 1) * TQ, :], x_sb[:, q * TQ:(q + 1) * TQ, :]).then_inc(residual_stored, 16)
                    for u in range(2):
                        sp.wait_ge(row_stored[u], 16 * (NT // 2))
                    sp.wait_ge(residual_stored, 16 * XQ)

                @block.tensor
                def _(pe):
                    pe.wait_ge(weights_in, 16 * len(loads))
                    for c in range(2):
                        for b in range(2):
                            mm = pe.matmul(p_w[:, c * 2 * H:(c + 1) * 2 * H], w_nat[:, b, c * P:(c + 1) * P],
                                           a_bd[:, b, :], start=b == 0, stop=b == 1)
                    mm.then_inc(prep_pe, 1)
                    pe.wait_ge(prep_dve, 1)
                    for h in range(H):
                        mm = pe.matmul(p_v[:, h * G:(h + 1) * G], bx_wide[:, h, :], ws_t[:], start=True, stop=True)
                    mm.then_inc(prep_pe, 1)
                    for c in range(2):
                        pe.wait_ge(prep_dve, 3 + c)
                        for h in range(H):
                            mm = pe.matmul(p_w[:, h * G:(h + 1) * G], wx[:, h, c * P:(c + 1) * P], ws_t[:],
                                           start=True, stop=True)
                        mm.then_inc(prep_pe, 1)
                    def turn(tile, u):
                        pe.wait_ge(xn_done, tile + 1)
                        wait(pe, xt_copied, tile - 1)
                        for b in range(2):
                            mm = pe.transpose(p_t[u][:, b * P:(b + 1) * P], xn[:, u, b * P:(b + 1) * P], ident[:])
                        mm.then_inc(xt_done, 1)

                    def products(tile, u):
                        pe.wait_ge(xt_copied, tile + 1)
                        wait(pe, h_copied, tile - 1)
                        wait(pe, r_added, tile - 1)
                        for b in range(2):
                            mm = pe.matmul(p_h[u][:], xn_t[:, u, b * P:(b + 1) * P], w_cat[:, b, :],
                                           start=b == 0, stop=b == 1)
                        mm.then_inc(h_done, 1)
                        for b in range(2):
                            mm = pe.matmul(p_r[u][:], xn_t[:, u, b * P:(b + 1) * P], wr_t[:, b, :],
                                           start=b == 0, stop=b == 1)
                        mm.then_inc(r_done, 1)

                    def pair(i):
                        for u in range(2):
                            turn(i * 2 + u + 1, 1 - u)
                            products(i * 2 + u, u)
                    turn(0, 0)
                    loop(pe, NT // 2 - 1, pair)
                    turn(NT - 1, 1)
                    products(NT - 2, 0)
                    products(NT - 1, 1)

                @block.scalar
                def _(act):
                    act.wait_ge(var_done, 1)
                    nc.scalar.activation(rstd[:], var[:], ACT.Sqrt).then_inc(std_done, 1)

                    def copy_rows(tile, u):
                        wait(act, r_done, tile - 1)
                        act.wait_ge(xt_done, tile + 1)
                        nc.scalar.copy(xn_t[:, u, :], p_t[u][:]).then_inc(xt_copied, 1)

                    def copy_features(tile, u, i):
                        wait(act, row_stored[u], i * 16)
                        act.wait_ge(h_done, tile + 1)
                        nc.scalar.copy(row_out[:, u, :], p_h[u][:, 0:ROW]).then_inc(h_copied, 1)

                    def pair(i):
                        for u in range(2):
                            copy_rows(i * 2 + u + 1, 1 - u)
                            copy_features(i * 2 + u, u, i)
                    copy_rows(0, 0)
                    loop(act, NT // 2 - 1, pair)
                    copy_rows(NT - 1, 1)
                    copy_features(NT - 2, 0, NT // 2 - 1)
                    copy_features(NT - 1, 1, NT // 2 - 1)

                @block.vector
                def _(dve):
                    step = Steps(dve, prep_dve)
                    dve.wait_ge(weights_in, 16 * len(loads))
                    step(nc.vector.tensor_copy(bx_wide[:], bx[:].unsqueeze(2).broadcast_to([G, H, P])))
                    step(nc.vector.tensor_scalar(temp[:], temp[:], 1e-6, None, ALU.max))
                    dve.wait_ge(prep_pe, 1)
                    step(nc.vector.tensor_copy(w_cat[:, :, C:ROW + H], p_w[:, 0:4 * H].rearrange("p (c a) -> p c a", c=2)))
                    dve.wait_ge(prep_pe, 2)
                    rt = temp[:].unsqueeze(2).broadcast_to([P, H, G])
                    bc3 = bc[:].rearrange("p (h g) -> p h g", h=H)
                    recip = sem("recip")
                    nc.vector.reciprocal(temp[:], temp[:]).then_inc(recip, 1)
                    dve.wait_ge(recip, 1)
                    for c in range(2):
                        dve.wait_ge(prep_pe, 3 + c)
                        step(nc.vector.tensor_tensor(wct[:, c, :].rearrange("p (h g) -> p h g", h=H),
                                                     p_w[:].rearrange("p (h g) -> p h g", h=H), rt, ALU.mult))
                    step(nc.vector.tensor_tensor(bc3, p_v[:].rearrange("p (h g) -> p h g", h=H),
                                                 bs[:].unsqueeze(1).broadcast_to([P, H, G]), ALU.add))
                    step(nc.vector.tensor_tensor(bc3, bc3, rt, ALU.mult))
                    norm_stats(dve, "first", x_in)
                    nc.vector.memset(stat2[:, 1, :], 0.0).then_inc(var_done, 1)
                    dve.wait_ge(std_done, 1)
                    nc.vector.reciprocal(rstd[:], rstd[:]).then_inc(rstd_done, 1)
                    dve.wait_ge(rstd_done, 1)

                    def normalise(tile, u):
                        wait(dve, xt_done, tile - 1)
                        nc.vector.tensor_scalar(xn[:, u, :], flat(x_sb[:, ds(tile, 1), :]),
                                                mean[:, ds(tile, 1)], rstd[:, ds(tile, 1)],
                                                ALU.subtract, ALU.mult).then_inc(xn_done, 1)

                    def residual(tile, u):
                        dve.wait_ge(h_copied, tile + 1)
                        nc.vector.tensor_tensor(flat(src_score[:, ds(tile, 1), :]),
                                                p_h[u][:, ROW:ROW + H], be[:], ALU.add)
                        dve.wait_ge(r_done, tile + 1)
                        dve.wait_ge(br_added, tile + 1)
                        xt = flat(x_sb[:, ds(tile, 1), :])
                        nc.vector.tensor_tensor(xt, xt, p_r[u][:], ALU.add).then_inc(r_added, 1)

                    def pair(i):
                        normalise(i * 2 + 1, 1)
                        residual(i * 2, 0)
                        normalise(i * 2 + 2, 0)
                        residual(i * 2 + 1, 1)
                    normalise(0, 0)
                    loop(dve, NT // 2 - 1, pair)
                    normalise(NT - 1, 1)
                    residual(NT - 2, 0)
                    residual(NT - 1, 1)

                @block.gpsimd
                def _(pool):
                    pool.wait_ge(weights_in, 16 * len(loads))
                    with pool.Fori(0, NT) as i:
                        pool.wait_ge(xn_done, i + 1)
                        xt = flat(x_sb[:, ds(i, 1), :])
                        nc.gpsimd.tensor_tensor(xt, xt, br[:], ALU.add).then_inc(br_added, 1)

        over = sb("over", [P, 2, NT])
        over_flag = sb("over_flag", [P, 1])
        over_int = sb("over_int", [P, 1], I32)
        with ExitStack() as c2:
            adj = sb("adj", [P, 2, N], c=c2)
            near = sb("near", [P, 2, K, ROW], c=c2)
            base = sb("base", [P, CAND], c=c2)
            we = sb("we", [P, H], c=c2)
            vals = sb("vals", [P, CAND], c=c2)
            where = sb("where", [P, CAND], U32, c=c2)
            keys = sb("keys", [P, 4, CAND], c=c2)
            key = sb("key", [P, 2, 4 * 8], c=c2)
            edge = sb("edge", [P, K], c=c2)
            column = sb("column", [P, 2, K], U32, c=c2)
            none = sb("none", [P, K], c=c2)
            picked = sb("picked", [P, K, CAND], c=c2)
            z = sb("z", [P, K, H], c=c2)
            edge_score = sb("edge_score", [P, 2, K, H], c=c2)
            gone = sb("gone", [P, 2, K], c=c2)
            w = sb("w", [P, 2, K, H], c=c2)
            stat = sb("stat", [P, 3, H], c=c2)
            p_o = [ps(f"p_o{u}", [P, C], c2) for u in range(2)]

            consts_in = sem("a_consts_in")
            adj_in = [sem(f"adj_in{u}") for u in range(2)]
            adj_read = sem("adj_read")
            columns_done = sem("columns_done")
            near_in = [sem(f"near_in{u}") for u in range(2)]
            z_done, w_done, w_normed = sem("z_done"), sem("w_done"), sem("w_normed")
            near_scaled_v, near_scaled_p, near_scaled_a = sem("near_scaled_v"), sem("near_scaled_p"), sem("near_scaled_a")
            summed, added = sem("summed"), sem("added")
            listed, soft = sem("listed"), sem("soft")
            cleared = sem("near_cleared")
            gate, pool_gate = sem("gate"), sem("pool_gate")
            flag_max, flag_all, flag_done = sem("flag_max"), sem("flag_all"), sem("flag_done")

            def scale_rows(eng, u, g):
                ks = slice(g * GR, (g + 1) * GR)
                rows = near[:, u, ks, 0:C].rearrange("p k (h d) -> p k h d", h=H)
                return eng.tensor_tensor(rows, rows, w[:, u, ks, :].unsqueeze(3).broadcast_to([P, GR, H, D]), ALU.mult)

            with nc.Block() as block:
                @block.sync
                def _(sp):
                    sp.dma_start(base[:], t["cand_base"]).then_inc(consts_in, 16)
                    sp.dma_start(we[:], t["We"]).then_inc(consts_in, 16)

                    def pair(i):
                        for u in range(2):
                            rows = (i * 2 + u) * P
                            rows = rows if isinstance(rows, int) else sp.snap(rows)
                            wait(sp, adj_read, i * 2 + u - 1)
                            sp.dma_start(adj[:, u, :], t["adj"][ds(rows, P), :]).then_inc(adj_in[u], 16)
                    loop(sp, NT // 2, pair)

                @block.vector
                def _(dve):
                    nc.vector.memset(near[:], 0.0).then_inc(cleared, 1)
                    list_step, soft_step = Steps(dve, listed, gate), Steps(dve, soft)
                    dve.wait_ge(consts_in, 32)

                    def list_edges(tile, u, i):
                        step = list_step
                        step.base, step.n = tile * 13, 0
                        dve.wait_ge(adj_in[u], (i + 1) * 16)
                        dve.sem_inc(gate, 1)
                        for c in range(NCH):
                            ins = nc.vector.max(vals[:, 8 * c:8 * c + 8], adj[:, u, bounds[c]:bounds[c + 1]])
                        step(ins)
                        for c in range(NCH):
                            ins = nc.vector.max_index(where[:, 8 * c:8 * c + 8], vals[:, 8 * c:8 * c + 8],
                                                      adj[:, u, bounds[c]:bounds[c + 1]])
                        ins.then_inc(adj_read, 1)
                        dve.wait_ge(adj_read, tile + 1)
                        step(nc.vector.tensor_tensor(keys[:, 3, :], where[:], base[:], ALU.add))
                        step(nc.vector.scalar_tensor_tensor(keys[:, 0, :], vals[:], 0.0, keys[:, 3, :], ALU.is_gt, ALU.mult))
                        for r in range(3):
                            step(nc.vector.max(key[:, u, 8 * r:8 * r + 8], keys[:, r, :]))
                            step(nc.vector.match_replace(keys[:, r + 1, :], key[:, u, 8 * r:8 * r + 8], keys[:, r, :], 0.0))
                        step(nc.vector.max(key[:, u, K:K + 8], keys[:, 3, :]))
                        nc.vector.tensor_reduce(over[:, 0, ds(tile, 1)], vals[:].rearrange("p (c e) -> p c e", e=8)[:, :, 7],
                                                AX.X, ALU.max)
                        nc.vector.tensor_copy(over[:, 1, ds(tile, 1)], key[:, u, K:K + 1])
                        step(nc.vector.tensor_scalar(none[:], key[:, u, 0:K], 0.0, 4.0 * N, ALU.is_equal, ALU.mult))
                        nc.vector.scalar_tensor_tensor(column[:, u, :], none[:], -1.0, key[:, u, 0:K],
                                                       ALU.add, ALU.add).then_inc(columns_done, 1)
                        for k in range(K):
                            ins = nc.vector.scalar_tensor_tensor(picked[:, k, :], keys[:, 0, :], key[:, u, k:k + 1], vals[:],
                                                                 ALU.is_equal, ALU.mult, accum_out=edge[:, k:k + 1])
                        step(ins)
                        nc.vector.tensor_scalar(gone[:, u, :], key[:, u, 0:K], 0.0, -BIG, ALU.is_equal, ALU.mult)
                        step(nc.vector.tensor_tensor(edge_score[:, u, :, :], edge[:].unsqueeze(2).broadcast_to([P, K, H]),
                                                     we[:].unsqueeze(1).broadcast_to([P, K, H]), ALU.mult))

                    def softmax(tile, u, i):
                        step = soft_step
                        step.base, step.n = tile * 7, 0
                        dve.wait_ge(near_in[u], (i + 1) * 16 * K)
                        step(nc.vector.tensor_tensor(z[:], near[:, u, :, C:ROW],
                                                     src_score[:, ds(tile, 1), :].broadcast_to([P, K, H]), ALU.add))
                        step(nc.vector.tensor_tensor(z[:], z[:], edge_score[:, u, :, :], ALU.add))
                        step(nc.vector.scalar_tensor_tensor(z[:], z[:], 0.2, z[:], ALU.mult, ALU.max))
                        step(nc.vector.tensor_tensor(z[:], z[:], gone[:, u, :].unsqueeze(2).broadcast_to([P, K, H]), ALU.add))
                        step(nc.vector.tensor_reduce(stat[:, 0, :], z[:].rearrange("p k h -> p h k"), AX.X, ALU.max))
                        nc.vector.tensor_tensor(z[:], z[:], stat[:, 0, :].unsqueeze(1).broadcast_to([P, K, H]),
                                                ALU.subtract).then_inc(z_done, 1)
                        dve.wait_ge(w_done, tile + 1)
                        step(nc.vector.tensor_reduce(stat[:, 1, :], w[:, u, :, :].rearrange("p k h -> p h k"), AX.X, ALU.add))
                        step(nc.vector.reciprocal(stat[:, 2, :], stat[:, 1, :]))
                        nc.vector.tensor_tensor(w[:, u, :, :], w[:, u, :, :], stat[:, 2, :].unsqueeze(1).broadcast_to([P, K, H]),
                                                ALU.mult).then_inc(w_normed, 1)
                        dve.wait_ge(w_normed, tile + 1)
                        for g in BY_VECTOR:
                            scale_rows(nc.vector, u, g).then_inc(near_scaled_v, 1)

                    def add(tile, u):
                        dve.wait_ge(summed, (tile + 1) * GROUPS)
                        xt = flat(x_sb[:, ds(tile, 1), :])
                        nc.vector.tensor_tensor(xt, xt, p_o[u][:], ALU.add).then_inc(added, 1)

                    list_edges(0, 0, 0)
                    list_edges(1, 1, 0)
                    softmax(0, 0, 0)
                    with dve.Fori(1, NT // 2) as i:
                        list_edges(i * 2, 0, i)
                        softmax(i * 2 - 1, 1, i - 1)
                        add(i * 2 - 2, 0)
                        list_edges(i * 2 + 1, 1, i)
                        softmax(i * 2, 0, i)
                        add(i * 2 - 1, 1)
                    softmax(NT - 1, 1, NT // 2 - 1)
                    add(NT - 2, 0)
                    add(NT - 1, 1)
                    nc.vector.tensor_reduce(over_flag[:], over[:].rearrange("p a t -> p (a t)"), AX.X, ALU.max).then_inc(flag_max, 1)
                    dve.wait_ge(flag_all, 1)
                    nc.vector.tensor_scalar(over_int[:], over_flag[:], 0.0, None, ALU.is_gt).then_inc(flag_done, 1)
                    dve.wait_ge(flag_done, 1)

                @block.scalar
                def _(act):
                    def pair(i):
                        for u in range(2):
                            tile = i * 2 + u
                            act.wait_ge(z_done, tile + 1)
                            wait(act, near_scaled_p, (tile - 1) * len(BY_POOL))
                            nc.scalar.activation(w[:, u, :, :], z[:], ACT.Exp).then_inc(w_done, 1)
                            act.wait_ge(w_normed, tile + 1)
                            for g in BY_SCALAR:
                                for k in range(g * GR, (g + 1) * GR):
                                    for h in range(H):
                                        part = near[:, u, k, h * D:(h + 1) * D]
                                        ins = nc.scalar.mul(part, part, w[:, u, k, h:h + 1])
                                ins.then_inc(near_scaled_a, 1)
                    loop(act, NT // 2, pair)

                @block.gpsimd
                def _(pool):
                    pool.wait_ge(cleared, 1)

                    def gather(tile, u):
                        pool.wait_ge(columns_done, tile + 1)
                        pool.sem_inc(pool_gate, 1)
                        for g in range(GROUPS):
                            if not isinstance(tile, int) or tile >= 2:
                                pool.wait_ge(summed, (tile - 2) * GROUPS + g + 1)
                                pool.sem_inc(pool_gate, 1)
                            for k in range(g * GR, (g + 1) * GR):
                                pool.indirect_dma_start(
                                    out=near[:, u, k, :], out_offset=None, in_=node_table,
                                    in_offset=bass.IndirectOffsetOnAxis(ap=column[:, u, k:k + 1], axis=0),
                                    bounds_check=N - 1, oob_is_err=False).then_inc(near_in[u], 16)

                    def scale(tile, u):
                        pool.wait_ge(w_normed, tile + 1)
                        for g in BY_POOL:
                            scale_rows(nc.gpsimd, u, g).then_inc(near_scaled_p, 1)

                    def pair(i):
                        gather(i * 2 + 1, 1)
                        scale(i * 2, 0)
                        gather(i * 2 + 2, 0)
                        scale(i * 2 + 1, 1)
                    gather(0, 0)
                    loop(pool, NT // 2 - 1, pair)
                    gather(NT - 1, 1)
                    scale(NT - 2, 0)
                    scale(NT - 1, 1)
                    pool.wait_ge(flag_max, 1)
                    nc.gpsimd.partition_all_reduce(over_flag[:], over_flag[:], P, bass.bass_isa.ReduceOp.max).then_inc(flag_all, 1)

                @block.tensor
                def _(pe):
                    def pair(i):
                        for u in range(2):
                            tile = i * 2 + u
                            wait(pe, added, tile - 1)
                            for groups, scaled in ((BY_VECTOR, near_scaled_v), (BY_POOL, near_scaled_p), (BY_SCALAR, near_scaled_a)):
                                for n, g in enumerate(groups):
                                    pe.wait_ge(scaled, tile * len(groups) + n + 1)
                                    for k in range(g * GR, (g + 1) * GR):
                                        mm = pe.matmul(p_o[u][:], ident[:], near[:, u, k, 0:C], start=k == 0, stop=k == K - 1)
                                    mm.then_inc(summed, 1)
                    loop(pe, NT // 2, pair)

        JB = 4 * P
        NJ = N // JB
        flag = nc.values_load(over_int[0:1, 0:1], min_val=0, max_val=1)
        with nc.If(flag > 0), ExitStack() as c3:
            a = sb("d_adj", [P, JB], c=c3)
            absent = sb("absent", [P, JB], c=c3)
            nodes = sb("nodes", [P, 4, ROW], c=c3)
            we = sb("d_we", [P, H], c=c3)
            dst_wide = sb("dst_wide", [P, 4, H, P], c=c3)
            z = sb("d_z", [P, H, JB], c=c3)
            w = sb("d_w", [P, H, JB], c=c3)
            w_t = sb("d_w_t", [P, H, 4, P], c=c3)
            stat = sb("d_stat", [P, 8, H], c=c3)
            MAX, BLOCK_MAX, NEW_MAX, DROP, KEEP, SUM, BLOCK_SUM, INV = range(8)
            acc = sb("acc", [P, C], c=c3)
            p_d = [ps(f"p_d{u}", [P, JB], c3) for u in range(2)]
            p_x = [ps(f"p_x{u}", [P, JB], c3) for u in range(2)]
            p_a = ps("p_a", [P, C], c3)
            d_in, base_in, d_gate, d_gate_v = sem("d_in"), sem("base_in"), sem("d_gate"), sem("d_gate_v")
            dv, dp, da_ = sem("dense_dve"), sem("dense_pe"), sem("dense_act")
            BEGIN, BLOCK, END = 3, 24, 3
            TILE = BEGIN + NJ * BLOCK + END

            with nc.Block() as block:
                @block.sync
                def _(sp):
                    sp.dma_start(we[:], t["We"]).then_inc(base_in, 16)
                    rr = residual_rows.rearrange("(t p) c -> p t c", p=P)
                    sp.dma_start(x_sb[:], rr).then_inc(base_in, 16)
                    with sp.Fori(0, NT) as i:
                        with sp.Fori(0, NJ) as j:
                            row, col = sp.snap(i * P), sp.snap(j * JB)
                            sp.wait_ge(dv, i * TILE + BEGIN + j * BLOCK)
                            sp.sem_inc(d_gate, 1)
                            sp.dma_start(a[:], t["adj"][ds(row, P), ds(col, JB)]).then_inc(d_in, 16)
                            sp.dma_start(nodes[:], node_table[ds(col, JB), :].rearrange("(b p) c -> p b c", p=P)).then_inc(d_in, 16)

                @block.vector
                def _(dve):
                    v = nc.vector
                    step = Steps(dve, dv, d_gate_v)
                    dve.wait_ge(base_in, 32)

                    def last(ap, n):
                        return ap.unsqueeze(2).broadcast_to([P, ap.shape[1], n])
                    with dve.Fori(0, NT) as i:
                        step.base, step.n = i * TILE, 0
                        step(v.memset(stat[:, MAX, :], -BIG))
                        step(v.memset(stat[:, SUM, :], 0.0))
                        step(v.memset(acc[:], 0.0))
                        assert step.n == BEGIN
                        with dve.Fori(0, NJ) as j:
                            step.base, step.n = i * TILE + j * BLOCK + BEGIN, 0
                            block_at = i * NJ + j
                            dve.wait_ge(d_in, (block_at + 1) * 32)
                            for b in range(4):
                                ins = v.tensor_copy(dst_wide[:, b, :, :], last(nodes[:, b, C:ROW], P))
                            step(ins)
                            step(v.tensor_scalar(absent[:], a[:], 0.0, -1.0, ALU.is_gt, ALU.add))
                            for h in range(H):
                                dve.wait_ge(dp, block_at * 17 + h + 1)
                                step(v.scalar_tensor_tensor(z[:, h, :], a[:], we[:, h:h + 1], p_d[h % 2][:], ALU.mult, ALU.add))
                            step(v.tensor_tensor(z[:], z[:], last(flat(src_score[:, ds(i, 1), :]), JB), ALU.add))
                            step(v.scalar_tensor_tensor(z[:], z[:], 0.2, z[:], ALU.mult, ALU.max))
                            step(v.scalar_tensor_tensor(z[:], absent[:].unsqueeze(1).broadcast_to([P, H, JB]), BIG, z[:],
                                                        ALU.mult, ALU.add))
                            step(v.tensor_reduce(stat[:, BLOCK_MAX, :], z[:], AX.X, ALU.max))
                            step(v.tensor_tensor(stat[:, NEW_MAX, :], stat[:, MAX, :], stat[:, BLOCK_MAX, :], ALU.max))
                            step(v.tensor_tensor(stat[:, DROP, :], stat[:, MAX, :], stat[:, NEW_MAX, :], ALU.subtract))
                            step(v.tensor_copy(stat[:, MAX, :], stat[:, NEW_MAX, :]))
                            step(v.tensor_tensor(z[:], z[:], last(stat[:, NEW_MAX, :], JB), ALU.subtract))
                            assert step.n == 18
                            dve.wait_ge(da_, block_at * 10 + 2)
                            step(v.tensor_reduce(stat[:, BLOCK_SUM, :], w[:], AX.X, ALU.add))
                            step(v.tensor_tensor(stat[:, SUM, :], stat[:, SUM, :], stat[:, KEEP, :], ALU.mult))
                            step(v.tensor_tensor(stat[:, SUM, :], stat[:, SUM, :], stat[:, BLOCK_SUM, :], ALU.add))
                            acc3 = acc[:].rearrange("p (h d) -> p h d", h=H)
                            step(v.tensor_tensor(acc3, acc3, last(stat[:, KEEP, :], D), ALU.mult))
                            dve.wait_ge(dp, block_at * 17 + 17)
                            step(v.tensor_tensor(acc[:], acc[:], p_a[:], ALU.add))
                            step(v.tensor_copy(stat[:, DROP, :], stat[:, KEEP, :]))
                            assert step.n == BLOCK
                        step.base, step.n = i * TILE + BEGIN + NJ * BLOCK, 0
                        step(v.reciprocal(stat[:, INV, :], stat[:, SUM, :]))
                        acc3 = acc[:].rearrange("p (h d) -> p h d", h=H)
                        step(v.tensor_tensor(acc3, acc3, last(stat[:, INV, :], D), ALU.mult))
                        xt = flat(x_sb[:, ds(i, 1), :])
                        step(v.tensor_tensor(xt, xt, acc[:], ALU.add))

                @block.scalar
                def _(act):
                    with act.Fori(0, NT) as i:
                        with act.Fori(0, NJ) as j:
                            block_at = i * NJ + j
                            act.wait_ge(dv, i * TILE + BEGIN + j * BLOCK + 18)
                            nc.scalar.activation(w[:], z[:], ACT.Exp).then_inc(da_, 1)
                            nc.scalar.activation(stat[:, KEEP, :], stat[:, DROP, :], ACT.Exp).then_inc(da_, 1)
                            for h in range(H):
                                act.wait_ge(dp, block_at * 17 + 8 + h + 1)
                                nc.scalar.copy(w_t[:, h, :, :].rearrange("p b i -> p (b i)"), p_x[h % 2][:]).then_inc(da_, 1)

                @block.tensor
                def _(pe):
                    with pe.Fori(0, NT) as i:
                        with pe.Fori(0, NJ) as j:
                            block_at = i * NJ + j
                            dve_at = i * TILE + BEGIN + j * BLOCK
                            for h in range(H):
                                pe.wait_ge(dv, dve_at + (1 if h < 2 else h + 1))
                                for b in range(4):
                                    mm = pe.matmul(p_d[h % 2][:, b * P:(b + 1) * P], dst_wide[:, b, h, :], ident[:],
                                                   start=True, stop=True)
                                mm.then_inc(dp, 1)
                            for h in range(H):
                                pe.wait_ge(da_, block_at * 10 + (2 if h < 2 else h + 1))
                                for b in range(4):
                                    mm = pe.transpose(p_x[h % 2][:, b * P:(b + 1) * P], w[:, h, b * P:(b + 1) * P], ident[:])
                                mm.then_inc(dp, 1)
                            pe.wait_ge(da_, block_at * 10 + 10)
                            for h in range(H):
                                for b in range(4):
                                    mm = pe.matmul(p_a[:, h * D:(h + 1) * D], w_t[:, h, b, :], nodes[:, b, h * D:(h + 1) * D],
                                                   start=b == 0, stop=b == 3)
                            mm.then_inc(dp, 1)

                @block.gpsimd
                def _(pool):
                    pool.wait_ge(base_in, 32)
        slice_sum = sb("slice_sum", [P, S])
        t1 = sb("t1", [P, 2, S])
        with ExitStack() as c4:
            xn = sb("b_xn", [P, 4, C], c=c4)
            xn_t = sb("b_xn_t", [P, 2, C], c=c4)
            logit = sb("logit", [P, 2, S], c=c4)
            ex = sb("ex", [P, 2, S], c=c4)
            sw = sb("sw", [P, 2, S], c=c4)
            sw_t = sb("sw_t", [P, 2, S], c=c4)
            top = sb("top", [P, 3, H], c=c4)
            p_t = [ps(f"b_p_t{u}", [P, C], c4) for u in range(2)]
            p_l = [ps(f"p_l{u}", [P, S], c4) for u in range(2)]
            p_s = [ps(f"p_s{u}", [P, S], c4) for u in range(2)]
            p_1 = [ps(f"p_1{b}", [P, S], c4) for b in range(2)]
            b_var, b_std, b_rstd = sem("b_var"), sem("b_std"), sem("b_rstd")
            xn_done, xt_done, xt_copied = sem("b_xn_done"), sem("b_xt_done"), sem("b_xt_copied")
            logit_done, shifted, ex_done = sem("logit_done"), sem("shifted"), sem("ex_done")
            sw_done, t1_done, swt_done, swt_copied = sem("sw_done"), sem("t1_done"), sem("swt_done"), sem("swt_copied")
            swt_stored = [sem(f"swt_stored{u}") for u in range(2)]
            shift_steps, weight_steps = sem("shift_steps"), sem("weight_steps")
            sum_done, t1_copied = sem("sum_done"), sem("t1_copied")

            def by_head(ap):
                return ap.rearrange("p (h g) -> p h g", h=H)

            with nc.Block() as block:
                @block.vector
                def _(dve):
                    norm_stats(dve, "second", None)
                    nc.vector.memset(stat2[:, 1, :], 0.0).then_inc(b_var, 1)
                    dve.wait_ge(b_std, 1)
                    nc.vector.reciprocal(rstd[:], rstd[:]).then_inc(b_rstd, 1)
                    dve.wait_ge(b_rstd, 1)
                    shift_step, weight_step = Steps(dve, shift_steps), Steps(dve, weight_steps)

                    def normalise(tile, j):
                        wait(dve, t1_done, tile - 3)
                        nc.vector.tensor_scalar(xn[:, j, :], flat(x_sb[:, ds(tile, 1), :]),
                                                mean[:, ds(tile, 1)], rstd[:, ds(tile, 1)],
                                                ALU.subtract, ALU.mult).then_inc(xn_done, 1)

                    def shift(tile, u):
                        step = shift_step
                        step.base, step.n = tile * 2, 0
                        lg = by_head(logit[:, u, :])
                        dve.wait_ge(logit_done, tile + 1)
                        wait(dve, ex_done, tile - 1)
                        step(nc.vector.tensor_tensor(logit[:, u, :], p_l[u][:], bc[:], ALU.add))
                        step(nc.vector.tensor_reduce(top[:, 0, :], lg, AX.X, ALU.max))
                        nc.vector.tensor_tensor(lg, lg, top[:, 0, :].unsqueeze(2).broadcast_to([P, H, G]),
                                                ALU.subtract).then_inc(shifted, 1)

                    def weights(tile, u):
                        step = weight_step
                        step.base, step.n = tile * 2, 0
                        dve.wait_ge(ex_done, tile + 1)
                        step(nc.vector.tensor_reduce(top[:, 1, :], by_head(ex[:, u, :]), AX.X, ALU.add))
                        step(nc.vector.reciprocal(top[:, 2, :], top[:, 1, :]))
                        wait(dve, t1_done, tile - 1)
                        wait(dve, sum_done, tile - 1)
                        nc.vector.tensor_tensor(by_head(sw[:, u, :]), by_head(ex[:, u, :]),
                                                top[:, 2, :].unsqueeze(2).broadcast_to([P, H, G]),
                                                ALU.mult).then_inc(sw_done, 1)

                    normalise(0, 0)
                    normalise(1, 1)

                    def body(t, j, i):
                        if has(t, NT):
                            shift(t, j % 2)
                        if has(t - 1, NT):
                            weights(t - 1, (j - 1) % 2)
                        if has(t + 2, NT):
                            normalise(t + 2, (j + 2) % 4)
                    pipeline(dve, NT, body)
                    dve.wait_ge(t1_done, NT)
                    nc.vector.tensor_copy(t1[:, 0, :], p_1[0][:]).then_inc(t1_copied, 1)

                @block.scalar
                def _(act):
                    act.wait_ge(b_var, 1)
                    nc.scalar.activation(rstd[:], var[:], ACT.Sqrt).then_inc(b_std, 1)

                    def copy_rows(tile, u):
                        act.wait_ge(xt_done, tile + 1)
                        wait(act, logit_done, tile - 1)
                        nc.scalar.copy(xn_t[:, u, :], p_t[u][:]).then_inc(xt_copied, 1)

                    def exponentials(tile, u):
                        wait(act, sw_done, tile - 1)
                        act.wait_ge(shifted, tile + 1)
                        nc.scalar.activation(ex[:, u, :], logit[:, u, :], ACT.Exp).then_inc(ex_done, 1)

                    def copy_weights(tile, u, i):
                        wait(act, swt_stored[u], i * 16)
                        act.wait_ge(swt_done, tile + 1)
                        nc.scalar.copy(sw_t[:, u, :], p_s[u][:]).then_inc(swt_copied, 1)

                    copy_rows(0, 0)
                    copy_rows(1, 1)

                    def body(t, j, i):
                        if has(t, NT):
                            exponentials(t, j % 2)
                        if has(t - 1, NT):
                            copy_weights(t - 1, (j - 1) % 2, i * 2 + (j - 1) // 2)
                        if has(t + 2, NT):
                            copy_rows(t + 2, j % 2)
                    pipeline(act, NT, body)
                    act.wait_ge(t1_done, NT)
                    nc.scalar.copy(t1[:, 1, :], p_1[1][:]).then_inc(t1_copied, 1)

                @block.tensor
                def _(pe):
                    def turn(tile, u, j):
                        pe.wait_ge(xn_done, tile + 1)
                        wait(pe, xt_copied, tile - 1)
                        for b in range(2):
                            mm = pe.transpose(p_t[u][:, b * P:(b + 1) * P], xn[:, j, b * P:(b + 1) * P], ident[:])
                        mm.then_inc(xt_done, 1)

                    def logits(tile, u):
                        pe.wait_ge(xt_copied, tile + 1)
                        wait(pe, shifted, tile - 1)
                        for b in range(2):
                            mm = pe.matmul(p_l[u][:], xn_t[:, u, b * P:(b + 1) * P], wct[:, b, :], start=b == 0, stop=b == 1)
                        mm.then_inc(logit_done, 1)

                    def sums(tile, u, j):
                        first, last = isinstance(tile, int) and tile == 0, isinstance(tile, int) and tile == NT - 1
                        pe.wait_ge(sw_done, tile + 1)
                        wait(pe, swt_copied, tile - 1)
                        for q in range(4):
                            mm = pe.transpose(p_s[u][:, q * P:(q + 1) * P], sw[:, u, q * P:(q + 1) * P], ident[:])
                        mm.then_inc(swt_done, 1)
                        for b in range(2):
                            mm = pe.matmul(p_1[b][:], xn[:, j, b * P:(b + 1) * P], sw[:, u, :], start=first, stop=last)
                        mm.then_inc(t1_done, 1)

                    turn(0, 0, 0)
                    turn(1, 1, 1)
                    logits(0, 0)

                    def body(t, j, i):
                        if has(t + 1, NT):
                            logits(t + 1, (j + 1) % 2)
                        if has(t - 1, NT):
                            sums(t - 1, (j - 1) % 2, (j - 1) % 4)
                        if has(t + 2, NT):
                            turn(t + 2, j % 2, (j + 2) % 4)
                    pipeline(pe, NT, body)

                @block.gpsimd
                def _(pool):
                    pool.wait_ge(sw_done, 1)
                    nc.gpsimd.tensor_copy(slice_sum[:], sw[:, 0, :]).then_inc(sum_done, 1)

                    def add(tile, u):
                        pool.wait_ge(sw_done, tile + 1)
                        pool.wait_ge(sum_done, tile)
                        nc.gpsimd.tensor_tensor(slice_sum[:], slice_sum[:], sw[:, u, :], ALU.add).then_inc(sum_done, 1)
                    add(1, 1)
                    with pool.Fori(1, NT // 2) as i:
                        for u in range(2):
                            add(i * 2 + u, u)

                @block.sync
                def _(sp):
                    def pair(i):
                        for u in range(2):
                            tile = i * 2 + u
                            if not isinstance(tile, int):
                                tile = sp.snap(tile)
                            sp.wait_ge(swt_copied, tile + 1)
                            sp.dma_start(weights_t[ds(tile, 1), :, :].rearrange("a p s -> p (a s)"), sw_t[:, u, :]).then_inc(swt_stored[u], 16)
                    loop(sp, NT // 2, pair)
                    for u in range(2):
                        sp.wait_ge(swt_stored[u], 16 * (NT // 2))

        L = G
        z_out = sb("z_out", [P, 4, C])
        with ExitStack() as c5:
            def w5(name, shape):
                return sb(name, shape, c=c5)
            IN = 2 * S + 2 * NS + 2 * H
            X0, B0, C0, DT0 = S, 2 * S, 2 * S + NS, 2 * S + 2 * NS
            wfx_t, b_fx = w5("wfx_t", [P, 2, S]), w5("b_fx", [1, S])
            in_wt, how_t, ow_t = w5("in_wt", [P, 4, IN]), w5("how_t", [P, 4, S]), w5("ow_t", [P, 4, C])
            fcd_t = w5("fcd_t", [P, 4, H])
            cw_x, cb_x = w5("cw_x", [P, 4, KC]), w5("cb_x", [P, 4])
            cw_bc, cb_bc = w5("cw_bc", [NS, 2, KC]), w5("cb_bc", [NS, 2])
            dt_bias, a_log, d_skip = w5("dt_bias", [L, 2 * H]), w5("a_log", [L, H]), w5("d_skip", [L, H])
            norm_w = w5("norm_w", [L, S])
            upto, onward = w5("upto", [L, L]), w5("onward", [L, L])
            sum_row = w5("sum_row", [1, S])
            rsum, u_sb, u_t = w5("rsum", [L, H]), w5("u_sb", [L, S]), w5("u_t", [P, 4, L])
            pad_x, pad_bc = w5("pad_x", [P, 4, L + KC - 1]), w5("pad_bc", [NS, 2, L + KC - 1])
            conv_x, conv_bc = w5("conv_x", [P, 4, L]), w5("conv_bc", [NS, 2, L])
            tap_x, tap_bc = w5("tap_x", [P, 4, L]), w5("tap_bc", [NS, 2, L])
            act_x, act_bc = w5("act_x", [P, 4, L]), w5("act_bc", [NS, 2, L])
            dt, dt_abs, dt_exp, dt_one, dt_log = [w5(f"dt{i}", [L, 2 * H]) for i in range(5)]
            da, da_wide = w5("da", [L, 2 * H]), w5("da_wide", [L, 2 * H, L])
            cum, decay = w5("cum", [L, 2 * H]), w5("decay", [L, 2 * H, L])
            cb, mix, x_row = w5("cb", [L, L]), w5("mix", [L, H, L]), w5("x_row", [L, S])
            gain, y_sb, gate, sq = w5("gain", [L, H]), w5("y_sb", [L, S]), w5("gate", [L, S]), w5("sq", [L, S])
            ms, y_t, pairs = w5("ms", [L, 4]), w5("y_t", [P, 4, L]), w5("pairs", [P, 4, P])
            bank = [ps(f"bank{i}", [P, 512], c5) for i in range(8)]

            h_in = sem("h_in")
            hp, ha, hv = sem("hydra_pe"), sem("hydra_act"), sem("hydra_dve")
            loads5 = [
                (wfx_t[:], t["W_fx_t"].rearrange("(b p) i -> p b i", p=P)), (b_fx[:], t["b_fx"]),
                (in_wt[:], t["hy_in_t"].rearrange("(b p) i -> p b i", p=P)),
                (how_t[:], t["hy_out_t"].rearrange("(b p) i -> p b i", p=P)),
                (ow_t[:], t["out_w_t"].rearrange("(b p) i -> p b i", p=P)),
                (fcd_t[:], t["fcD_t"].rearrange("(b p) i -> p b i", p=P)),
                (cw_x[:], t["conv_w"][0:S, :].rearrange("(b p) i -> p b i", p=P)),
                (cb_x[:], t["conv_b_x"]),
                (cw_bc[:], t["conv_w"][S:S + 2 * NS, :].rearrange("(b p) i -> p b i", p=NS)),
                (cb_bc[:], t["conv_b_bc"]),
                (dt_bias[:], t["dt_bias"]), (a_log[:], t["A_log"]), (d_skip[:], t["hy_D"]), (norm_w[:], t["norm_w"]),
                (upto[:], t["upto"]), (onward[:], t["onward"]),
            ]
            h3 = lambda ap: ap.rearrange("p (h g) -> p h g", h=H)
            b4 = lambda ap: ap.rearrange("p (b l) -> p b l", b=4)
            mid = lambda ap, n, m: ap.unsqueeze(1).broadcast_to([m, n, ap.shape[1]])
            last = lambda ap, n: ap.unsqueeze(2).broadcast_to([ap.shape[0], ap.shape[1], n])

            with nc.Block() as block:
                @block.sync
                def _(sp):
                    for dst, src in loads5:
                        sp.dma_start(dst, src).then_inc(h_in, 16)

                @block.tensor
                def _(pe):
                    pe.wait_ge(h_in, 16 * len(loads5))
                    for h in range(H):
                        pe.matmul(bank[0][0:L, h:h + 1], slice_sum[:, h * G:(h + 1) * G], ones[:, 0:1], start=True, stop=True)
                    pe.matmul(bank[1][0:1, :], ones[:, 0:1], slice_sum[:], start=True, stop=True).then_inc(hp, 1)
                    pe.wait_ge(t1_copied, 2)
                    pe.wait_ge(ha, 1)
                    for h in range(H):
                        g = slice(h * G, (h + 1) * G)
                        for b in range(2):
                            pe.matmul(bank[2][0:L, g], t1[:, b, g], wfx_t[:, b, g], start=b == 0, stop=False)
                        mm = pe.matmul(bank[2][0:L, g], sum_row[0:1, g], b_fx[0:1, g], start=False, stop=True)
                    mm.then_inc(hp, 1)
                    pe.wait_ge(hv, 3)
                    for b in range(4):
                        mm = pe.transpose(bank[3][:, b * L:(b + 1) * L], u_sb[:, b * P:(b + 1) * P], ident[0:L, 0:L])
                    mm.then_inc(hp, 1)
                    pe.wait_ge(ha, 2)
                    for b in range(4):
                        pe.matmul(bank[4][0:L, :], u_t[:, b, :], in_wt[:, b, 0:S], start=b == 0, stop=b == 3)
                    for b in range(4):
                        pe.matmul(bank[5][0:L, 0:2 * H], u_t[:, b, :], in_wt[:, b, DT0:IN], start=b == 0, stop=b == 3)
                    for q in range(4):
                        for b in range(4):
                            pe.matmul(bank[6][:, q * L:(q + 1) * L], in_wt[:, b, X0 + q * P:X0 + (q + 1) * P], u_t[:, b, :],
                                      start=b == 0, stop=b == 3)
                    for q in range(2):
                        for b in range(4):
                            mm = pe.matmul(bank[7][0:NS, q * L:(q + 1) * L], in_wt[:, b, B0 + q * NS:B0 + (q + 1) * NS],
                                           u_t[:, b, :], start=b == 0, stop=b == 3)
                    mm.then_inc(hp, 1)
                    pe.wait_ge(hv, NV_DA)
                    pe.matmul(bank[0][0:L, 0:H], upto[:], da[:, 0:H], start=True, stop=True)
                    pe.matmul(bank[0][0:L, H:2 * H], onward[:], da[:, H:2 * H], start=True, stop=True)
                    for h in range(H):
                        pe.matmul(bank[1][0:L, h * L:(h + 1) * L], da_wide[:, h, :], upto[:], start=True, stop=True)
                        mm = pe.matmul(bank[2][0:L, h * L:(h + 1) * L], da_wide[:, H + h, :], onward[:], start=True, stop=True)
                    mm.then_inc(hp, 1)
                    pe.wait_ge(hv, NV_ACT)
                    pe.matmul(bank[3][0:L, 0:L], act_bc[:, 0, :], act_bc[:, 1, :], start=True, stop=True)
                    for b in range(4):
                        pe.transpose(bank[6][0:L, b * P:(b + 1) * P], act_x[:, b, :], ident[:])
                    for b in range(4):
                        mm = pe.matmul(bank[7][0:L, 0:H], act_x[:, b, :], fcd_t[:, b, :], start=b == 0, stop=b == 3)
                    mm.then_inc(hp, 1)
                    pe.wait_ge(hv, NV_MIX)
                    for h in range(H):
                        mm = pe.matmul(bank[5][0:L, h * G:(h + 1) * G], mix[:, h, :], x_row[:, h * G:(h + 1) * G],
                                       start=True, stop=True)
                    mm.then_inc(hp, 1)
                    pe.wait_ge(hv, NV_Y)
                    for b in range(4):
                        mm = pe.transpose(bank[3][:, b * L:(b + 1) * L], y_sb[:, b * P:(b + 1) * P], ident[0:L, 0:L])
                    mm.then_inc(hp, 1)
                    pe.wait_ge(ha, NA_YT)
                    for q in range(4):
                        for b in range(4):
                            mm = pe.matmul(bank[0][:, q * L:(q + 1) * L], how_t[:, b, q * P:(q + 1) * P], y_t[:, b, :],
                                           start=b == 0, stop=b == 3)
                    mm.then_inc(hp, 1)
                    pe.wait_ge(hv, NV_Y + 1)
                    for q in range(4):
                        mm = pe.matmul(bank[1 + q // 2][:, (q % 2) * C:(q % 2 + 1) * C], pairs[:, q, :], ow_t[:, q, :],
                                       start=True, stop=True)
                    mm.then_inc(hp, 1)

                @block.scalar
                def _(act):
                    step = Steps(act, ha)
                    act.wait_ge(h_in, 16 * len(loads5))
                    act.wait_ge(hp, 1)
                    step(nc.scalar.copy(sum_row[:], bank[1][0:1, :]))
                    act.wait_ge(hp, 3)
                    step(nc.scalar.copy(u_t[:].rearrange("p b l -> p (b l)"), bank[3][:, 0:4 * L]))
                    step(nc.scalar.activation(a_log[:], a_log[:], ACT.Exp))
                    act.wait_ge(hv, NV_ABS)
                    step(nc.scalar.activation(dt_exp[:], dt_abs[:], ACT.Exp, scale=-1.0))
                    act.wait_ge(hv, NV_ABS + 1)
                    step(nc.scalar.activation(dt_log[:], dt_one[:], ACT.Ln))
                    act.wait_ge(hv, NV_CONV)
                    nc.scalar.activation(tap_x[:], conv_x[:], ACT.Exp, scale=-1.0)
                    step(nc.scalar.activation(tap_bc[:], conv_bc[:], ACT.Exp, scale=-1.0))
                    step(nc.scalar.activation(gate[:], bank[4][0:L, :], ACT.Exp, scale=-1.0))
                    act.wait_ge(hp, 6)
                    step(nc.scalar.copy(x_row[:], bank[6][0:L, :]))
                    act.wait_ge(hv, NV_DECAY)
                    step(nc.scalar.activation(decay[:], decay[:], ACT.Exp))
                    act.wait_ge(hv, NV_MS)
                    step(nc.scalar.activation(ms[:, 2:3], ms[:, 1:2], ACT.Sqrt))
                    act.wait_ge(hp, 8)
                    step(nc.scalar.copy(y_t[:].rearrange("p b l -> p (b l)"), bank[3][:, 0:4 * L]))
                    act.wait_ge(hp, 10)
                    for q in range(2):
                        step(nc.scalar.copy(z_out[:, 2 * q:2 * q + 2, :].rearrange("p a c -> p (a c)"), bank[1 + q][:]))

                @block.vector
                def _(dve):
                    step = Steps(dve, hv)
                    v = nc.vector
                    dve.wait_ge(h_in, 16 * len(loads5))
                    dve.wait_ge(hp, 1)
                    step(v.tensor_scalar(rsum[:], bank[0][0:L, 0:H], 1e-5, None, ALU.add))
                    step(v.reciprocal(rsum[:], rsum[:]))
                    dve.wait_ge(hp, 2)
                    step(v.tensor_tensor(h3(u_sb[:]), h3(bank[2][0:L, :]), last(rsum[:], G), ALU.mult))
                    assert step.n == 3
                    step(v.memset(pad_x[:], 0.0))
                    step(v.memset(pad_bc[:], 0.0))
                    dve.wait_ge(hp, 4)
                    step(v.tensor_tensor(dt[:], bank[5][0:L, 0:2 * H], dt_bias[:], ALU.add))
                    step(v.scalar_tensor_tensor(dt_abs[:], dt[:], -1.0, dt[:], ALU.mult, ALU.max))
                    assert step.n == NV_ABS
                    dve.wait_ge(ha, 4)
                    step(v.tensor_scalar(dt_one[:], dt_exp[:], 1.0, None, ALU.add))
                    step(v.tensor_scalar(dt_abs[:], dt_one[:], -1.0, None, ALU.add))
                    step(v.tensor_tensor(dt_exp[:], dt_exp[:], dt_abs[:], ALU.subtract))
                    step(v.reciprocal(dt_abs[:], dt_one[:]))
                    step(v.tensor_tensor(dt_exp[:], dt_exp[:], dt_abs[:], ALU.mult))
                    step(v.scalar_tensor_tensor(dt[:], dt[:], 0.0, dt_exp[:], ALU.max, ALU.add))
                    dve.wait_ge(ha, 5)
                    step(v.tensor_tensor(dt[:], dt[:], dt_log[:], ALU.add))
                    step(v.scalar_tensor_tensor(da[:].rearrange("p (a h) -> p a h", a=2), dt[:].rearrange("p (a h) -> p a h", a=2),
                                                -1.0, mid(a_log[:], 2, L), ALU.mult, ALU.mult))
                    step(v.tensor_copy(da_wide[:], last(da[:], L)))
                    assert step.n == NV_DA, step.n
                    step(v.tensor_copy(pad_x[:, :, KC - 1:], b4(bank[6][:, 0:4 * L])))
                    step(v.tensor_copy(pad_bc[:, :, KC - 1:], bank[7][0:NS, 0:2 * L].rearrange("p (b l) -> p b l", b=2)))
                    for pad, cw, bias, conv, tap in ((pad_x, cw_x, cb_x, conv_x, tap_x), (pad_bc, cw_bc, cb_bc, conv_bc, tap_bc)):
                        step(v.tensor_tensor(conv[:], pad[:, :, 0:L], last(cw[:, :, 0], L), ALU.mult))
                        for k in range(1, KC):
                            step(v.tensor_tensor(tap[:], pad[:, :, k:k + L], last(cw[:, :, k], L), ALU.mult))
                            step(v.tensor_tensor(conv[:], conv[:], tap[:], ALU.add))
                        step(v.tensor_tensor(conv[:], conv[:], last(bias[:], L), ALU.add))
                    assert step.n == NV_CONV, step.n
                    dve.wait_ge(ha, 6)
                    for conv, tap, out in ((conv_x, tap_x, act_x), (conv_bc, tap_bc, act_bc)):
                        step(v.tensor_scalar(tap[:], tap[:], 1.0, None, ALU.add))
                        step(v.reciprocal(tap[:], tap[:]))
                        step(v.tensor_tensor(out[:], conv[:], tap[:], ALU.mult))
                    assert step.n == NV_ACT, step.n
                    dve.wait_ge(hp, 5)
                    step(v.tensor_copy(cum[:], bank[0][0:L, 0:2 * H]))
                    for a in range(2):
                        step(v.tensor_tensor(decay[:, a * H:(a + 1) * H, :], bank[1 + a][0:L, :].rearrange("p (h l) -> p h l", h=H),
                                             last(cum[:, a * H:(a + 1) * H], L), ALU.subtract))
                    step(v.tensor_scalar(decay[:], decay[:], 0.0, None, ALU.min))
                    assert step.n == NV_DECAY, step.n
                    dve.wait_ge(ha, 9)
                    dve.wait_ge(hp, 6)
                    step(v.tensor_copy(cb[:], bank[3][0:L, 0:L]))
                    for a, mask in ((0, upto), (1, onward)):
                        part = decay[:, a * H:(a + 1) * H, :]
                        step(v.tensor_tensor(part, part, mid(mask[:], H, L), ALU.mult))
                        step(v.tensor_tensor(part, part, mid(cb[:], H, L), ALU.mult))
                        step(v.tensor_tensor(part, part, last(dt[:, a * H:(a + 1) * H], L), ALU.mult))
                    step(v.memset(mix[:], 0.0))
                    step(v.tensor_copy(mix[:, :, 1:L], decay[:, 0:H, 0:L - 1]))
                    step(v.tensor_tensor(mix[:, :, 0:L - 1], mix[:, :, 0:L - 1], decay[:, H:2 * H, 1:L], ALU.add))
                    assert step.n == NV_MIX, step.n
                    step(v.tensor_tensor(gain[:], bank[7][0:L, 0:H], d_skip[:], ALU.add))
                    step(v.tensor_tensor(h3(sq[:]), h3(x_row[:]), last(gain[:], G), ALU.mult))
                    step(v.tensor_scalar(gate[:], gate[:], 1.0, None, ALU.add))
                    step(v.reciprocal(gate[:], gate[:]))
                    step(v.tensor_tensor(gate[:], gate[:], bank[4][0:L, :], ALU.mult))
                    dve.wait_ge(hp, 7)
                    step(v.tensor_tensor(y_sb[:], sq[:], bank[5][0:L, :], ALU.add))
                    step(v.tensor_tensor(y_sb[:], y_sb[:], gate[:], ALU.mult))
                    step(v.tensor_tensor(sq[:], y_sb[:], y_sb[:], ALU.mult))
                    step(v.tensor_reduce(ms[:, 0:1], sq[:], AX.X, ALU.add))
                    step(v.tensor_scalar(ms[:, 1:2], ms[:, 0:1], 1.0 / S, EPS, ALU.mult, ALU.add))
                    assert step.n == NV_MS, step.n
                    dve.wait_ge(ha, 10)
                    step(v.reciprocal(ms[:, 3:4], ms[:, 2:3]))
                    step(v.tensor_scalar(y_sb[:], y_sb[:], ms[:, 3:4], None, ALU.mult))
                    step(v.tensor_tensor(y_sb[:], y_sb[:], norm_w[:], ALU.mult))
                    step(v.memset(pairs[:], 0.0))
                    assert step.n == NV_Y, step.n
                    dve.wait_ge(hp, 9)
                    for a in range(2):
                        ins = v.tensor_copy(pairs[a * L:(a + 1) * L, :, a * L:(a + 1) * L],
                                            b4(bank[0][a * L:(a + 1) * L, 0:4 * L]))
                    step(ins)

        with ExitStack() as c6:
            wt = sb("wt", [P, 4, S], c=c6)
            ob = sb("ob", [P, 2, C], c=c6)
            out_b = sb("out_b", [1, C], c=c6)
            p_y = [ps(f"p_y{u}", [P, C], c6) for u in range(2)]
            ob_in = sem("ob_in")
            wt_in = [sem(f"wt_in{u}") for u in range(4)]
            y_done, y_added = sem("y_done"), sem("y_added")
            y_stored = [sem(f"y_stored{u}") for u in range(2)]
            with nc.Block() as block:
                @block.sync
                def _(sp):
                    sp.dma_start(out_b[:], t["out_b"]).then_inc(ob_in, 16)

                    def four(i):
                        for u in range(4):
                            tile = i * 4 + u
                            at = tile if isinstance(tile, int) else sp.snap(tile)
                            wait(sp, y_done, i * 4 + u - 3)
                            sp.dma_start(wt[:, u, :], weights_t[ds(at, 1), :, :].rearrange("a p s -> p (a s)")).then_inc(wt_in[u], 16)
                    loop(sp, NT // 4, four)

                @block.tensor
                def _(pe):
                    pe.wait_ge(ob_in, 16)

                    def four(i):
                        for u in range(4):
                            tile = i * 4 + u
                            pe.wait_ge(wt_in[u], (i + 1) * 16)
                            wait(pe, y_added, tile - 1)
                            for q in range(4):
                                pe.matmul(p_y[u % 2][:], wt[:, u, q * P:(q + 1) * P], z_out[:, q, :], start=q == 0, stop=False)
                            pe.matmul(p_y[u % 2][:], ones[0:1, :], out_b[:], start=False, stop=True).then_inc(y_done, 1)
                    loop(pe, NT // 4, four)

                @block.vector
                def _(dve):
                    def pair(i):
                        for u in range(2):
                            tile = i * 2 + u
                            wait(dve, y_stored[u], i * 16)
                            dve.wait_ge(y_done, tile + 1)
                            nc.vector.tensor_tensor(ob[:, u, :], flat(x_sb[:, ds(tile, 1), :]), p_y[u][:],
                                                    ALU.add).then_inc(y_added, 1)
                    loop(dve, NT // 2, pair)

                @block.scalar
                def _(act):
                    def pair(i):
                        for u in range(2):
                            tile = i * 2 + u
                            rows = tile * P
                            rows = rows if isinstance(rows, int) else act.snap(rows)
                            act.wait_ge(y_added, tile + 1)
                            act.dma_start(t["out"][ds(rows, P), :], ob[:, u, :]).then_inc(y_stored[u], 16)
                    loop(act, NT // 2, pair)
                    for u in range(2):
                        act.wait_ge(y_stored[u], 16 * (NT // 2))


def pick(inputs):
    g = {k: np.asarray(v) for k, v in inputs.items()}
    n = g["x"].shape[0]

    def rows(v, m=P):
        return np.broadcast_to(v.reshape(1, -1), (m, v.size))

    a_bd = np.zeros((H * D, 2 * H), g["x"].dtype)
    for h in range(H):
        a_bd[h * D:(h + 1) * D, h] = g["L0_gnn_a_dst"][h]
        a_bd[h * D:(h + 1) * D, H + h] = g["L0_gnn_a_src"][h]
    f = "L0_ffn_"
    b = chunk_bounds(n)
    t = {
        "x": g["x"], "adj": g["adj"],
        "ident": np.eye(P, dtype=np.float32), "ones": np.ones((P, P), np.float32),
        "cand_base": rows(np.repeat(np.asarray(b[:-1], np.float32) + 1, 8)),
        "upto": np.triu(np.ones((G, G), np.float32)), "onward": np.tril(np.ones((G, G), np.float32)),
        "W": g["L0_gnn_W"], "W_t": g["L0_gnn_W"].T, "Wr_t": g["L0_gnn_Wr"].T, "a_bd": a_bd,
        "br": rows(g["L0_gnn_br"]), "be": rows(g["L0_gnn_be"]), "We": rows(g["L0_gnn_We"]),
        "W_x": g[f + "W_x"], "W_slice_t": g[f + "W_slice"].T, "b_x_t": g[f + "b_x"].reshape(H, G).T,
        "b_slice": rows(g[f + "b_slice"]), "temp": rows(g[f + "temperature"]),
        "W_fx_t": g[f + "W_fx"].T, "b_fx": g[f + "b_fx"].reshape(1, S),
        "hy_in_t": g[f + "hy_in_w"].T, "hy_out_t": g[f + "hy_out_w"].T, "out_w_t": g[f + "out_w"].T,
        "fcD_t": g[f + "hy_fcD_w"].T, "conv_w": g[f + "hy_conv_w"], "conv_b_x": g[f + "hy_conv_b"][:S].reshape(4, P).T,
        "conv_b_bc": g[f + "hy_conv_b"][S:].reshape(2, NS).T,
        "dt_bias": rows(np.concatenate([g[f + "hy_dt_bias"]] * 2), G), "A_log": rows(g[f + "hy_A_log"], G),
        "hy_D": rows(g[f + "hy_D"], G), "norm_w": rows(g[f + "hy_norm_w"], G), "out_b": g[f + "out_b"].reshape(1, C),
    }
    return {k: np.ascontiguousarray(v) for k, v in t.items()}


def kernel(**inputs):
    import concourse.bacc as bacc
    from concourse.bass_utils import run_bass_kernel_spmd

    arrays = pick(inputs)
    nc = bacc.Bacc("TRN2", target_bir_lowering=False, num_devices=1)
    t = {k: nc.dram_tensor(f"in_{k}", v.shape, mybir.dt.from_np(v.dtype), kind="ExternalInput").ap() for k, v in arrays.items()}
    t["out"] = nc.dram_tensor("out", arrays["x"].shape, F32, kind="ExternalOutput").ap()
    build(nc, t)
    r = run_bass_kernel_spmd(nc, [{f"in_{k}": v for k, v in arrays.items()}], core_ids=[0])
    return r.results[0]["out"]
```

```python
from contextlib import ExitStack

import numpy as np

import concourse.bass as bass
from concourse import mybir

P = 128
H = 8
D = 32
C = 256
G = 64
S = H * G
NS = 64
KC = 3
ROW = C + H
NCH = 12
CAND = 8 * NCH
K = 24
GR = 4
GROUPS = K // GR
TQ = 8
BY_VECTOR, BY_POOL, BY_SCALAR = (0,), (1,), (2, 3, 4, 5)
EPS = 1e-5
BIG = 1e30

NV_ABS = 7
NV_DA = 16
NV_CONV = 30
NV_ACT = 36
NV_DECAY = 40
NV_MIX = 50
NV_MS = 60
NV_Y = 64
NA_YT = 11

ALU = mybir.AluOpType
ACT = mybir.ActivationFunctionType
F32 = mybir.dt.float32
U32 = mybir.dt.uint32
I32 = mybir.dt.int32
AX = mybir.AxisListType
ds = bass.ds


class Steps:

    def __init__(self, eng, sem, gate=None):
        self.eng, self.sem, self.n, self.base, self.gate = eng, sem, 0, 0, gate

    def __call__(self, ins):
        self.n += 1
        ins.then_inc(self.sem, 1)
        self.eng.wait_ge(self.sem, self.base + self.n)
        if self.gate is not None:
            self.eng.sem_inc(self.gate, 1)


class Chain:

    def __init__(self, eng, sem, gate):
        self.eng, self.sem, self.gate, self.base, self.n = eng, sem, gate, 0, 0

    def at(self, base, n):
        self.base, self.n = base, n
        return self

    def after_last(self):
        if not isinstance(self.base, int) or self.base + self.n > 0:
            self.eng.wait_ge(self.sem, self.base + self.n)
            self.eng.sem_inc(self.gate, 1)
        return self

    def step(self, ins):
        self.n += 1
        return ins.then_inc(self.sem, 1)


def wait(eng, sem, value):
    if isinstance(value, int) and value <= 0:
        return
    eng.wait_ge(sem, value)


def loop(eng, n, body):
    body(0)
    if n > 1:
        with eng.Fori(1, n) as i:
            body(i)


def pipeline(eng, n, body):
    for t in range(4):
        body(t, t, 0)
    if n > 8:
        with eng.Fori(1, n // 4 - 1) as i:
            for j in range(4):
                body(i * 4 + j, j, i)
    for t in range(n - 4, n + 1):
        body(t, t % 4, t // 4)


def by_piece(eng, n, body):
    body(0, False)
    if n > 2:
        with eng.Fori(1, n - 1) as q:
            body(q, False)
    body(n - 1, True)


def has(t, n):
    return not isinstance(t, int) or 0 <= t < n


def flat(ap):
    return ap.rearrange("p a c -> p (a c)")


def chunk_bounds(n):
    return [n * c // NCH for c in range(NCH + 1)]


def build(nc, t):
    N = t["x"].shape[0]
    NT = N // P
    XQ = NT // TQ
    node_table = nc.dram_tensor("node_table", [N, ROW], F32, kind="Internal").ap()
    residual_rows = nc.dram_tensor("residual_rows", [N, C], F32, kind="Internal").ap()
    weights_t = nc.dram_tensor("slice_weights_t", [NT, P, S], F32, kind="Internal").ap()
    bounds = chunk_bounds(N)

    with ExitStack() as ctx:
        def sb(name, shape, dt=F32, c=ctx):
            return c.enter_context(nc.sbuf_tensor(name, shape, dt))

        def sem(name):
            return ctx.enter_context(nc.semaphore(name))

        def ps(name, shape, c):
            return c.enter_context(nc.psum_tensor(name, [P, 512], F32))[:, 0:shape[1]]

        x_sb = sb("x_sb", [P, NT, C])
        src_score = sb("src_score", [P, NT, H])
        ident = sb("ident", [P, P])
        ones = sb("ones", [P, P])
        wct = sb("wct", [P, 2, S])
        bc = sb("bc", [P, S])
        stat6 = sb("stat6", [P, TQ, 6])
        moments = sb("moments", [P, TQ, 2])
        root_var = sb("root_var", [P, 2, TQ])
        mean = sb("mean", [P, NT])
        rstd = sb("rstd", [P, NT])

        class Norm:

            def __init__(self, name):
                self.gate, self.collected, self.aggregated = sem(f"{name}_gate"), sem(f"{name}_collected"), sem(f"{name}_aggregated")
                self.var_done, self.std_done = sem(f"{name}_var"), sem(f"{name}_std")
                self.inverted, self.rstd_done = sem(f"{name}_inverted"), sem(f"{name}_rstd")

            def collect(self, dve, q, j):
                if j == 0:
                    wait(dve, self.var_done, q)
                    dve.sem_inc(self.gate, 1)
                nc.vector.bn_stats(stat6[:, j, :], flat(x_sb[:, ds(q * TQ + j, 1), :])).then_inc(self.collected, 1)

            def aggregate(self, dve, q, j):
                dve.wait_ge(self.collected, q * TQ + j + 1)
                dve.sem_inc(self.gate, 1)
                nc.vector.bn_aggr(moments[:, j, :], stat6[:, j, :]).then_inc(self.aggregated, 1)

            def add_eps(self, dve, q):
                dve.wait_ge(self.aggregated, (q + 1) * TQ)
                wait(dve, self.rstd_done, q)
                dve.sem_inc(self.gate, 1)
                nc.vector.tensor_copy(mean[:, ds(q * TQ, TQ)], moments[:, :, 0])
                nc.vector.tensor_scalar(root_var[:, 0, :], moments[:, :, 1], EPS, None, ALU.add).then_inc(self.var_done, 1)

            def root(self, act, q):
                act.wait_ge(self.var_done, q + 1)
                nc.scalar.activation(root_var[:, 1, :], root_var[:, 0, :], ACT.Sqrt).then_inc(self.std_done, 1)

            def invert(self, dve, q):
                dve.wait_ge(self.std_done, q + 1)
                dve.sem_inc(self.gate, 1)
                nc.vector.reciprocal(root_var[:, 1, :], root_var[:, 1, :]).then_inc(self.inverted, 1)
                dve.wait_ge(self.inverted, q + 1)
                dve.sem_inc(self.gate, 1)
                nc.vector.tensor_copy(rstd[:, ds(q * TQ, TQ)], root_var[:, 1, :]).then_inc(self.rstd_done, 1)

            def turn(self, dve, q, j):
                if j < 2:
                    for k in range(TQ // 2):
                        self.collect(dve, q, j * TQ // 2 + k)
                if 1 <= j < 3:
                    for k in range(TQ // 2):
                        self.aggregate(dve, q, (j - 1) * TQ // 2 + k)
                if j == 3:
                    self.add_eps(dve, q)
                if j == 4:
                    self.invert(dve, q)

            def normalise(self, dve, out, tile, q):
                dve.wait_ge(self.rstd_done, q + 1)
                return nc.vector.tensor_scalar(out, flat(x_sb[:, ds(tile, 1), :]), mean[:, ds(tile, 1)],
                                               rstd[:, ds(tile, 1)], ALU.subtract, ALU.mult)

        over = sb("over", [P, 2, NT])
        over_flag = sb("over_flag", [P, 1])
        over_int = sb("over_int", [P, 1], I32)
        scan = ctx.enter_context(ExitStack())
        adj = sb("adj", [P, 2, N], c=scan)
        base = sb("base", [P, CAND], c=scan)
        we = sb("we", [P, H], c=scan)
        adj_in = [sem(f"adj_in{u}") for u in range(2)]
        consts_in = sem("a_consts_in")

        with ExitStack() as c1:
            w_nat = sb("w_nat", [P, 2, C], c=c1)
            a_bd = sb("a_bd", [P, 2, 2 * H], c=c1)
            w_cat = sb("w_cat", [P, 2, ROW + H], c=c1)
            wr_t = sb("wr_t", [P, 2, C], c=c1)
            br = sb("br", [P, C], c=c1)
            be = sb("be", [P, H], c=c1)
            wx = sb("wx", [G, H, C], c=c1)
            ws_t = sb("ws_t", [G, G], c=c1)
            bx = sb("bx", [G, H], c=c1)
            bx_wide = sb("bx_wide", [G, H, P], c=c1)
            bs = sb("bs", [P, G], c=c1)
            temp = sb("temp", [P, H], c=c1)
            xn = sb("xn", [P, 4, C], c=c1)
            xn_t = sb("xn_t", [P, 4, C], c=c1)
            row_out = sb("row_out", [P, 2, ROW], c=c1)
            p_t = [ps(f"p_t{u}", [P, C], c1) for u in range(2)]
            p_h = [ps(f"p_h{u}", [P, ROW + H], c1) for u in range(2)]
            p_r = [ps(f"p_r{u}", [P, C], c1) for u in range(2)]
            p_w = ps("p_w", [P, S], c1)
            p_v = ps("p_v", [P, S], c1)

            weights_in = sem("weights_in")
            x_in = sem("x_in")
            prep_pe, prep_dve = sem("prep_pe"), sem("prep_dve")
            xn_done, xt_done, xt_copied = sem("xn_done"), sem("xt_done"), sem("xt_copied")
            h_done, h_copied = sem("h_done"), sem("h_copied")
            r_done, r_added, br_added = sem("r_done"), sem("r_added"), sem("br_added")
            row_stored = [sem(f"row_stored{u}") for u in range(2)]
            residual_stored = sem("residual_stored")
            norm = Norm("first")
            loads = [
                (ident[:], t["ident"]), (ones[:], t["ones"]),
                (w_nat[:], t["W"].rearrange("(b p) i -> p b i", p=P)),
                (a_bd[:], t["a_bd"].rearrange("(b p) i -> p b i", p=P)),
                (w_cat[:, :, 0:C], t["W_t"].rearrange("(b p) i -> p b i", p=P)),
                (wr_t[:], t["Wr_t"].rearrange("(b p) i -> p b i", p=P)),
                (br[:], t["br"]), (be[:], t["be"]),
                (wx[:], t["W_x"].rearrange("(h p) i -> p h i", p=G)),
                (ws_t[:], t["W_slice_t"]), (bx[:], t["b_x_t"]), (bs[:], t["b_slice"]), (temp[:], t["temp"]),
            ]
            with nc.Block() as block:
                @block.sync
                def _(sp):
                    xr = t["x"].rearrange("(t p) c -> p t c", p=P)
                    rr = residual_rows.rearrange("(t p) c -> p t c", p=P)

                    def load_piece(q):
                        at = q * TQ if isinstance(q, int) else sp.snap(q * TQ)
                        wait(sp, x_in, q * 16)
                        sp.dma_start(x_sb[:, ds(at, TQ), :], xr[:, ds(at, TQ), :]).then_inc(x_in, 16)

                    def store_piece(q):
                        at = q * TQ if isinstance(q, int) else sp.snap(q * TQ)
                        sp.wait_ge(r_added, (q + 1) * TQ)
                        sp.dma_start(rr[:, ds(at, TQ), :], x_sb[:, ds(at, TQ), :]).then_inc(residual_stored, 16)

                    load_piece(0)
                    for dst, src in loads:
                        sp.dma_start(dst, src).then_inc(weights_in, 16)
                    load_piece(1)

                    def piece(q, more):
                        if more:
                            load_piece(q + 2)
                        for j in range(TQ):
                            rows = (q * TQ + j) * P
                            rows = rows if isinstance(rows, int) else sp.snap(rows)
                            sp.wait_ge(h_copied, q * TQ + j + 1)
                            sp.dma_start(node_table[ds(rows, P), :], row_out[:, j % 2, :]).then_inc(row_stored[j % 2], 16)
                        store_piece(q)
                    if XQ > 2:
                        piece(0, True)
                    if XQ > 3:
                        with sp.Fori(1, XQ - 2) as q:
                            piece(q, True)
                    piece(XQ - 2, False)
                    piece(XQ - 1, False)
                    sp.dma_start(base[:], t["cand_base"]).then_inc(consts_in, 16)
                    sp.dma_start(we[:], t["We"]).then_inc(consts_in, 16)
                    for u in range(2):
                        sp.dma_start(adj[:, u, :], t["adj"][u * P:(u + 1) * P, :]).then_inc(adj_in[u], 16)
                    for u in range(2):
                        sp.wait_ge(row_stored[u], 16 * (NT // 2))
                    sp.wait_ge(residual_stored, 16 * XQ)

                @block.tensor
                def _(pe):
                    pe.wait_ge(weights_in, 16 * len(loads))
                    for c in range(2):
                        for b in range(2):
                            mm = pe.matmul(p_w[:, c * 2 * H:(c + 1) * 2 * H], w_nat[:, b, c * P:(c + 1) * P],
                                           a_bd[:, b, :], start=b == 0, stop=b == 1)
                    mm.then_inc(prep_pe, 1)
                    pe.wait_ge(prep_dve, 1)
                    for h in range(H):
                        mm = pe.matmul(p_v[:, h * G:(h + 1) * G], bx_wide[:, h, :], ws_t[:], start=True, stop=True)
                    mm.then_inc(prep_pe, 1)
                    for c in range(2):
                        pe.wait_ge(prep_dve, 3 + c)
                        for h in range(H):
                            mm = pe.matmul(p_w[:, h * G:(h + 1) * G], wx[:, h, c * P:(c + 1) * P], ws_t[:],
                                           start=True, stop=True)
                        mm.then_inc(prep_pe, 1)
                    def turn(tile, j):
                        pe.wait_ge(xn_done, tile + 1)
                        wait(pe, xt_copied, tile - 1)
                        for b in range(2):
                            mm = pe.transpose(p_t[j % 2][:, b * P:(b + 1) * P], xn[:, j % 4, b * P:(b + 1) * P], ident[:])
                        mm.then_inc(xt_done, 1)

                    def products(tile, j):
                        u = j % 2
                        pe.wait_ge(xt_copied, tile + 1)
                        wait(pe, h_copied, tile - 1)
                        wait(pe, r_added, tile - 1)
                        for b in range(2):
                            mm = pe.matmul(p_h[u][:], xn_t[:, j % 4, b * P:(b + 1) * P], w_cat[:, b, :],
                                           start=b == 0, stop=b == 1)
                        mm.then_inc(h_done, 1)
                        for b in range(2):
                            mm = pe.matmul(p_r[u][:], xn_t[:, j % 4, b * P:(b + 1) * P], wr_t[:, b, :],
                                           start=b == 0, stop=b == 1)
                        mm.then_inc(r_done, 1)

                    def piece(q, last):
                        for j in range(TQ):
                            if not last or j + 2 < TQ:
                                turn(q * TQ + j + 2, j + 2)
                            products(q * TQ + j, j)
                    turn(0, 0)
                    turn(1, 1)
                    by_piece(pe, XQ, piece)

                @block.scalar
                def _(act):
                    def copy_rows(tile, j):
                        wait(act, r_done, tile - 3)
                        act.wait_ge(xt_done, tile + 1)
                        nc.scalar.copy(xn_t[:, j % 4, :], p_t[j % 2][:]).then_inc(xt_copied, 1)

                    def copy_features(tile, u):
                        wait(act, row_stored[u], (tile - u) * 8)
                        act.wait_ge(h_done, tile + 1)
                        nc.scalar.copy(row_out[:, u, :], p_h[u][:, 0:ROW]).then_inc(h_copied, 1)

                    def piece(q, last):
                        for j in range(TQ):
                            if not last or j + 2 < TQ:
                                copy_rows(q * TQ + j + 2, j + 2)
                            copy_features(q * TQ + j, j % 2)
                            if j == 2 and not last:
                                norm.root(act, q + 1)
                    norm.root(act, 0)
                    copy_rows(0, 0)
                    copy_rows(1, 1)
                    by_piece(act, XQ, piece)

                @block.vector
                def _(dve):
                    dve.wait_ge(x_in, 16)
                    for j in range(4):
                        norm.turn(dve, 0, j)
                    step = Steps(dve, prep_dve)
                    dve.wait_ge(weights_in, 16 * len(loads))
                    step(nc.vector.tensor_copy(bx_wide[:], bx[:].unsqueeze(2).broadcast_to([G, H, P])))
                    step(nc.vector.tensor_scalar(temp[:], temp[:], 1e-6, None, ALU.max))
                    dve.wait_ge(prep_pe, 1)
                    step(nc.vector.tensor_copy(w_cat[:, :, C:ROW + H], p_w[:, 0:4 * H].rearrange("p (c a) -> p c a", c=2)))
                    dve.wait_ge(prep_pe, 2)
                    rt = temp[:].unsqueeze(2).broadcast_to([P, H, G])
                    bc3 = bc[:].rearrange("p (h g) -> p h g", h=H)
                    recip = sem("recip")
                    nc.vector.reciprocal(temp[:], temp[:]).then_inc(recip, 1)
                    dve.wait_ge(recip, 1)
                    for c in range(2):
                        dve.wait_ge(prep_pe, 3 + c)
                        step(nc.vector.tensor_tensor(wct[:, c, :].rearrange("p (h g) -> p h g", h=H),
                                                     p_w[:].rearrange("p (h g) -> p h g", h=H), rt, ALU.mult))
                    step(nc.vector.tensor_tensor(bc3, p_v[:].rearrange("p (h g) -> p h g", h=H),
                                                 bs[:].unsqueeze(1).broadcast_to([P, H, G]), ALU.add))
                    step(nc.vector.tensor_tensor(bc3, bc3, rt, ALU.mult))
                    norm.invert(dve, 0)

                    def normalise(tile, j, q):
                        wait(dve, xt_done, tile - 3)
                        norm.normalise(dve, xn[:, j % 4, :], tile, q).then_inc(xn_done, 1)

                    def residual(tile, u):
                        dve.wait_ge(h_copied, tile + 1)
                        nc.vector.tensor_tensor(flat(src_score[:, ds(tile, 1), :]),
                                                p_h[u][:, ROW:ROW + H], be[:], ALU.add)
                        dve.wait_ge(r_done, tile + 1)
                        dve.wait_ge(br_added, tile + 1)
                        xt = flat(x_sb[:, ds(tile, 1), :])
                        nc.vector.tensor_tensor(xt, xt, p_r[u][:], ALU.add).then_inc(r_added, 1)

                    def piece(q, last):
                        for j in range(TQ):
                            if not last:
                                if j == 0:
                                    dve.wait_ge(x_in, (q + 2) * 16)
                                norm.turn(dve, q + 1, j)
                            if j + AHEAD < TQ:
                                normalise(q * TQ + j + AHEAD, j + AHEAD, q)
                            elif not last:
                                normalise(q * TQ + j + AHEAD, j + AHEAD, q + 1)
                            residual(q * TQ + j, j % 2)
                    AHEAD = 3
                    for j in range(AHEAD):
                        normalise(j, j, 0)
                    by_piece(dve, XQ, piece)

                @block.gpsimd
                def _(pool):
                    pool.wait_ge(weights_in, 16 * len(loads))
                    with pool.Fori(0, NT) as i:
                        pool.wait_ge(xn_done, i + 1)
                        xt = flat(x_sb[:, ds(i, 1), :])
                        nc.gpsimd.tensor_tensor(xt, xt, br[:], ALU.add).then_inc(br_added, 1)

        with ExitStack() as c2:
            near = sb("near", [P, 2, K, ROW], c=c2)
            vals = sb("vals", [P, 2, CAND], c=c2)
            where = sb("where", [P, 2, CAND], U32, c=c2)
            keys = sb("keys", [P, 4, CAND], c=c2)
            key = sb("key", [P, 2, 4 * 8], c=c2)
            edge = sb("edge", [P, K], c=c2)
            column = sb("column", [P, 2, K], U32, c=c2)
            none = sb("none", [P, K], c=c2)
            picked = sb("picked", [P, K, CAND], c=c2)
            z = sb("z", [P, K, H], c=c2)
            edge_score = sb("edge_score", [P, K, H], c=c2)
            gone = sb("gone", [P, 2, K], c=c2)
            w = sb("w", [P, 2, K, H], c=c2)
            stat = sb("stat", [P, 3, H], c=c2)
            p_o = [ps(f"p_o{u}", [P, C], c2) for u in range(2)]

            adj_read = sem("adj_read")
            columns_done = sem("columns_done")
            near_in = [sem(f"near_in{u}") for u in range(2)]
            w_done, w_normed = sem("w_done"), sem("w_normed")
            near_scaled_v, near_scaled_p, near_scaled_a = sem("near_scaled_v"), sem("near_scaled_p"), sem("near_scaled_a")
            summed, added = sem("summed"), sem("added")
            maxed, listed, picked_all, soft = sem("maxed"), sem("listed"), sem("picked_all"), sem("soft")
            cleared = sem("near_cleared")
            gate, pool_gate = sem("gate"), sem("pool_gate")
            flag_max, flag_all, flag_done = sem("flag_max"), sem("flag_all"), sem("flag_done")

            def scale_rows(eng, u, g):
                ks = slice(g * GR, (g + 1) * GR)
                rows = near[:, u, ks, 0:C].rearrange("p k (h d) -> p k h d", h=H)
                return eng.tensor_tensor(rows, rows, w[:, u, ks, :].unsqueeze(3).broadcast_to([P, GR, H, D]), ALU.mult)

            with nc.Block() as block:
                @block.sync
                def _(sp):
                    with sp.Fori(1, NT // 2) as i:
                        for u in range(2):
                            rows = sp.snap((i * 2 + u) * P)
                            sp.wait_ge(adj_read, i * 2 + u - 1)
                            sp.dma_start(adj[:, u, :], t["adj"][ds(rows, P), :]).then_inc(adj_in[u], 16)

                @block.vector
                def _(dve):
                    listing, softening = Chain(dve, listed, gate), Chain(dve, soft, gate)
                    dve.wait_ge(consts_in, 32)
                    v = nc.vector
                    LIST, SOFT = 10, 9

                    def largest(tile, u, i, c):
                        if c == 0:
                            dve.wait_ge(adj_in[u], (i + 1) * 16)
                            wait(dve, picked_all, tile - 1)
                            dve.sem_inc(gate, 1)
                        ins = v.max(vals[:, u, 8 * c:8 * c + 8], adj[:, u, bounds[c]:bounds[c + 1]])
                        if c == NCH - 1:
                            ins.then_inc(maxed, 1)

                    def locate(tile, u, c):
                        if c == 0:
                            dve.wait_ge(maxed, tile + 1)
                            dve.sem_inc(gate, 1)
                        at = slice(8 * c, 8 * c + 8)
                        ins = v.max_index(where[:, u, at], vals[:, u, at], adj[:, u, bounds[c]:bounds[c + 1]])
                        if c == NCH - 1:
                            ins.then_inc(adj_read, 1)

                    def compact(tile, u, n):
                        chain = listing.at(tile * LIST, n)
                        if n == 0:
                            dve.wait_ge(adj_read, tile + 1)
                            chain.step(v.tensor_tensor(keys[:, 3, :], where[:, u, :], base[:], ALU.add))
                        elif n == 1:
                            chain.after_last().step(v.scalar_tensor_tensor(keys[:, 0, :], vals[:, u, :], 0.0, keys[:, 3, :],
                                                                           ALU.is_gt, ALU.mult))
                        elif n < 8:
                            r = (n - 2) // 2
                            at = slice(8 * r, 8 * r + 8)
                            chain.after_last()
                            if n % 2 == 0:
                                chain.step(v.max(key[:, u, at], keys[:, r, :]))
                            else:
                                chain.step(v.match_replace(keys[:, r + 1, :], key[:, u, at], keys[:, r, :], 0.0))
                        elif n == 8:
                            chain.after_last().step(v.max(key[:, u, K:K + 8], keys[:, 3, :]))
                            chain.step(v.tensor_scalar(none[:], key[:, u, 0:K], 0.0, 4.0 * N, ALU.is_equal, ALU.mult))
                        elif n == 9:
                            chain.at(tile * LIST, LIST).after_last()
                            v.scalar_tensor_tensor(column[:, u, :], none[:], -1.0, key[:, u, 0:K],
                                                   ALU.add, ALU.add).then_inc(columns_done, 1)
                        elif n == 10:
                            v.tensor_reduce(over[:, 0, ds(tile, 1)], vals[:, u, :].rearrange("p (c e) -> p c e", e=8)[:, :, 7],
                                            AX.X, ALU.max)
                            v.tensor_copy(over[:, 1, ds(tile, 1)], key[:, u, K:K + 1])
                            v.tensor_scalar(gone[:, u, :], key[:, u, 0:K], 0.0, -BIG, ALU.is_equal, ALU.mult)

                    def pick(tile, u, k):
                        ins = v.scalar_tensor_tensor(picked[:, k, :], keys[:, 0, :], key[:, u, k:k + 1], vals[:, u, :],
                                                     ALU.is_equal, ALU.mult, accum_out=edge[:, k:k + 1])
                        if k == K - 1:
                            ins.then_inc(picked_all, 1)

                    def soften(tile, u, i, n):
                        chain = softening.at(tile * SOFT, n)
                        if n == 0:
                            dve.wait_ge(picked_all, tile + 1)
                            chain.step(v.tensor_tensor(edge_score[:], edge[:].unsqueeze(2).broadcast_to([P, K, H]),
                                                       we[:].unsqueeze(1).broadcast_to([P, K, H]), ALU.mult))
                        elif n == 1:
                            dve.wait_ge(near_in[u], (i + 1) * 16 * K)
                            chain.step(v.tensor_tensor(z[:], near[:, u, :, C:ROW],
                                                       src_score[:, ds(tile, 1), :].broadcast_to([P, K, H]), ALU.add))
                        elif n == 2:
                            chain.after_last().step(v.tensor_tensor(z[:], z[:], edge_score[:], ALU.add))
                        elif n == 3:
                            chain.after_last().step(v.scalar_tensor_tensor(z[:], z[:], 0.2, z[:], ALU.mult, ALU.max))
                        elif n == 4:
                            chain.after_last().step(v.tensor_tensor(z[:], z[:], gone[:, u, :].unsqueeze(2).broadcast_to([P, K, H]),
                                                                    ALU.add))
                        elif n == 5:
                            chain.after_last().step(v.tensor_reduce(stat[:, 0, :], z[:].rearrange("p k h -> p h k"), AX.X, ALU.max))
                        elif n == 6:
                            chain.after_last()
                            chain.step(v.tensor_tensor(z[:], z[:], stat[:, 0, :].unsqueeze(1).broadcast_to([P, K, H]),
                                                       ALU.subtract))
                        elif n == 7:
                            dve.wait_ge(w_done, tile + 1)
                            chain.step(v.tensor_reduce(stat[:, 1, :], w[:, u, :, :].rearrange("p k h -> p h k"), AX.X, ALU.add))
                        elif n == 8:
                            chain.after_last().step(v.reciprocal(stat[:, 2, :], stat[:, 1, :]))
                        elif n == 9:
                            chain.after_last()
                            v.tensor_tensor(w[:, u, :, :], w[:, u, :, :], stat[:, 2, :].unsqueeze(1).broadcast_to([P, K, H]),
                                            ALU.mult).then_inc(w_normed, 1)
                        elif n - 10 < len(BY_VECTOR):
                            if n == 10:
                                dve.wait_ge(w_normed, tile + 1)
                            scale_rows(v, u, BY_VECTOR[n - 10]).then_inc(near_scaled_v, 1)

                    def add(tile, u):
                        dve.wait_ge(summed, (tile + 1) * GROUPS)
                        xt = flat(x_sb[:, ds(tile, 1), :])
                        v.tensor_tensor(xt, xt, p_o[u][:], ALU.add).then_inc(added, 1)

                    def turn(t, u, i):
                        for c in range(NCH):
                            if has(t, NT):
                                largest(t, u, i, c)
                            if has(t - 1, NT):
                                compact(t - 1, 1 - u, c)
                            if has(t - 2, NT) and c == 0:
                                soften(t - 2, u, i - 1, 0)
                        for c in range(NCH):
                            if has(t, NT):
                                locate(t, u, c)
                            if has(t - 1, NT):
                                if c == 0:
                                    dve.wait_ge(columns_done, t)
                                    wait(dve, soft, (t - 2) * SOFT + 1)
                                for k in range(c * K // NCH, (c + 1) * K // NCH):
                                    pick(t - 1, 1 - u, k)
                            if has(t - 2, NT) and c > 0:
                                soften(t - 2, u, i - 1, c)
                            if has(t - 3, NT) and c == NCH - 2:
                                add(t - 3, 1 - u)

                    for t in range(4):
                        turn(t, t % 2, t // 2)
                    with dve.Fori(2, NT // 2) as i:
                        for u in range(2):
                            turn(i * 2 + u, u, i)
                    for t in range(NT, NT + 3):
                        turn(t, t % 2, t // 2)
                    nc.vector.tensor_reduce(over_flag[:], over[:].rearrange("p a t -> p (a t)"), AX.X, ALU.max).then_inc(flag_max, 1)
                    dve.wait_ge(flag_all, 1)
                    nc.vector.tensor_scalar(over_int[:], over_flag[:], 0.0, None, ALU.is_gt).then_inc(flag_done, 1)
                    dve.wait_ge(flag_done, 1)

                @block.scalar
                def _(act):
                    def pair(i):
                        for u in range(2):
                            tile = i * 2 + u
                            act.wait_ge(soft, tile * 9 + 7)
                            wait(act, near_scaled_p, (tile - 1) * len(BY_POOL))
                            nc.scalar.activation(w[:, u, :, :], z[:], ACT.Exp).then_inc(w_done, 1)
                            act.wait_ge(w_normed, tile + 1)
                            for g in BY_SCALAR:
                                for k in range(g * GR, (g + 1) * GR):
                                    for h in range(H):
                                        part = near[:, u, k, h * D:(h + 1) * D]
                                        ins = nc.scalar.mul(part, part, w[:, u, k, h:h + 1])
                                ins.then_inc(near_scaled_a, 1)
                    loop(act, NT // 2, pair)

                @block.gpsimd
                def _(pool):
                    nc.gpsimd.memset(near[:], 0.0).then_inc(cleared, 1)
                    pool.wait_ge(cleared, 1)

                    def gather(tile, u):
                        pool.wait_ge(columns_done, tile + 1)
                        pool.sem_inc(pool_gate, 1)
                        for g in range(GROUPS):
                            if not isinstance(tile, int) or tile >= 2:
                                pool.wait_ge(summed, (tile - 2) * GROUPS + g + 1)
                                pool.sem_inc(pool_gate, 1)
                            for k in range(g * GR, (g + 1) * GR):
                                pool.indirect_dma_start(
                                    out=near[:, u, k, :], out_offset=None, in_=node_table,
                                    in_offset=bass.IndirectOffsetOnAxis(ap=column[:, u, k:k + 1], axis=0),
                                    bounds_check=N - 1, oob_is_err=False).then_inc(near_in[u], 16)

                    def scale(tile, u):
                        pool.wait_ge(w_normed, tile + 1)
                        for g in BY_POOL:
                            scale_rows(nc.gpsimd, u, g).then_inc(near_scaled_p, 1)

                    def pair(i):
                        gather(i * 2 + 1, 1)
                        scale(i * 2, 0)
                        gather(i * 2 + 2, 0)
                        scale(i * 2 + 1, 1)
                    gather(0, 0)
                    loop(pool, NT // 2 - 1, pair)
                    gather(NT - 1, 1)
                    scale(NT - 2, 0)
                    scale(NT - 1, 1)
                    pool.wait_ge(flag_max, 1)
                    nc.gpsimd.partition_all_reduce(over_flag[:], over_flag[:], P, bass.bass_isa.ReduceOp.max).then_inc(flag_all, 1)

                @block.tensor
                def _(pe):
                    def pair(i):
                        for u in range(2):
                            tile = i * 2 + u
                            wait(pe, added, tile - 1)
                            for groups, scaled in ((BY_VECTOR, near_scaled_v), (BY_POOL, near_scaled_p), (BY_SCALAR, near_scaled_a)):
                                for n, g in enumerate(groups):
                                    pe.wait_ge(scaled, tile * len(groups) + n + 1)
                                    for k in range(g * GR, (g + 1) * GR):
                                        mm = pe.matmul(p_o[u][:], ident[:], near[:, u, k, 0:C], start=k == 0, stop=k == K - 1)
                                    mm.then_inc(summed, 1)
                    loop(pe, NT // 2, pair)

        scan.close()
        JB = 4 * P
        NJ = N // JB
        flag = nc.values_load(over_int[0:1, 0:1], min_val=0, max_val=1)
        with nc.If(flag > 0), ExitStack() as c3:
            a = sb("d_adj", [P, JB], c=c3)
            absent = sb("absent", [P, JB], c=c3)
            nodes = sb("nodes", [P, 4, ROW], c=c3)
            we = sb("d_we", [P, H], c=c3)
            dst_wide = sb("dst_wide", [P, 4, H, P], c=c3)
            z = sb("d_z", [P, H, JB], c=c3)
            w = sb("d_w", [P, H, JB], c=c3)
            w_t = sb("d_w_t", [P, H, 4, P], c=c3)
            stat = sb("d_stat", [P, 8, H], c=c3)
            MAX, BLOCK_MAX, NEW_MAX, DROP, KEEP, SUM, BLOCK_SUM, INV = range(8)
            acc = sb("acc", [P, C], c=c3)
            p_d = [ps(f"p_d{u}", [P, JB], c3) for u in range(2)]
            p_x = [ps(f"p_x{u}", [P, JB], c3) for u in range(2)]
            p_a = ps("p_a", [P, C], c3)
            d_in, base_in, d_gate, d_gate_v = sem("d_in"), sem("base_in"), sem("d_gate"), sem("d_gate_v")
            dv, dp, da_ = sem("dense_dve"), sem("dense_pe"), sem("dense_act")
            BEGIN, BLOCK, END = 3, 24, 3
            TILE = BEGIN + NJ * BLOCK + END

            with nc.Block() as block:
                @block.sync
                def _(sp):
                    sp.dma_start(we[:], t["We"]).then_inc(base_in, 16)
                    rr = residual_rows.rearrange("(t p) c -> p t c", p=P)
                    sp.dma_start(x_sb[:], rr).then_inc(base_in, 16)
                    with sp.Fori(0, NT) as i:
                        with sp.Fori(0, NJ) as j:
                            row, col = sp.snap(i * P), sp.snap(j * JB)
                            sp.wait_ge(dv, i * TILE + BEGIN + j * BLOCK)
                            sp.sem_inc(d_gate, 1)
                            sp.dma_start(a[:], t["adj"][ds(row, P), ds(col, JB)]).then_inc(d_in, 16)
                            sp.dma_start(nodes[:], node_table[ds(col, JB), :].rearrange("(b p) c -> p b c", p=P)).then_inc(d_in, 16)

                @block.vector
                def _(dve):
                    v = nc.vector
                    step = Steps(dve, dv, d_gate_v)
                    dve.wait_ge(base_in, 32)

                    def last(ap, n):
                        return ap.unsqueeze(2).broadcast_to([P, ap.shape[1], n])
                    with dve.Fori(0, NT) as i:
                        step.base, step.n = i * TILE, 0
                        step(v.memset(stat[:, MAX, :], -BIG))
                        step(v.memset(stat[:, SUM, :], 0.0))
                        step(v.memset(acc[:], 0.0))
                        assert step.n == BEGIN
                        with dve.Fori(0, NJ) as j:
                            step.base, step.n = i * TILE + j * BLOCK + BEGIN, 0
                            block_at = i * NJ + j
                            dve.wait_ge(d_in, (block_at + 1) * 32)
                            for b in range(4):
                                ins = v.tensor_copy(dst_wide[:, b, :, :], last(nodes[:, b, C:ROW], P))
                            step(ins)
                            step(v.tensor_scalar(absent[:], a[:], 0.0, -1.0, ALU.is_gt, ALU.add))
                            for h in range(H):
                                dve.wait_ge(dp, block_at * 17 + h + 1)
                                step(v.scalar_tensor_tensor(z[:, h, :], a[:], we[:, h:h + 1], p_d[h % 2][:], ALU.mult, ALU.add))
                            step(v.tensor_tensor(z[:], z[:], last(flat(src_score[:, ds(i, 1), :]), JB), ALU.add))
                            step(v.scalar_tensor_tensor(z[:], z[:], 0.2, z[:], ALU.mult, ALU.max))
                            step(v.scalar_tensor_tensor(z[:], absent[:].unsqueeze(1).broadcast_to([P, H, JB]), BIG, z[:],
                                                        ALU.mult, ALU.add))
                            step(v.tensor_reduce(stat[:, BLOCK_MAX, :], z[:], AX.X, ALU.max))
                            step(v.tensor_tensor(stat[:, NEW_MAX, :], stat[:, MAX, :], stat[:, BLOCK_MAX, :], ALU.max))
                            step(v.tensor_tensor(stat[:, DROP, :], stat[:, MAX, :], stat[:, NEW_MAX, :], ALU.subtract))
                            step(v.tensor_copy(stat[:, MAX, :], stat[:, NEW_MAX, :]))
                            step(v.tensor_tensor(z[:], z[:], last(stat[:, NEW_MAX, :], JB), ALU.subtract))
                            assert step.n == 18
                            dve.wait_ge(da_, block_at * 10 + 2)
                            step(v.tensor_reduce(stat[:, BLOCK_SUM, :], w[:], AX.X, ALU.add))
                            step(v.tensor_tensor(stat[:, SUM, :], stat[:, SUM, :], stat[:, KEEP, :], ALU.mult))
                            step(v.tensor_tensor(stat[:, SUM, :], stat[:, SUM, :], stat[:, BLOCK_SUM, :], ALU.add))
                            acc3 = acc[:].rearrange("p (h d) -> p h d", h=H)
                            step(v.tensor_tensor(acc3, acc3, last(stat[:, KEEP, :], D), ALU.mult))
                            dve.wait_ge(dp, block_at * 17 + 17)
                            step(v.tensor_tensor(acc[:], acc[:], p_a[:], ALU.add))
                            step(v.tensor_copy(stat[:, DROP, :], stat[:, KEEP, :]))
                            assert step.n == BLOCK
                        step.base, step.n = i * TILE + BEGIN + NJ * BLOCK, 0
                        step(v.reciprocal(stat[:, INV, :], stat[:, SUM, :]))
                        acc3 = acc[:].rearrange("p (h d) -> p h d", h=H)
                        step(v.tensor_tensor(acc3, acc3, last(stat[:, INV, :], D), ALU.mult))
                        xt = flat(x_sb[:, ds(i, 1), :])
                        step(v.tensor_tensor(xt, xt, acc[:], ALU.add))

                @block.scalar
                def _(act):
                    with act.Fori(0, NT) as i:
                        with act.Fori(0, NJ) as j:
                            block_at = i * NJ + j
                            act.wait_ge(dv, i * TILE + BEGIN + j * BLOCK + 18)
                            nc.scalar.activation(w[:], z[:], ACT.Exp).then_inc(da_, 1)
                            nc.scalar.activation(stat[:, KEEP, :], stat[:, DROP, :], ACT.Exp).then_inc(da_, 1)
                            for h in range(H):
                                act.wait_ge(dp, block_at * 17 + 8 + h + 1)
                                nc.scalar.copy(w_t[:, h, :, :].rearrange("p b i -> p (b i)"), p_x[h % 2][:]).then_inc(da_, 1)

                @block.tensor
                def _(pe):
                    with pe.Fori(0, NT) as i:
                        with pe.Fori(0, NJ) as j:
                            block_at = i * NJ + j
                            dve_at = i * TILE + BEGIN + j * BLOCK
                            for h in range(H):
                                pe.wait_ge(dv, dve_at + (1 if h < 2 else h + 1))
                                for b in range(4):
                                    mm = pe.matmul(p_d[h % 2][:, b * P:(b + 1) * P], dst_wide[:, b, h, :], ident[:],
                                                   start=True, stop=True)
                                mm.then_inc(dp, 1)
                            for h in range(H):
                                pe.wait_ge(da_, block_at * 10 + (2 if h < 2 else h + 1))
                                for b in range(4):
                                    mm = pe.transpose(p_x[h % 2][:, b * P:(b + 1) * P], w[:, h, b * P:(b + 1) * P], ident[:])
                                mm.then_inc(dp, 1)
                            pe.wait_ge(da_, block_at * 10 + 10)
                            for h in range(H):
                                for b in range(4):
                                    mm = pe.matmul(p_a[:, h * D:(h + 1) * D], w_t[:, h, b, :], nodes[:, b, h * D:(h + 1) * D],
                                                   start=b == 0, stop=b == 3)
                            mm.then_inc(dp, 1)

                @block.gpsimd
                def _(pool):
                    pool.wait_ge(base_in, 32)
        slice_sum = sb("slice_sum", [P, S])
        t1 = sb("t1", [P, 2, S])
        with ExitStack() as c4:
            xn = sb("b_xn", [P, 4, C], c=c4)
            xn_t = sb("b_xn_t", [P, 2, C], c=c4)
            logit = sb("logit", [P, 2, S], c=c4)
            ex = sb("ex", [P, 2, S], c=c4)
            sw = sb("sw", [P, 2, S], c=c4)
            sw_t = sb("sw_t", [P, 2, S], c=c4)
            top = sb("top", [P, 3, H], c=c4)
            p_t = [ps(f"b_p_t{u}", [P, C], c4) for u in range(2)]
            p_l = [ps(f"p_l{u}", [P, S], c4) for u in range(2)]
            p_s = [ps(f"p_s{u}", [P, S], c4) for u in range(2)]
            p_1 = [ps(f"p_1{b}", [P, S], c4) for b in range(2)]
            norm = Norm("second")
            xn_done, xt_done, xt_copied = sem("b_xn_done"), sem("b_xt_done"), sem("b_xt_copied")
            logit_done, shifted, ex_done = sem("logit_done"), sem("shifted"), sem("ex_done")
            sw_done, t1_done, swt_done, swt_copied = sem("sw_done"), sem("t1_done"), sem("swt_done"), sem("swt_copied")
            swt_stored = [sem(f"swt_stored{u}") for u in range(2)]
            shift_steps, weight_steps = sem("shift_steps"), sem("weight_steps")
            sum_done, t1_copied = sem("sum_done"), sem("t1_copied")

            def by_head(ap):
                return ap.rearrange("p (h g) -> p h g", h=H)

            with nc.Block() as block:
                @block.vector
                def _(dve):
                    def all_stats(q, last):
                        for j in range(4):
                            if j == 3 and (not isinstance(q, int) or q > 0):
                                norm.invert(dve, q - 1)
                            norm.turn(dve, q, j)
                    by_piece(dve, XQ, all_stats)
                    norm.invert(dve, XQ - 1)
                    shift_step, weight_step = Steps(dve, shift_steps), Steps(dve, weight_steps)

                    def normalise(tile, j):
                        wait(dve, t1_done, tile - 3)
                        norm.normalise(dve, xn[:, j, :], tile, XQ - 1).then_inc(xn_done, 1)

                    def shift(tile, u):
                        step = shift_step
                        step.base, step.n = tile * 2, 0
                        lg = by_head(logit[:, u, :])
                        dve.wait_ge(logit_done, tile + 1)
                        wait(dve, ex_done, tile - 1)
                        step(nc.vector.tensor_tensor(logit[:, u, :], p_l[u][:], bc[:], ALU.add))
                        step(nc.vector.tensor_reduce(top[:, 0, :], lg, AX.X, ALU.max))
                        nc.vector.tensor_tensor(lg, lg, top[:, 0, :].unsqueeze(2).broadcast_to([P, H, G]),
                                                ALU.subtract).then_inc(shifted, 1)

                    def weights(tile, u):
                        step = weight_step
                        step.base, step.n = tile * 2, 0
                        dve.wait_ge(ex_done, tile + 1)
                        step(nc.vector.tensor_reduce(top[:, 1, :], by_head(ex[:, u, :]), AX.X, ALU.add))
                        step(nc.vector.reciprocal(top[:, 2, :], top[:, 1, :]))
                        wait(dve, t1_done, tile - 1)
                        wait(dve, sum_done, tile - 1)
                        nc.vector.tensor_tensor(by_head(sw[:, u, :]), by_head(ex[:, u, :]),
                                                top[:, 2, :].unsqueeze(2).broadcast_to([P, H, G]),
                                                ALU.mult).then_inc(sw_done, 1)

                    normalise(0, 0)
                    normalise(1, 1)

                    def body(t, j, i):
                        if has(t, NT):
                            shift(t, j % 2)
                        if has(t - 1, NT):
                            weights(t - 1, (j - 1) % 2)
                        if has(t + 2, NT):
                            normalise(t + 2, (j + 2) % 4)
                    pipeline(dve, NT, body)
                    dve.wait_ge(t1_done, NT)
                    nc.vector.tensor_copy(t1[:, 0, :], p_1[0][:]).then_inc(t1_copied, 1)

                @block.scalar
                def _(act):
                    with act.Fori(0, XQ) as q:
                        norm.root(act, q)

                    def copy_rows(tile, u):
                        act.wait_ge(xt_done, tile + 1)
                        wait(act, logit_done, tile - 1)
                        nc.scalar.copy(xn_t[:, u, :], p_t[u][:]).then_inc(xt_copied, 1)

                    def exponentials(tile, u):
                        wait(act, sw_done, tile - 1)
                        act.wait_ge(shifted, tile + 1)
                        nc.scalar.activation(ex[:, u, :], logit[:, u, :], ACT.Exp).then_inc(ex_done, 1)

                    def copy_weights(tile, u, i):
                        wait(act, swt_stored[u], i * 16)
                        act.wait_ge(swt_done, tile + 1)
                        nc.scalar.copy(sw_t[:, u, :], p_s[u][:]).then_inc(swt_copied, 1)

                    copy_rows(0, 0)
                    copy_rows(1, 1)

                    def body(t, j, i):
                        if has(t, NT):
                            exponentials(t, j % 2)
                        if has(t - 1, NT):
                            copy_weights(t - 1, (j - 1) % 2, i * 2 + (j - 1) // 2)
                        if has(t + 2, NT):
                            copy_rows(t + 2, j % 2)
                    pipeline(act, NT, body)
                    act.wait_ge(t1_done, NT)
                    nc.scalar.copy(t1[:, 1, :], p_1[1][:]).then_inc(t1_copied, 1)

                @block.tensor
                def _(pe):
                    def turn(tile, u, j):
                        pe.wait_ge(xn_done, tile + 1)
                        wait(pe, xt_copied, tile - 1)
                        for b in range(2):
                            mm = pe.transpose(p_t[u][:, b * P:(b + 1) * P], xn[:, j, b * P:(b + 1) * P], ident[:])
                        mm.then_inc(xt_done, 1)

                    def logits(tile, u):
                        pe.wait_ge(xt_copied, tile + 1)
                        wait(pe, shifted, tile - 1)
                        for b in range(2):
                            mm = pe.matmul(p_l[u][:], xn_t[:, u, b * P:(b + 1) * P], wct[:, b, :], start=b == 0, stop=b == 1)
                        mm.then_inc(logit_done, 1)

                    def sums(tile, u, j):
                        first, last = isinstance(tile, int) and tile == 0, isinstance(tile, int) and tile == NT - 1
                        pe.wait_ge(sw_done, tile + 1)
                        wait(pe, swt_copied, tile - 1)
                        for q in range(4):
                            mm = pe.transpose(p_s[u][:, q * P:(q + 1) * P], sw[:, u, q * P:(q + 1) * P], ident[:])
                        mm.then_inc(swt_done, 1)
                        for b in range(2):
                            mm = pe.matmul(p_1[b][:], xn[:, j, b * P:(b + 1) * P], sw[:, u, :], start=first, stop=last)
                        mm.then_inc(t1_done, 1)

                    turn(0, 0, 0)
                    turn(1, 1, 1)
                    logits(0, 0)

                    def body(t, j, i):
                        if has(t + 1, NT):
                            logits(t + 1, (j + 1) % 2)
                        if has(t - 1, NT):
                            sums(t - 1, (j - 1) % 2, (j - 1) % 4)
                        if has(t + 2, NT):
                            turn(t + 2, j % 2, (j + 2) % 4)
                    pipeline(pe, NT, body)

                @block.gpsimd
                def _(pool):
                    pool.wait_ge(sw_done, 1)
                    nc.gpsimd.tensor_copy(slice_sum[:], sw[:, 0, :]).then_inc(sum_done, 1)

                    def add(tile, u):
                        pool.wait_ge(sw_done, tile + 1)
                        pool.wait_ge(sum_done, tile)
                        nc.gpsimd.tensor_tensor(slice_sum[:], slice_sum[:], sw[:, u, :], ALU.add).then_inc(sum_done, 1)
                    add(1, 1)
                    with pool.Fori(1, NT // 2) as i:
                        for u in range(2):
                            add(i * 2 + u, u)

                @block.sync
                def _(sp):
                    def pair(i):
                        for u in range(2):
                            tile = i * 2 + u
                            if not isinstance(tile, int):
                                tile = sp.snap(tile)
                            sp.wait_ge(swt_copied, tile + 1)
                            sp.dma_start(weights_t[ds(tile, 1), :, :].rearrange("a p s -> p (a s)"), sw_t[:, u, :]).then_inc(swt_stored[u], 16)
                    loop(sp, NT // 2, pair)
                    for u in range(2):
                        sp.wait_ge(swt_stored[u], 16 * (NT // 2))

        L = G
        z_out = sb("z_out", [P, 4, C])
        with ExitStack() as c5:
            def w5(name, shape):
                return sb(name, shape, c=c5)
            IN = 2 * S + 2 * NS + 2 * H
            X0, B0, C0, DT0 = S, 2 * S, 2 * S + NS, 2 * S + 2 * NS
            wfx_t, b_fx = w5("wfx_t", [P, 2, S]), w5("b_fx", [1, S])
            in_wt, how_t, ow_t = w5("in_wt", [P, 4, IN]), w5("how_t", [P, 4, S]), w5("ow_t", [P, 4, C])
            fcd_t = w5("fcd_t", [P, 4, H])
            cw_x, cb_x = w5("cw_x", [P, 4, KC]), w5("cb_x", [P, 4])
            cw_bc, cb_bc = w5("cw_bc", [NS, 2, KC]), w5("cb_bc", [NS, 2])
            dt_bias, a_log, d_skip = w5("dt_bias", [L, 2 * H]), w5("a_log", [L, H]), w5("d_skip", [L, H])
            norm_w = w5("norm_w", [L, S])
            upto, onward = w5("upto", [L, L]), w5("onward", [L, L])
            sum_row = w5("sum_row", [1, S])
            rsum, u_sb, u_t = w5("rsum", [L, H]), w5("u_sb", [L, S]), w5("u_t", [P, 4, L])
            pad_x, pad_bc = w5("pad_x", [P, 4, L + KC - 1]), w5("pad_bc", [NS, 2, L + KC - 1])
            conv_x, conv_bc = w5("conv_x", [P, 4, L]), w5("conv_bc", [NS, 2, L])
            tap_x, tap_bc = w5("tap_x", [P, 4, L]), w5("tap_bc", [NS, 2, L])
            act_x, act_bc = w5("act_x", [P, 4, L]), w5("act_bc", [NS, 2, L])
            dt, dt_abs, dt_exp, dt_one, dt_log = [w5(f"dt{i}", [L, 2 * H]) for i in range(5)]
            da, da_wide = w5("da", [L, 2 * H]), w5("da_wide", [L, 2 * H, L])
            cum, decay = w5("cum", [L, 2 * H]), w5("decay", [L, 2 * H, L])
            cb, mix, x_row = w5("cb", [L, L]), w5("mix", [L, H, L]), w5("x_row", [L, S])
            gain, y_sb, gate, sq = w5("gain", [L, H]), w5("y_sb", [L, S]), w5("gate", [L, S]), w5("sq", [L, S])
            ms, y_t, pairs = w5("ms", [L, 4]), w5("y_t", [P, 4, L]), w5("pairs", [P, 4, P])
            bank = [ps(f"bank{i}", [P, 512], c5) for i in range(8)]

            h_in = sem("h_in")
            hp, ha, hv = sem("hydra_pe"), sem("hydra_act"), sem("hydra_dve")
            loads5 = [
                (wfx_t[:], t["W_fx_t"].rearrange("(b p) i -> p b i", p=P)), (b_fx[:], t["b_fx"]),
                (in_wt[:], t["hy_in_t"].rearrange("(b p) i -> p b i", p=P)),
                (how_t[:], t["hy_out_t"].rearrange("(b p) i -> p b i", p=P)),
                (ow_t[:], t["out_w_t"].rearrange("(b p) i -> p b i", p=P)),
                (fcd_t[:], t["fcD_t"].rearrange("(b p) i -> p b i", p=P)),
                (cw_x[:], t["conv_w"][0:S, :].rearrange("(b p) i -> p b i", p=P)),
                (cb_x[:], t["conv_b_x"]),
                (cw_bc[:], t["conv_w"][S:S + 2 * NS, :].rearrange("(b p) i -> p b i", p=NS)),
                (cb_bc[:], t["conv_b_bc"]),
                (dt_bias[:], t["dt_bias"]), (a_log[:], t["A_log"]), (d_skip[:], t["hy_D"]), (norm_w[:], t["norm_w"]),
                (upto[:], t["upto"]), (onward[:], t["onward"]),
            ]
            h3 = lambda ap: ap.rearrange("p (h g) -> p h g", h=H)
            b4 = lambda ap: ap.rearrange("p (b l) -> p b l", b=4)
            mid = lambda ap, n, m: ap.unsqueeze(1).broadcast_to([m, n, ap.shape[1]])
            last = lambda ap, n: ap.unsqueeze(2).broadcast_to([ap.shape[0], ap.shape[1], n])

            with nc.Block() as block:
                @block.sync
                def _(sp):
                    for dst, src in loads5:
                        sp.dma_start(dst, src).then_inc(h_in, 16)

                @block.tensor
                def _(pe):
                    pe.wait_ge(h_in, 16 * len(loads5))
                    for h in range(H):
                        pe.matmul(bank[0][0:L, h:h + 1], slice_sum[:, h * G:(h + 1) * G], ones[:, 0:1], start=True, stop=True)
                    pe.matmul(bank[1][0:1, :], ones[:, 0:1], slice_sum[:], start=True, stop=True).then_inc(hp, 1)
                    pe.wait_ge(t1_copied, 2)
                    pe.wait_ge(ha, 1)
                    for h in range(H):
                        g = slice(h * G, (h + 1) * G)
                        for b in range(2):
                            pe.matmul(bank[2][0:L, g], t1[:, b, g], wfx_t[:, b, g], start=b == 0, stop=False)
                        mm = pe.matmul(bank[2][0:L, g], sum_row[0:1, g], b_fx[0:1, g], start=False, stop=True)
                    mm.then_inc(hp, 1)
                    pe.wait_ge(hv, 3)
                    for b in range(4):
                        mm = pe.transpose(bank[3][:, b * L:(b + 1) * L], u_sb[:, b * P:(b + 1) * P], ident[0:L, 0:L])
                    mm.then_inc(hp, 1)
                    pe.wait_ge(ha, 2)
                    for b in range(4):
                        pe.matmul(bank[4][0:L, :], u_t[:, b, :], in_wt[:, b, 0:S], start=b == 0, stop=b == 3)
                    for b in range(4):
                        pe.matmul(bank[5][0:L, 0:2 * H], u_t[:, b, :], in_wt[:, b, DT0:IN], start=b == 0, stop=b == 3)
                    for q in range(4):
                        for b in range(4):
                            pe.matmul(bank[6][:, q * L:(q + 1) * L], in_wt[:, b, X0 + q * P:X0 + (q + 1) * P], u_t[:, b, :],
                                      start=b == 0, stop=b == 3)
                    for q in range(2):
                        for b in range(4):
                            mm = pe.matmul(bank[7][0:NS, q * L:(q + 1) * L], in_wt[:, b, B0 + q * NS:B0 + (q + 1) * NS],
                                           u_t[:, b, :], start=b == 0, stop=b == 3)
                    mm.then_inc(hp, 1)
                    pe.wait_ge(hv, NV_DA)
                    pe.matmul(bank[0][0:L, 0:H], upto[:], da[:, 0:H], start=True, stop=True)
                    pe.matmul(bank[0][0:L, H:2 * H], onward[:], da[:, H:2 * H], start=True, stop=True)
                    for h in range(H):
                        pe.matmul(bank[1][0:L, h * L:(h + 1) * L], da_wide[:, h, :], upto[:], start=True, stop=True)
                        mm = pe.matmul(bank[2][0:L, h * L:(h + 1) * L], da_wide[:, H + h, :], onward[:], start=True, stop=True)
                    mm.then_inc(hp, 1)
                    pe.wait_ge(hv, NV_ACT)
                    pe.matmul(bank[3][0:L, 0:L], act_bc[:, 0, :], act_bc[:, 1, :], start=True, stop=True)
                    for b in range(4):
                        pe.transpose(bank[6][0:L, b * P:(b + 1) * P], act_x[:, b, :], ident[:])
                    for b in range(4):
                        mm = pe.matmul(bank[7][0:L, 0:H], act_x[:, b, :], fcd_t[:, b, :], start=b == 0, stop=b == 3)
                    mm.then_inc(hp, 1)
                    pe.wait_ge(hv, NV_MIX)
                    for h in range(H):
                        mm = pe.matmul(bank[5][0:L, h * G:(h + 1) * G], mix[:, h, :], x_row[:, h * G:(h + 1) * G],
                                       start=True, stop=True)
                    mm.then_inc(hp, 1)
                    pe.wait_ge(hv, NV_Y)
                    for b in range(4):
                        mm = pe.transpose(bank[3][:, b * L:(b + 1) * L], y_sb[:, b * P:(b + 1) * P], ident[0:L, 0:L])
                    mm.then_inc(hp, 1)
                    pe.wait_ge(ha, NA_YT)
                    for q in range(4):
                        for b in range(4):
                            mm = pe.matmul(bank[0][:, q * L:(q + 1) * L], how_t[:, b, q * P:(q + 1) * P], y_t[:, b, :],
                                           start=b == 0, stop=b == 3)
                    mm.then_inc(hp, 1)
                    pe.wait_ge(hv, NV_Y + 1)
                    for q in range(4):
                        mm = pe.matmul(bank[1 + q // 2][:, (q % 2) * C:(q % 2 + 1) * C], pairs[:, q, :], ow_t[:, q, :],
                                       start=True, stop=True)
                    mm.then_inc(hp, 1)

                @block.scalar
                def _(act):
                    step = Steps(act, ha)
                    act.wait_ge(h_in, 16 * len(loads5))
                    act.wait_ge(hp, 1)
                    step(nc.scalar.copy(sum_row[:], bank[1][0:1, :]))
                    act.wait_ge(hp, 3)
                    step(nc.scalar.copy(u_t[:].rearrange("p b l -> p (b l)"), bank[3][:, 0:4 * L]))
                    step(nc.scalar.activation(a_log[:], a_log[:], ACT.Exp))
                    act.wait_ge(hv, NV_ABS)
                    step(nc.scalar.activation(dt_exp[:], dt_abs[:], ACT.Exp, scale=-1.0))
                    act.wait_ge(hv, NV_ABS + 1)
                    step(nc.scalar.activation(dt_log[:], dt_one[:], ACT.Ln))
                    act.wait_ge(hv, NV_CONV)
                    nc.scalar.activation(tap_x[:], conv_x[:], ACT.Exp, scale=-1.0)
                    step(nc.scalar.activation(tap_bc[:], conv_bc[:], ACT.Exp, scale=-1.0))
                    step(nc.scalar.activation(gate[:], bank[4][0:L, :], ACT.Exp, scale=-1.0))
                    act.wait_ge(hp, 6)
                    step(nc.scalar.copy(x_row[:], bank[6][0:L, :]))
                    act.wait_ge(hv, NV_DECAY)
                    step(nc.scalar.activation(decay[:], decay[:], ACT.Exp))
                    act.wait_ge(hv, NV_MS)
                    step(nc.scalar.activation(ms[:, 2:3], ms[:, 1:2], ACT.Sqrt))
                    act.wait_ge(hp, 8)
                    step(nc.scalar.copy(y_t[:].rearrange("p b l -> p (b l)"), bank[3][:, 0:4 * L]))
                    act.wait_ge(hp, 10)
                    for q in range(2):
                        step(nc.scalar.copy(z_out[:, 2 * q:2 * q + 2, :].rearrange("p a c -> p (a c)"), bank[1 + q][:]))

                @block.vector
                def _(dve):
                    step = Steps(dve, hv)
                    v = nc.vector
                    dve.wait_ge(h_in, 16 * len(loads5))
                    dve.wait_ge(hp, 1)
                    step(v.tensor_scalar(rsum[:], bank[0][0:L, 0:H], 1e-5, None, ALU.add))
                    step(v.reciprocal(rsum[:], rsum[:]))
                    dve.wait_ge(hp, 2)
                    step(v.tensor_tensor(h3(u_sb[:]), h3(bank[2][0:L, :]), last(rsum[:], G), ALU.mult))
                    assert step.n == 3
                    step(v.memset(pad_x[:], 0.0))
                    step(v.memset(pad_bc[:], 0.0))
                    dve.wait_ge(hp, 4)
                    step(v.tensor_tensor(dt[:], bank[5][0:L, 0:2 * H], dt_bias[:], ALU.add))
                    step(v.scalar_tensor_tensor(dt_abs[:], dt[:], -1.0, dt[:], ALU.mult, ALU.max))
                    assert step.n == NV_ABS
                    dve.wait_ge(ha, 4)
                    step(v.tensor_scalar(dt_one[:], dt_exp[:], 1.0, None, ALU.add))
                    step(v.tensor_scalar(dt_abs[:], dt_one[:], -1.0, None, ALU.add))
                    step(v.tensor_tensor(dt_exp[:], dt_exp[:], dt_abs[:], ALU.subtract))
                    step(v.reciprocal(dt_abs[:], dt_one[:]))
                    step(v.tensor_tensor(dt_exp[:], dt_exp[:], dt_abs[:], ALU.mult))
                    step(v.scalar_tensor_tensor(dt[:], dt[:], 0.0, dt_exp[:], ALU.max, ALU.add))
                    dve.wait_ge(ha, 5)
                    step(v.tensor_tensor(dt[:], dt[:], dt_log[:], ALU.add))
                    step(v.scalar_tensor_tensor(da[:].rearrange("p (a h) -> p a h", a=2), dt[:].rearrange("p (a h) -> p a h", a=2),
                                                -1.0, mid(a_log[:], 2, L), ALU.mult, ALU.mult))
                    step(v.tensor_copy(da_wide[:], last(da[:], L)))
                    assert step.n == NV_DA, step.n
                    step(v.tensor_copy(pad_x[:, :, KC - 1:], b4(bank[6][:, 0:4 * L])))
                    step(v.tensor_copy(pad_bc[:, :, KC - 1:], bank[7][0:NS, 0:2 * L].rearrange("p (b l) -> p b l", b=2)))
                    for pad, cw, bias, conv, tap in ((pad_x, cw_x, cb_x, conv_x, tap_x), (pad_bc, cw_bc, cb_bc, conv_bc, tap_bc)):
                        step(v.tensor_tensor(conv[:], pad[:, :, 0:L], last(cw[:, :, 0], L), ALU.mult))
                        for k in range(1, KC):
                            step(v.tensor_tensor(tap[:], pad[:, :, k:k + L], last(cw[:, :, k], L), ALU.mult))
                            step(v.tensor_tensor(conv[:], conv[:], tap[:], ALU.add))
                        step(v.tensor_tensor(conv[:], conv[:], last(bias[:], L), ALU.add))
                    assert step.n == NV_CONV, step.n
                    dve.wait_ge(ha, 6)
                    for conv, tap, out in ((conv_x, tap_x, act_x), (conv_bc, tap_bc, act_bc)):
                        step(v.tensor_scalar(tap[:], tap[:], 1.0, None, ALU.add))
                        step(v.reciprocal(tap[:], tap[:]))
                        step(v.tensor_tensor(out[:], conv[:], tap[:], ALU.mult))
                    assert step.n == NV_ACT, step.n
                    dve.wait_ge(hp, 5)
                    step(v.tensor_copy(cum[:], bank[0][0:L, 0:2 * H]))
                    for a in range(2):
                        step(v.tensor_tensor(decay[:, a * H:(a + 1) * H, :], bank[1 + a][0:L, :].rearrange("p (h l) -> p h l", h=H),
                                             last(cum[:, a * H:(a + 1) * H], L), ALU.subtract))
                    step(v.tensor_scalar(decay[:], decay[:], 0.0, None, ALU.min))
                    assert step.n == NV_DECAY, step.n
                    dve.wait_ge(ha, 9)
                    dve.wait_ge(hp, 6)
                    step(v.tensor_copy(cb[:], bank[3][0:L, 0:L]))
                    for a, mask in ((0, upto), (1, onward)):
                        part = decay[:, a * H:(a + 1) * H, :]
                        step(v.tensor_tensor(part, part, mid(mask[:], H, L), ALU.mult))
                        step(v.tensor_tensor(part, part, mid(cb[:], H, L), ALU.mult))
                        step(v.tensor_tensor(part, part, last(dt[:, a * H:(a + 1) * H], L), ALU.mult))
                    step(v.memset(mix[:], 0.0))
                    step(v.tensor_copy(mix[:, :, 1:L], decay[:, 0:H, 0:L - 1]))
                    step(v.tensor_tensor(mix[:, :, 0:L - 1], mix[:, :, 0:L - 1], decay[:, H:2 * H, 1:L], ALU.add))
                    assert step.n == NV_MIX, step.n
                    step(v.tensor_tensor(gain[:], bank[7][0:L, 0:H], d_skip[:], ALU.add))
                    step(v.tensor_tensor(h3(sq[:]), h3(x_row[:]), last(gain[:], G), ALU.mult))
                    step(v.tensor_scalar(gate[:], gate[:], 1.0, None, ALU.add))
                    step(v.reciprocal(gate[:], gate[:]))
                    step(v.tensor_tensor(gate[:], gate[:], bank[4][0:L, :], ALU.mult))
                    dve.wait_ge(hp, 7)
                    step(v.tensor_tensor(y_sb[:], sq[:], bank[5][0:L, :], ALU.add))
                    step(v.tensor_tensor(y_sb[:], y_sb[:], gate[:], ALU.mult))
                    step(v.tensor_tensor(sq[:], y_sb[:], y_sb[:], ALU.mult))
                    step(v.tensor_reduce(ms[:, 0:1], sq[:], AX.X, ALU.add))
                    step(v.tensor_scalar(ms[:, 1:2], ms[:, 0:1], 1.0 / S, EPS, ALU.mult, ALU.add))
                    assert step.n == NV_MS, step.n
                    dve.wait_ge(ha, 10)
                    step(v.reciprocal(ms[:, 3:4], ms[:, 2:3]))
                    step(v.tensor_scalar(y_sb[:], y_sb[:], ms[:, 3:4], None, ALU.mult))
                    step(v.tensor_tensor(y_sb[:], y_sb[:], norm_w[:], ALU.mult))
                    step(v.memset(pairs[:], 0.0))
                    assert step.n == NV_Y, step.n
                    dve.wait_ge(hp, 9)
                    for a in range(2):
                        ins = v.tensor_copy(pairs[a * L:(a + 1) * L, :, a * L:(a + 1) * L],
                                            b4(bank[0][a * L:(a + 1) * L, 0:4 * L]))
                    step(ins)

        with ExitStack() as c6:
            wt = sb("wt", [P, 4, S], c=c6)
            ob = sb("ob", [P, 2, C], c=c6)
            out_b = sb("out_b", [1, C], c=c6)
            p_y = [ps(f"p_y{u}", [P, C], c6) for u in range(2)]
            ob_in = sem("ob_in")
            wt_in = [sem(f"wt_in{u}") for u in range(4)]
            y_done, y_added = sem("y_done"), sem("y_added")
            y_stored = [sem(f"y_stored{u}") for u in range(2)]
            with nc.Block() as block:
                @block.sync
                def _(sp):
                    sp.dma_start(out_b[:], t["out_b"]).then_inc(ob_in, 16)

                    def four(i):
                        for u in range(4):
                            tile = i * 4 + u
                            at = tile if isinstance(tile, int) else sp.snap(tile)
                            wait(sp, y_done, i * 4 + u - 3)
                            sp.dma_start(wt[:, u, :], weights_t[ds(at, 1), :, :].rearrange("a p s -> p (a s)")).then_inc(wt_in[u], 16)
                    loop(sp, NT // 4, four)

                @block.tensor
                def _(pe):
                    pe.wait_ge(ob_in, 16)

                    def four(i):
                        for u in range(4):
                            tile = i * 4 + u
                            pe.wait_ge(wt_in[u], (i + 1) * 16)
                            wait(pe, y_added, tile - 1)
                            for q in range(4):
                                pe.matmul(p_y[u % 2][:], wt[:, u, q * P:(q + 1) * P], z_out[:, q, :], start=q == 0, stop=False)
                            pe.matmul(p_y[u % 2][:], ones[0:1, :], out_b[:], start=False, stop=True).then_inc(y_done, 1)
                    loop(pe, NT // 4, four)

                @block.vector
                def _(dve):
                    def pair(i):
                        for u in range(2):
                            tile = i * 2 + u
                            wait(dve, y_stored[u], i * 16)
                            dve.wait_ge(y_done, tile + 1)
                            nc.vector.tensor_tensor(ob[:, u, :], flat(x_sb[:, ds(tile, 1), :]), p_y[u][:],
                                                    ALU.add).then_inc(y_added, 1)
                    loop(dve, NT // 2, pair)

                @block.scalar
                def _(act):
                    def pair(i):
                        for u in range(2):
                            tile = i * 2 + u
                            rows = tile * P
                            rows = rows if isinstance(rows, int) else act.snap(rows)
                            act.wait_ge(y_added, tile + 1)
                            act.dma_start(t["out"][ds(rows, P), :], ob[:, u, :]).then_inc(y_stored[u], 16)
                    loop(act, NT // 2, pair)
                    for u in range(2):
                        act.wait_ge(y_stored[u], 16 * (NT // 2))


def pick(inputs):
    g = {k: np.asarray(v) for k, v in inputs.items()}
    n = g["x"].shape[0]

    def rows(v, m=P):
        return np.broadcast_to(v.reshape(1, -1), (m, v.size))

    a_bd = np.zeros((H * D, 2 * H), g["x"].dtype)
    for h in range(H):
        a_bd[h * D:(h + 1) * D, h] = g["L0_gnn_a_dst"][h]
        a_bd[h * D:(h + 1) * D, H + h] = g["L0_gnn_a_src"][h]
    f = "L0_ffn_"
    b = chunk_bounds(n)
    t = {
        "x": g["x"], "adj": g["adj"],
        "ident": np.eye(P, dtype=np.float32), "ones": np.ones((P, P), np.float32),
        "cand_base": rows(np.repeat(np.asarray(b[:-1], np.float32) + 1, 8)),
        "upto": np.triu(np.ones((G, G), np.float32)), "onward": np.tril(np.ones((G, G), np.float32)),
        "W": g["L0_gnn_W"], "W_t": g["L0_gnn_W"].T, "Wr_t": g["L0_gnn_Wr"].T, "a_bd": a_bd,
        "br": rows(g["L0_gnn_br"]), "be": rows(g["L0_gnn_be"]), "We": rows(g["L0_gnn_We"]),
        "W_x": g[f + "W_x"], "W_slice_t": g[f + "W_slice"].T, "b_x_t": g[f + "b_x"].reshape(H, G).T,
        "b_slice": rows(g[f + "b_slice"]), "temp": rows(g[f + "temperature"]),
        "W_fx_t": g[f + "W_fx"].T, "b_fx": g[f + "b_fx"].reshape(1, S),
        "hy_in_t": g[f + "hy_in_w"].T, "hy_out_t": g[f + "hy_out_w"].T, "out_w_t": g[f + "out_w"].T,
        "fcD_t": g[f + "hy_fcD_w"].T, "conv_w": g[f + "hy_conv_w"], "conv_b_x": g[f + "hy_conv_b"][:S].reshape(4, P).T,
        "conv_b_bc": g[f + "hy_conv_b"][S:].reshape(2, NS).T,
        "dt_bias": rows(np.concatenate([g[f + "hy_dt_bias"]] * 2), G), "A_log": rows(g[f + "hy_A_log"], G),
        "hy_D": rows(g[f + "hy_D"], G), "norm_w": rows(g[f + "hy_norm_w"], G), "out_b": g[f + "out_b"].reshape(1, C),
    }
    return {k: np.ascontiguousarray(v) for k, v in t.items()}


def kernel(**inputs):
    import concourse.bacc as bacc
    from concourse.bass_utils import run_bass_kernel_spmd

    arrays = pick(inputs)
    nc = bacc.Bacc("TRN2", target_bir_lowering=False, num_devices=1)
    t = {k: nc.dram_tensor(f"in_{k}", v.shape, mybir.dt.from_np(v.dtype), kind="ExternalInput").ap() for k, v in arrays.items()}
    t["out"] = nc.dram_tensor("out", arrays["x"].shape, F32, kind="ExternalOutput").ap()
    build(nc, t)
    r = run_bass_kernel_spmd(nc, [{f"in_{k}": v for k, v in arrays.items()}], core_ids=[0])
    return r.results[0]["out"]
```

```python
from contextlib import ExitStack

import numpy as np

import concourse.bass as bass
from concourse import mybir

P = 128
H = 8
D = 32
C = 256
G = 64
S = H * G
NS = 64
KC = 3
ROW = C + H
NCH = 11
CAND = 8 * NCH
K = 24
GR = 4
GROUPS = K // GR
TQ = 8
SHARES = BY_VECTOR, BY_POOL, BY_SCALAR = (0,), (1,), (2, 3, 4, 5)
LAST_SHARES = LAST_BY_VECTOR, LAST_BY_POOL, LAST_BY_SCALAR = (0, 1, 2, 3), (4, 5), ()
EPS = 1e-5
BIG = 1e30

NV_ABS = 7
NV_DA = 16
NV_CONV = 30
NV_ACT = 36
NV_DECAY = 40
NV_MIX = 50
NV_MS = 60
NV_Y = 64
NA_YT = 11

ALU = mybir.AluOpType
ACT = mybir.ActivationFunctionType
F32 = mybir.dt.float32
U32 = mybir.dt.uint32
I32 = mybir.dt.int32
AX = mybir.AxisListType
ds = bass.ds


class Steps:

    def __init__(self, eng, sem, gate=None):
        self.eng, self.sem, self.n, self.base, self.gate = eng, sem, 0, 0, gate

    def __call__(self, ins):
        self.n += 1
        ins.then_inc(self.sem, 1)
        self.eng.wait_ge(self.sem, self.base + self.n)
        if self.gate is not None:
            self.eng.sem_inc(self.gate, 1)


class Chain:

    def __init__(self, eng, sem, gate):
        self.eng, self.sem, self.gate, self.base, self.n = eng, sem, gate, 0, 0

    def at(self, base, n):
        self.base, self.n = base, n
        return self

    def after_last(self):
        if not isinstance(self.base, int) or self.base + self.n > 0:
            self.eng.wait_ge(self.sem, self.base + self.n)
            self.eng.sem_inc(self.gate, 1)
        return self

    def step(self, ins):
        self.n += 1
        return ins.then_inc(self.sem, 1)


def wait(eng, sem, value):
    if isinstance(value, int) and value <= 0:
        return
    eng.wait_ge(sem, value)


def loop(eng, n, body):
    body(0)
    if n > 1:
        with eng.Fori(1, n) as i:
            body(i)


def by_piece(eng, n, body):
    body(0, False)
    if n > 2:
        with eng.Fori(1, n - 1) as q:
            body(q, False)
    body(n - 1, True)


def has(t, n):
    return not isinstance(t, int) or 0 <= t < n


def flat(ap):
    return ap.rearrange("p a c -> p (a c)")


def chunk_bounds(n):
    return [n * c // NCH for c in range(NCH + 1)]


def build(nc, t):
    N = t["x"].shape[0]
    NT = N // P
    XQ = NT // TQ
    node_table = nc.dram_tensor("node_table", [N, ROW], F32, kind="Internal").ap()
    residual_rows = nc.dram_tensor("residual_rows", [N, C], F32, kind="Internal").ap()
    weights_t = nc.dram_tensor("slice_weights_t", [NT, P, S], F32, kind="Internal").ap()
    bounds = chunk_bounds(N)

    with ExitStack() as ctx:
        def sb(name, shape, dt=F32, c=ctx):
            return c.enter_context(nc.sbuf_tensor(name, shape, dt))

        def sem(name):
            return ctx.enter_context(nc.semaphore(name))

        def ps(name, shape, c):
            return c.enter_context(nc.psum_tensor(name, [P, 512], F32))[:, 0:shape[1]]

        x_sb = sb("x_sb", [P, NT, C])
        src_score = sb("src_score", [P, NT, H])
        ident = sb("ident", [P, P])
        ones = sb("ones", [P, P])
        wct = sb("wct", [P, 2, S])
        bc = sb("bc", [P, S])
        stat6 = sb("stat6", [P, TQ, 6])
        moments = sb("moments", [P, TQ, 2])
        root_var = sb("root_var", [P, 2, TQ])
        mean = sb("mean", [P, NT])
        rstd = sb("rstd", [P, NT])

        class Norm:

            def __init__(self, name):
                self.gate, self.collected, self.aggregated = sem(f"{name}_gate"), sem(f"{name}_collected"), sem(f"{name}_aggregated")
                self.var_done, self.std_done = sem(f"{name}_var"), sem(f"{name}_std")
                self.inverted, self.rstd_done = sem(f"{name}_inverted"), sem(f"{name}_rstd")

            def collect(self, dve, q, j):
                if j == 0:
                    wait(dve, self.var_done, q)
                    dve.sem_inc(self.gate, 1)
                nc.vector.bn_stats(stat6[:, j, :], flat(x_sb[:, ds(q * TQ + j, 1), :])).then_inc(self.collected, 1)

            def aggregate(self, dve, q, j):
                dve.wait_ge(self.collected, q * TQ + j + 1)
                dve.sem_inc(self.gate, 1)
                nc.vector.bn_aggr(moments[:, j, :], stat6[:, j, :]).then_inc(self.aggregated, 1)

            def add_eps(self, dve, q):
                dve.wait_ge(self.aggregated, (q + 1) * TQ)
                wait(dve, self.rstd_done, q)
                dve.sem_inc(self.gate, 1)
                nc.vector.tensor_copy(mean[:, ds(q * TQ, TQ)], moments[:, :, 0])
                nc.vector.tensor_scalar(root_var[:, 0, :], moments[:, :, 1], EPS, None, ALU.add).then_inc(self.var_done, 1)

            def root(self, act, q):
                act.wait_ge(self.var_done, q + 1)
                nc.scalar.activation(root_var[:, 1, :], root_var[:, 0, :], ACT.Sqrt).then_inc(self.std_done, 1)

            def invert(self, dve, q):
                dve.wait_ge(self.std_done, q + 1)
                dve.sem_inc(self.gate, 1)
                nc.vector.reciprocal(root_var[:, 1, :], root_var[:, 1, :]).then_inc(self.inverted, 1)
                dve.wait_ge(self.inverted, q + 1)
                dve.sem_inc(self.gate, 1)
                nc.vector.tensor_copy(rstd[:, ds(q * TQ, TQ)], root_var[:, 1, :]).then_inc(self.rstd_done, 1)

            def turn(self, dve, q, j):
                if j < TQ // 2:
                    self.collect(dve, q, 2 * j)
                    self.collect(dve, q, 2 * j + 1)
                if 1 <= j <= TQ // 2:
                    self.aggregate(dve, q, 2 * j - 2)
                    self.aggregate(dve, q, 2 * j - 1)
                if j == TQ // 2:
                    self.add_eps(dve, q)
                if j == TQ // 2 + 1:
                    self.invert(dve, q)

            def first(self, dve):
                for j in range(TQ // 2 + 1):
                    self.turn(dve, 0, j)

            def normalise(self, dve, out, tile, q):
                dve.wait_ge(self.rstd_done, q + 1)
                return nc.vector.tensor_scalar(out, flat(x_sb[:, ds(tile, 1), :]), mean[:, ds(tile, 1)],
                                               rstd[:, ds(tile, 1)], ALU.subtract, ALU.mult)

        over = sb("over", [P, 2, NT])
        over_flag = sb("over_flag", [P, 1])
        over_int = sb("over_int", [P, 1], I32)
        scan = ctx.enter_context(ExitStack())
        adj = sb("adj", [P, 2, N], c=scan)
        base = sb("base", [P, CAND], c=scan)
        we = sb("we", [P, H], c=scan)
        adj_in = [sem(f"adj_in{u}") for u in range(2)]
        consts_in = sem("a_consts_in")

        with ExitStack() as c1:
            w_nat = sb("w_nat", [P, 2, C], c=c1)
            a_bd = sb("a_bd", [P, 2, 2 * H], c=c1)
            w_cat = sb("w_cat", [P, 2, ROW + H], c=c1)
            wr_t = sb("wr_t", [P, 2, C], c=c1)
            br = sb("br", [P, C], c=c1)
            be = sb("be", [P, H], c=c1)
            wx = sb("wx", [G, H, C], c=c1)
            ws_t = sb("ws_t", [G, G], c=c1)
            bx = sb("bx", [G, H], c=c1)
            bx_wide = sb("bx_wide", [G, H, P], c=c1)
            bs = sb("bs", [P, G], c=c1)
            temp = sb("temp", [P, H], c=c1)
            xn = sb("xn", [P, 4, C], c=c1)
            xn_t = sb("xn_t", [P, 4, C], c=c1)
            row_out = sb("row_out", [P, TQ, ROW], c=c1)
            p_t = [ps(f"p_t{u}", [P, C], c1) for u in range(2)]
            p_h = [ps(f"p_h{u}", [P, ROW + H], c1) for u in range(2)]
            p_r = [ps(f"p_r{u}", [P, C], c1) for u in range(2)]
            p_w = ps("p_w", [P, S], c1)
            p_v = ps("p_v", [P, S], c1)

            weights_in = sem("weights_in")
            x_in = sem("x_in")
            prep_pe, prep_dve = sem("prep_pe"), sem("prep_dve")
            xn_done, xt_done, xt_copied = sem("xn_done"), sem("xt_done"), sem("xt_copied")
            h_done, h_copied = sem("h_done"), sem("h_copied")
            r_done, r_added, br_added = sem("r_done"), sem("r_added"), sem("br_added")
            row_stored = [sem(f"row_stored{j}") for j in range(TQ)]
            residual_stored = sem("residual_stored")
            norm = Norm("first")
            loads = [
                (ident[:], t["ident"]), (ones[:], t["ones"]),
                (w_nat[:], t["W"].rearrange("(b p) i -> p b i", p=P)),
                (a_bd[:], t["a_bd"].rearrange("(b p) i -> p b i", p=P)),
                (w_cat[:, :, 0:C], t["W_t"].rearrange("(b p) i -> p b i", p=P)),
                (wr_t[:], t["Wr_t"].rearrange("(b p) i -> p b i", p=P)),
                (br[:], t["br"]), (be[:], t["be"]),
                (wx[:], t["W_x"].rearrange("(h p) i -> p h i", p=G)),
                (ws_t[:], t["W_slice_t"]), (bx[:], t["b_x_t"]), (bs[:], t["b_slice"]), (temp[:], t["temp"]),
            ]
            with nc.Block() as block:
                @block.sync
                def _(sp):
                    xr = t["x"].rearrange("(t p) c -> p t c", p=P)
                    rr = residual_rows.rearrange("(t p) c -> p t c", p=P)

                    def load_piece(q):
                        at = q * TQ if isinstance(q, int) else sp.snap(q * TQ)
                        wait(sp, x_in, q * 16)
                        sp.dma_start(x_sb[:, ds(at, TQ), :], xr[:, ds(at, TQ), :]).then_inc(x_in, 16)

                    def store_piece(q):
                        at = q * TQ if isinstance(q, int) else sp.snap(q * TQ)
                        sp.wait_ge(r_added, (q + 1) * TQ)
                        sp.dma_start(rr[:, ds(at, TQ), :], x_sb[:, ds(at, TQ), :]).then_inc(residual_stored, 16)

                    load_piece(0)
                    for dst, src in loads:
                        sp.dma_start(dst, src).then_inc(weights_in, 16)
                    load_piece(1)

                    def piece(q, more):
                        if more:
                            load_piece(q + 2)
                        for j in range(TQ):
                            rows = (q * TQ + j) * P
                            rows = rows if isinstance(rows, int) else sp.snap(rows)
                            sp.wait_ge(h_copied, q * TQ + j + 1)
                            sp.dma_start(node_table[ds(rows, P), :], row_out[:, j, :]).then_inc(row_stored[j], 16)
                        store_piece(q)
                    if XQ > 2:
                        piece(0, True)
                    if XQ > 3:
                        with sp.Fori(1, XQ - 2) as q:
                            piece(q, True)
                    sp.dma_start(base[:], t["cand_base"]).then_inc(consts_in, 16)
                    sp.dma_start(we[:], t["We"]).then_inc(consts_in, 16)
                    for u in range(2):
                        sp.dma_start(adj[:, u, :], t["adj"][u * P:(u + 1) * P, :]).then_inc(adj_in[u], 16)
                        piece(XQ - 2 + u, False)
                    for j in range(TQ):
                        sp.wait_ge(row_stored[j], 16 * XQ)
                    sp.wait_ge(residual_stored, 16 * XQ)

                @block.tensor
                def _(pe):
                    pe.wait_ge(weights_in, 16 * len(loads))
                    for c in range(2):
                        for b in range(2):
                            mm = pe.matmul(p_w[:, c * 2 * H:(c + 1) * 2 * H], w_nat[:, b, c * P:(c + 1) * P],
                                           a_bd[:, b, :], start=b == 0, stop=b == 1)
                    mm.then_inc(prep_pe, 1)
                    pe.wait_ge(prep_dve, 1)
                    for h in range(H):
                        mm = pe.matmul(p_v[:, h * G:(h + 1) * G], bx_wide[:, h, :], ws_t[:], start=True, stop=True)
                    mm.then_inc(prep_pe, 1)
                    for c in range(2):
                        pe.wait_ge(prep_dve, 3 + c)
                        for h in range(H):
                            mm = pe.matmul(p_w[:, h * G:(h + 1) * G], wx[:, h, c * P:(c + 1) * P], ws_t[:],
                                           start=True, stop=True)
                        mm.then_inc(prep_pe, 1)
                    def turn(tile, j):
                        pe.wait_ge(xn_done, tile + 1)
                        wait(pe, xt_copied, tile - 1)
                        for b in range(2):
                            mm = pe.transpose(p_t[j % 2][:, b * P:(b + 1) * P], xn[:, j % 4, b * P:(b + 1) * P], ident[:])
                        mm.then_inc(xt_done, 1)

                    def products(tile, j):
                        u = j % 2
                        pe.wait_ge(xt_copied, tile + 1)
                        wait(pe, h_copied, tile - 1)
                        wait(pe, r_added, tile - 1)
                        for b in range(2):
                            mm = pe.matmul(p_h[u][:], xn_t[:, j % 4, b * P:(b + 1) * P], w_cat[:, b, :],
                                           start=b == 0, stop=b == 1)
                        mm.then_inc(h_done, 1)
                        for b in range(2):
                            mm = pe.matmul(p_r[u][:], xn_t[:, j % 4, b * P:(b + 1) * P], wr_t[:, b, :],
                                           start=b == 0, stop=b == 1)
                        mm.then_inc(r_done, 1)

                    def piece(q, last):
                        for j in range(TQ):
                            if not last or j + 2 < TQ:
                                turn(q * TQ + j + 2, j + 2)
                            products(q * TQ + j, j)
                    turn(0, 0)
                    turn(1, 1)
                    by_piece(pe, XQ, piece)

                @block.scalar
                def _(act):
                    def copy_rows(tile, j):
                        wait(act, r_done, tile - 3)
                        act.wait_ge(xt_done, tile + 1)
                        nc.scalar.copy(xn_t[:, j % 4, :], p_t[j % 2][:]).then_inc(xt_copied, 1)

                    def copy_features(q, j):
                        tile, u = q * TQ + j, j % 2
                        wait(act, row_stored[j], q * 16)
                        act.wait_ge(h_done, tile + 1)
                        nc.scalar.copy(row_out[:, j, :], p_h[u][:, 0:ROW]).then_inc(h_copied, 1)

                    def piece(q, last):
                        for j in range(TQ):
                            if not last or j + 2 < TQ:
                                copy_rows(q * TQ + j + 2, j + 2)
                            copy_features(q, j)
                            if j == 3 and not last:
                                norm.root(act, q + 1)
                    norm.root(act, 0)
                    copy_rows(0, 0)
                    copy_rows(1, 1)
                    by_piece(act, XQ, piece)

                @block.vector
                def _(dve):
                    dve.wait_ge(x_in, 16)
                    norm.first(dve)
                    step = Steps(dve, prep_dve)
                    dve.wait_ge(weights_in, 16 * len(loads))
                    step(nc.vector.tensor_copy(bx_wide[:], bx[:].unsqueeze(2).broadcast_to([G, H, P])))
                    step(nc.vector.tensor_scalar(temp[:], temp[:], 1e-6, None, ALU.max))
                    dve.wait_ge(prep_pe, 1)
                    step(nc.vector.tensor_copy(w_cat[:, :, C:ROW + H], p_w[:, 0:4 * H].rearrange("p (c a) -> p c a", c=2)))
                    dve.wait_ge(prep_pe, 2)
                    rt = temp[:].unsqueeze(2).broadcast_to([P, H, G])
                    bc3 = bc[:].rearrange("p (h g) -> p h g", h=H)
                    recip = sem("recip")
                    nc.vector.reciprocal(temp[:], temp[:]).then_inc(recip, 1)
                    dve.wait_ge(recip, 1)
                    for c in range(2):
                        dve.wait_ge(prep_pe, 3 + c)
                        step(nc.vector.tensor_tensor(wct[:, c, :].rearrange("p (h g) -> p h g", h=H),
                                                     p_w[:].rearrange("p (h g) -> p h g", h=H), rt, ALU.mult))
                    step(nc.vector.tensor_tensor(bc3, p_v[:].rearrange("p (h g) -> p h g", h=H),
                                                 bs[:].unsqueeze(1).broadcast_to([P, H, G]), ALU.add))
                    step(nc.vector.tensor_tensor(bc3, bc3, rt, ALU.mult))
                    norm.invert(dve, 0)

                    def normalise(tile, j, q):
                        wait(dve, xt_done, tile - 3)
                        norm.normalise(dve, xn[:, j % 4, :], tile, q).then_inc(xn_done, 1)

                    def residual(tile, u):
                        dve.wait_ge(h_copied, tile + 1)
                        nc.vector.tensor_tensor(flat(src_score[:, ds(tile, 1), :]),
                                                p_h[u][:, ROW:ROW + H], be[:], ALU.add)
                        dve.wait_ge(r_done, tile + 1)
                        dve.wait_ge(br_added, tile + 1)
                        xt = flat(x_sb[:, ds(tile, 1), :])
                        nc.vector.tensor_tensor(xt, xt, p_r[u][:], ALU.add).then_inc(r_added, 1)

                    def piece(q, last):
                        for j in range(TQ):
                            if not last:
                                if j == 0:
                                    dve.wait_ge(x_in, (q + 2) * 16)
                                norm.turn(dve, q + 1, j)
                            if j + AHEAD < TQ:
                                normalise(q * TQ + j + AHEAD, j + AHEAD, q)
                            elif not last:
                                normalise(q * TQ + j + AHEAD, j + AHEAD, q + 1)
                            residual(q * TQ + j, j % 2)
                    AHEAD = 3
                    for j in range(AHEAD):
                        normalise(j, j, 0)
                    by_piece(dve, XQ, piece)

                @block.gpsimd
                def _(pool):
                    pool.wait_ge(weights_in, 16 * len(loads))
                    with pool.Fori(0, NT) as i:
                        pool.wait_ge(xn_done, i + 1)
                        xt = flat(x_sb[:, ds(i, 1), :])
                        nc.gpsimd.tensor_tensor(xt, xt, br[:], ALU.add).then_inc(br_added, 1)

        with ExitStack() as c2:
            near = sb("near", [P, 2, K, ROW], c=c2)
            vals = sb("vals", [P, 2, CAND], c=c2)
            where = sb("where", [P, 2, CAND], U32, c=c2)
            keys = sb("keys", [P, 4, CAND], c=c2)
            key = sb("key", [P, 2, 4 * 8], c=c2)
            edge = sb("edge", [P, 2, K], c=c2)
            column = sb("column", [P, 2, K], U32, c=c2)
            none = sb("none", [P, K], c=c2)
            picked = sb("picked", [P, K, CAND], c=c2)
            z = sb("z", [P, K, H], c=c2)
            edge_score = sb("edge_score", [P, K, H], c=c2)
            gone = sb("gone", [P, 2, K], c=c2)
            w = sb("w", [P, 2, K, H], c=c2)
            stat = sb("stat", [P, 3, H], c=c2)
            p_o = [ps(f"p_o{u}", [P, C], c2) for u in range(2)]

            adj_read = sem("adj_read")
            columns_done = sem("columns_done")
            near_in = [sem(f"near_in{u}") for u in range(2)]
            w_done, w_normed = sem("w_done"), sem("w_normed")
            near_scaled_v, near_scaled_p, near_scaled_a = sem("near_scaled_v"), sem("near_scaled_p"), sem("near_scaled_a")
            summed, added = sem("summed"), sem("added")
            maxed, listed, picked_all, soft = sem("maxed"), sem("listed"), sem("picked_all"), sem("soft")
            cleared, edge_scored = sem("near_cleared"), sem("edge_scored")
            gate, pool_gate = sem("gate"), sem("pool_gate")
            flag_max, flag_all, flag_done = sem("flag_max"), sem("flag_all"), sem("flag_done")

            SOFT = 6

            def scale_rows(eng, u, g):
                ks = slice(g * GR, (g + 1) * GR)
                rows = near[:, u, ks, 0:C].rearrange("p k (h d) -> p k h d", h=H)
                return eng.tensor_tensor(rows, rows, w[:, u, ks, :].unsqueeze(3).broadcast_to([P, GR, H, D]), ALU.mult)

            with nc.Block() as block:
                @block.sync
                def _(sp):
                    with sp.Fori(1, NT // 2) as i:
                        for u in range(2):
                            rows = sp.snap((i * 2 + u) * P)
                            sp.wait_ge(adj_read, i * 2 + u - 1)
                            sp.dma_start(adj[:, u, :], t["adj"][ds(rows, P), :]).then_inc(adj_in[u], 16)

                @block.vector
                def _(dve):
                    listing, softening = Chain(dve, listed, gate), Chain(dve, soft, gate)
                    dve.wait_ge(consts_in, 32)
                    v = nc.vector
                    LIST = 10

                    def largest(tile, u, i, c):
                        if c == 0:
                            dve.wait_ge(adj_in[u], (i + 1) * 16)
                            wait(dve, picked_all, tile - 1)
                            dve.sem_inc(gate, 1)
                        ins = v.max(vals[:, u, 8 * c:8 * c + 8], adj[:, u, bounds[c]:bounds[c + 1]])
                        if c == NCH - 1:
                            ins.then_inc(maxed, 1)

                    def locate(tile, u, c):
                        if c == 0:
                            dve.wait_ge(maxed, tile + 1)
                            dve.sem_inc(gate, 1)
                        at = slice(8 * c, 8 * c + 8)
                        ins = v.max_index(where[:, u, at], vals[:, u, at], adj[:, u, bounds[c]:bounds[c + 1]])
                        if c == NCH - 1:
                            ins.then_inc(adj_read, 1)

                    def compact(tile, u, n):
                        chain = listing.at(tile * LIST, n)
                        if n == 0:
                            dve.wait_ge(adj_read, tile + 1)
                            chain.step(v.tensor_tensor(keys[:, 3, :], where[:, u, :], base[:], ALU.add))
                        elif n == 1:
                            chain.after_last().step(v.scalar_tensor_tensor(keys[:, 0, :], vals[:, u, :], 0.0, keys[:, 3, :],
                                                                           ALU.is_gt, ALU.mult))
                        elif n < 8:
                            r = (n - 2) // 2
                            at = slice(8 * r, 8 * r + 8)
                            chain.after_last()
                            if n % 2 == 0:
                                chain.step(v.max(key[:, u, at], keys[:, r, :]))
                            else:
                                chain.step(v.match_replace(keys[:, r + 1, :], key[:, u, at], keys[:, r, :], 0.0))
                        elif n == 8:
                            chain.after_last().step(v.max(key[:, u, K:K + 8], keys[:, 3, :]))
                            chain.step(v.tensor_scalar(none[:], key[:, u, 0:K], 0.0, 4.0 * N, ALU.is_equal, ALU.mult))
                        elif n == 9:
                            chain.at(tile * LIST, LIST).after_last()
                            v.scalar_tensor_tensor(column[:, u, :], none[:], -1.0, key[:, u, 0:K],
                                                   ALU.add, ALU.add).then_inc(columns_done, 1)
                        elif n == 10:
                            v.tensor_reduce(over[:, 0, ds(tile, 1)], vals[:, u, :].rearrange("p (c e) -> p c e", e=8)[:, :, 7],
                                            AX.X, ALU.max)
                            v.tensor_copy(over[:, 1, ds(tile, 1)], key[:, u, K:K + 1])
                            v.tensor_scalar(gone[:, u, :], key[:, u, 0:K], 0.0, -BIG, ALU.is_equal, ALU.mult)

                    def pick(tile, u, k):
                        ins = v.scalar_tensor_tensor(picked[:, k, :], keys[:, 0, :], key[:, u, k:k + 1], vals[:, u, :],
                                                     ALU.is_equal, ALU.mult, accum_out=edge[:, u, k:k + 1])
                        if k == K - 1:
                            ins.then_inc(picked_all, 1)

                    def soften(tile, u, i, n):
                        chain = softening.at(tile * SOFT, n)
                        if n == 0:
                            dve.wait_ge(near_in[u], (i + 1) * 16 * K)
                            dve.wait_ge(edge_scored, (tile + 1) * 3)
                            chain.step(v.tensor_tensor(z[:], near[:, u, :, C:ROW], edge_score[:], ALU.add))
                        elif n == 1:
                            chain.after_last().step(v.scalar_tensor_tensor(z[:], z[:], 0.2, z[:], ALU.mult, ALU.max))
                        elif n == 2:
                            chain.after_last().step(v.tensor_reduce(stat[:, 0, :], z[:].rearrange("p k h -> p h k"), AX.X, ALU.max))
                        elif n == 3:
                            chain.after_last()
                            chain.step(v.tensor_tensor(z[:], z[:], stat[:, 0, :].unsqueeze(1).broadcast_to([P, K, H]),
                                                       ALU.subtract))
                        elif n == 4:
                            dve.wait_ge(w_done, tile + 1)
                            chain.step(v.tensor_reduce(stat[:, 1, :], w[:, u, :, :].rearrange("p k h -> p h k"), AX.X, ALU.add))
                        elif n == 5:
                            chain.after_last().step(v.reciprocal(stat[:, 2, :], stat[:, 1, :]))
                        elif n == 6:
                            chain.after_last()
                            v.tensor_tensor(w[:, u, :, :], w[:, u, :, :], stat[:, 2, :].unsqueeze(1).broadcast_to([P, K, H]),
                                            ALU.mult).then_inc(w_normed, 1)
                        elif n == 7:
                            dve.wait_ge(w_normed, tile + 1)
                            for g in LAST_BY_VECTOR if isinstance(tile, int) and tile == NT - 1 else BY_VECTOR:
                                scale_rows(v, u, g).then_inc(near_scaled_v, 1)

                    def add(tile, u):
                        dve.wait_ge(summed, (tile + 1) * GROUPS)
                        xt = flat(x_sb[:, ds(tile, 1), :])
                        v.tensor_tensor(xt, xt, p_o[u][:], ALU.add).then_inc(added, 1)

                    SOFTEN_FROM = NCH - 8
                    ADD_AT = 5

                    def turn(t, u, i):
                        for c in range(NCH):
                            if has(t, NT):
                                largest(t, u, i, c)
                            if has(t - 1, NT):
                                compact(t - 1, 1 - u, c)
                            if has(t - 4, NT) and c == ADD_AT:
                                add(t - 4, u)
                        for c in range(NCH):
                            if has(t, NT):
                                locate(t, u, c)
                            if has(t - 1, NT):
                                if c == 0:
                                    dve.wait_ge(columns_done, t)
                                    wait(dve, edge_scored, (t - 2) * 3)
                                for k in range(c * K // NCH, (c + 1) * K // NCH):
                                    pick(t - 1, 1 - u, k)
                            if has(t - 2, NT) and c >= SOFTEN_FROM:
                                soften(t - 2, u, i - 1, c - SOFTEN_FROM)

                    for t in range(4):
                        turn(t, t % 2, t // 2)
                    with dve.Fori(2, NT // 2) as i:
                        for u in range(2):
                            turn(i * 2 + u, u, i)
                    for t in range(NT, NT + 4):
                        turn(t, t % 2, t // 2)
                    nc.vector.tensor_reduce(over_flag[:], over[:].rearrange("p a t -> p (a t)"), AX.X, ALU.max).then_inc(flag_max, 1)
                    dve.wait_ge(flag_all, 1)
                    nc.vector.tensor_scalar(over_int[:], over_flag[:], 0.0, None, ALU.is_gt).then_inc(flag_done, 1)
                    dve.wait_ge(flag_done, 1)

                @block.scalar
                def _(act):
                    def exponentials(tile, u):
                        act.wait_ge(soft, tile * SOFT + 4)
                        wait(act, near_scaled_p, (tile - 1) * len(BY_POOL))
                        nc.scalar.activation(w[:, u, :, :], z[:], ACT.Exp).then_inc(w_done, 1)

                    def scale(u, g):
                        for k in range(g * GR, (g + 1) * GR):
                            for h in range(H):
                                part = near[:, u, k, h * D:(h + 1) * D]
                                ins = nc.scalar.mul(part, part, w[:, u, k, h:h + 1])
                        ins.then_inc(near_scaled_a, 1)

                    def turn(tile, u):
                        act.wait_ge(w_normed, tile + 1)
                        for g in BY_SCALAR[:-1]:
                            scale(u, g)
                        exponentials(tile + 1, 1 - u)
                        scale(u, BY_SCALAR[-1])

                    def pair(i):
                        for u in range(2):
                            turn(i * 2 + u, u)
                    exponentials(0, 0)
                    loop(act, NT // 2 - 1, pair)
                    turn(NT - 2, 0)
                    act.wait_ge(w_normed, NT)
                    for g in LAST_BY_SCALAR:
                        scale(1, g)

                @block.gpsimd
                def _(pool):
                    nc.gpsimd.memset(near[:], 0.0).then_inc(cleared, 1)
                    pool.wait_ge(cleared, 1)

                    def gather(tile, u):
                        pool.wait_ge(columns_done, tile + 1)
                        pool.sem_inc(pool_gate, 1)
                        for g in range(GROUPS):
                            if not isinstance(tile, int) or tile >= 2:
                                pool.wait_ge(summed, (tile - 2) * GROUPS + g + 1)
                                pool.sem_inc(pool_gate, 1)
                            for k in range(g * GR, (g + 1) * GR):
                                pool.indirect_dma_start(
                                    out=near[:, u, k, :], out_offset=None, in_=node_table,
                                    in_offset=bass.IndirectOffsetOnAxis(ap=column[:, u, k:k + 1], axis=0),
                                    bounds_check=N - 1, oob_is_err=False).then_inc(near_in[u], 16)

                    def scale(tile, u, groups=BY_POOL):
                        pool.wait_ge(w_normed, tile + 1)
                        for g in groups:
                            scale_rows(nc.gpsimd, u, g).then_inc(near_scaled_p, 1)

                    def score_edges(tile, u):
                        step = Steps(pool, edge_scored)
                        step.base = tile * 3
                        pool.wait_ge(picked_all, tile + 1)
                        if not isinstance(tile, int) or tile > 0:
                            pool.wait_ge(soft, tile * SOFT - (SOFT - 1))
                        by_edge = edge[:, u, :].unsqueeze(2).broadcast_to([P, K, H])
                        by_gone = gone[:, u, :].unsqueeze(2).broadcast_to([P, K, H])
                        step(nc.gpsimd.tensor_tensor(edge_score[:], by_edge, we[:].unsqueeze(1).broadcast_to([P, K, H]), ALU.mult))
                        step(nc.gpsimd.tensor_tensor(edge_score[:], edge_score[:], by_gone, ALU.add))
                        step(nc.gpsimd.tensor_tensor(edge_score[:], edge_score[:],
                                                     src_score[:, ds(tile, 1), :].broadcast_to([P, K, H]), ALU.add))

                    def pair(i):
                        gather(i * 2 + 1, 1)
                        scale(i * 2, 0)
                        score_edges(i * 2 + 1, 1)
                        gather(i * 2 + 2, 0)
                        scale(i * 2 + 1, 1)
                        score_edges(i * 2 + 2, 0)
                    gather(0, 0)
                    score_edges(0, 0)
                    loop(pool, NT // 2 - 1, pair)
                    gather(NT - 1, 1)
                    scale(NT - 2, 0)
                    score_edges(NT - 1, 1)
                    scale(NT - 1, 1, LAST_BY_POOL)
                    pool.wait_ge(flag_max, 1)
                    nc.gpsimd.partition_all_reduce(over_flag[:], over_flag[:], P, bass.bass_isa.ReduceOp.max).then_inc(flag_all, 1)

                @block.tensor
                def _(pe):
                    def turn(tile, u, shares):
                        wait(pe, added, tile - 1)
                        for groups, usual, scaled in zip(shares, SHARES, (near_scaled_v, near_scaled_p, near_scaled_a)):
                            for n, g in enumerate(groups):
                                pe.wait_ge(scaled, tile * len(usual) + n + 1)
                                for k in range(g * GR, (g + 1) * GR):
                                    mm = pe.matmul(p_o[u][:], ident[:], near[:, u, k, 0:C], start=k == 0, stop=k == K - 1)
                                mm.then_inc(summed, 1)

                    def pair(i):
                        for u in range(2):
                            turn(i * 2 + u, u, SHARES)
                    loop(pe, NT // 2 - 1, pair)
                    turn(NT - 2, 0, SHARES)
                    turn(NT - 1, 1, LAST_SHARES)

        scan.close()
        JB = 4 * P
        NJ = N // JB
        flag = nc.values_load(over_int[0:1, 0:1], min_val=0, max_val=1)
        with nc.If(flag > 0), ExitStack() as c3:
            a = sb("d_adj", [P, JB], c=c3)
            absent = sb("absent", [P, JB], c=c3)
            nodes = sb("nodes", [P, 4, ROW], c=c3)
            we = sb("d_we", [P, H], c=c3)
            dst_wide = sb("dst_wide", [P, 4, H, P], c=c3)
            z = sb("d_z", [P, H, JB], c=c3)
            w = sb("d_w", [P, H, JB], c=c3)
            w_t = sb("d_w_t", [P, H, 4, P], c=c3)
            stat = sb("d_stat", [P, 8, H], c=c3)
            MAX, BLOCK_MAX, NEW_MAX, DROP, KEEP, SUM, BLOCK_SUM, INV = range(8)
            acc = sb("acc", [P, C], c=c3)
            p_d = [ps(f"p_d{u}", [P, JB], c3) for u in range(2)]
            p_x = [ps(f"p_x{u}", [P, JB], c3) for u in range(2)]
            p_a = ps("p_a", [P, C], c3)
            d_in, base_in, d_gate, d_gate_v = sem("d_in"), sem("base_in"), sem("d_gate"), sem("d_gate_v")
            dv, dp, da_ = sem("dense_dve"), sem("dense_pe"), sem("dense_act")
            BEGIN, BLOCK, END = 3, 24, 3
            TILE = BEGIN + NJ * BLOCK + END

            with nc.Block() as block:
                @block.sync
                def _(sp):
                    sp.dma_start(we[:], t["We"]).then_inc(base_in, 16)
                    rr = residual_rows.rearrange("(t p) c -> p t c", p=P)
                    sp.dma_start(x_sb[:], rr).then_inc(base_in, 16)
                    with sp.Fori(0, NT) as i:
                        with sp.Fori(0, NJ) as j:
                            row, col = sp.snap(i * P), sp.snap(j * JB)
                            sp.wait_ge(dv, i * TILE + BEGIN + j * BLOCK)
                            sp.sem_inc(d_gate, 1)
                            sp.dma_start(a[:], t["adj"][ds(row, P), ds(col, JB)]).then_inc(d_in, 16)
                            sp.dma_start(nodes[:], node_table[ds(col, JB), :].rearrange("(b p) c -> p b c", p=P)).then_inc(d_in, 16)

                @block.vector
                def _(dve):
                    v = nc.vector
                    step = Steps(dve, dv, d_gate_v)
                    dve.wait_ge(base_in, 32)

                    def last(ap, n):
                        return ap.unsqueeze(2).broadcast_to([P, ap.shape[1], n])
                    with dve.Fori(0, NT) as i:
                        step.base, step.n = i * TILE, 0
                        step(v.memset(stat[:, MAX, :], -BIG))
                        step(v.memset(stat[:, SUM, :], 0.0))
                        step(v.memset(acc[:], 0.0))
                        assert step.n == BEGIN
                        with dve.Fori(0, NJ) as j:
                            step.base, step.n = i * TILE + j * BLOCK + BEGIN, 0
                            block_at = i * NJ + j
                            dve.wait_ge(d_in, (block_at + 1) * 32)
                            for b in range(4):
                                ins = v.tensor_copy(dst_wide[:, b, :, :], last(nodes[:, b, C:ROW], P))
                            step(ins)
                            step(v.tensor_scalar(absent[:], a[:], 0.0, -1.0, ALU.is_gt, ALU.add))
                            for h in range(H):
                                dve.wait_ge(dp, block_at * 17 + h + 1)
                                step(v.scalar_tensor_tensor(z[:, h, :], a[:], we[:, h:h + 1], p_d[h % 2][:], ALU.mult, ALU.add))
                            step(v.tensor_tensor(z[:], z[:], last(flat(src_score[:, ds(i, 1), :]), JB), ALU.add))
                            step(v.scalar_tensor_tensor(z[:], z[:], 0.2, z[:], ALU.mult, ALU.max))
                            step(v.scalar_tensor_tensor(z[:], absent[:].unsqueeze(1).broadcast_to([P, H, JB]), BIG, z[:],
                                                        ALU.mult, ALU.add))
                            step(v.tensor_reduce(stat[:, BLOCK_MAX, :], z[:], AX.X, ALU.max))
                            step(v.tensor_tensor(stat[:, NEW_MAX, :], stat[:, MAX, :], stat[:, BLOCK_MAX, :], ALU.max))
                            step(v.tensor_tensor(stat[:, DROP, :], stat[:, MAX, :], stat[:, NEW_MAX, :], ALU.subtract))
                            step(v.tensor_copy(stat[:, MAX, :], stat[:, NEW_MAX, :]))
                            step(v.tensor_tensor(z[:], z[:], last(stat[:, NEW_MAX, :], JB), ALU.subtract))
                            assert step.n == 18
                            dve.wait_ge(da_, block_at * 10 + 2)
                            step(v.tensor_reduce(stat[:, BLOCK_SUM, :], w[:], AX.X, ALU.add))
                            step(v.tensor_tensor(stat[:, SUM, :], stat[:, SUM, :], stat[:, KEEP, :], ALU.mult))
                            step(v.tensor_tensor(stat[:, SUM, :], stat[:, SUM, :], stat[:, BLOCK_SUM, :], ALU.add))
                            acc3 = acc[:].rearrange("p (h d) -> p h d", h=H)
                            step(v.tensor_tensor(acc3, acc3, last(stat[:, KEEP, :], D), ALU.mult))
                            dve.wait_ge(dp, block_at * 17 + 17)
                            step(v.tensor_tensor(acc[:], acc[:], p_a[:], ALU.add))
                            step(v.tensor_copy(stat[:, DROP, :], stat[:, KEEP, :]))
                            assert step.n == BLOCK
                        step.base, step.n = i * TILE + BEGIN + NJ * BLOCK, 0
                        step(v.reciprocal(stat[:, INV, :], stat[:, SUM, :]))
                        acc3 = acc[:].rearrange("p (h d) -> p h d", h=H)
                        step(v.tensor_tensor(acc3, acc3, last(stat[:, INV, :], D), ALU.mult))
                        xt = flat(x_sb[:, ds(i, 1), :])
                        step(v.tensor_tensor(xt, xt, acc[:], ALU.add))

                @block.scalar
                def _(act):
                    with act.Fori(0, NT) as i:
                        with act.Fori(0, NJ) as j:
                            block_at = i * NJ + j
                            act.wait_ge(dv, i * TILE + BEGIN + j * BLOCK + 18)
                            nc.scalar.activation(w[:], z[:], ACT.Exp).then_inc(da_, 1)
                            nc.scalar.activation(stat[:, KEEP, :], stat[:, DROP, :], ACT.Exp).then_inc(da_, 1)
                            for h in range(H):
                                act.wait_ge(dp, block_at * 17 + 8 + h + 1)
                                nc.scalar.copy(w_t[:, h, :, :].rearrange("p b i -> p (b i)"), p_x[h % 2][:]).then_inc(da_, 1)

                @block.tensor
                def _(pe):
                    with pe.Fori(0, NT) as i:
                        with pe.Fori(0, NJ) as j:
                            block_at = i * NJ + j
                            dve_at = i * TILE + BEGIN + j * BLOCK
                            for h in range(H):
                                pe.wait_ge(dv, dve_at + (1 if h < 2 else h + 1))
                                for b in range(4):
                                    mm = pe.matmul(p_d[h % 2][:, b * P:(b + 1) * P], dst_wide[:, b, h, :], ident[:],
                                                   start=True, stop=True)
                                mm.then_inc(dp, 1)
                            for h in range(H):
                                pe.wait_ge(da_, block_at * 10 + (2 if h < 2 else h + 1))
                                for b in range(4):
                                    mm = pe.transpose(p_x[h % 2][:, b * P:(b + 1) * P], w[:, h, b * P:(b + 1) * P], ident[:])
                                mm.then_inc(dp, 1)
                            pe.wait_ge(da_, block_at * 10 + 10)
                            for h in range(H):
                                for b in range(4):
                                    mm = pe.matmul(p_a[:, h * D:(h + 1) * D], w_t[:, h, b, :], nodes[:, b, h * D:(h + 1) * D],
                                                   start=b == 0, stop=b == 3)
                            mm.then_inc(dp, 1)

                @block.gpsimd
                def _(pool):
                    pool.wait_ge(base_in, 32)
        L = G
        IN = 2 * S + 2 * NS + 2 * H
        X0, B0, C0, DT0 = S, 2 * S, 2 * S + NS, 2 * S + 2 * NS
        wfx_t, b_fx = sb("wfx_t", [P, 2, S]), sb("b_fx", [1, S])
        in_wt, how_t, ow_t = sb("in_wt", [P, 4, IN]), sb("how_t", [P, 4, S]), sb("ow_t", [P, 4, C])
        fcd_t = sb("fcd_t", [P, 4, H])
        cw_x, cb_x = sb("cw_x", [P, 4, KC]), sb("cb_x", [P, 4])
        cw_bc, cb_bc = sb("cw_bc", [NS, 2, KC]), sb("cb_bc", [NS, 2])
        dt_bias, a_log, d_skip = sb("dt_bias", [L, 2 * H]), sb("a_log", [L, H]), sb("d_skip", [L, H])
        norm_w = sb("norm_w", [L, S])
        upto, onward = sb("upto", [L, L]), sb("onward", [L, L])
        out_b = sb("out_b", [P, C])
        wt = sb("wt", [P, 4, S])
        h_in = sem("h_in")
        wt_in = [sem(f"wt_in{u}") for u in range(4)]
        loads5 = [
            (wfx_t[:], t["W_fx_t"].rearrange("(b p) i -> p b i", p=P)), (b_fx[:], t["b_fx"]),
            (in_wt[:], t["hy_in_t"].rearrange("(b p) i -> p b i", p=P)),
            (how_t[:], t["hy_out_t"].rearrange("(b p) i -> p b i", p=P)),
            (ow_t[:], t["out_w_t"].rearrange("(b p) i -> p b i", p=P)),
            (fcd_t[:], t["fcD_t"].rearrange("(b p) i -> p b i", p=P)),
            (cw_x[:], t["conv_w"][0:S, :].rearrange("(b p) i -> p b i", p=P)),
            (cb_x[:], t["conv_b_x"]),
            (cw_bc[:], t["conv_w"][S:S + 2 * NS, :].rearrange("(b p) i -> p b i", p=NS)),
            (cb_bc[:], t["conv_b_bc"]),
            (dt_bias[:], t["dt_bias"]), (a_log[:], t["A_log"]), (d_skip[:], t["hy_D"]), (norm_w[:], t["norm_w"]),
            (upto[:], t["upto"]), (onward[:], t["onward"]),
            (out_b[:], t["out_b"]),
        ]

        slice_sum = sb("slice_sum", [P, S])
        t1 = sb("t1", [P, 2, S])
        with ExitStack() as c4:
            xn = sb("b_xn", [P, 8, C], c=c4)
            xn_t = sb("b_xn_t", [P, 4, C], c=c4)
            logit = sb("logit", [P, 2, S], c=c4)
            ex = sb("ex", [P, 2, S], c=c4)
            sw = sb("sw", [P, 2, S], c=c4)
            sw_t = sb("sw_t", [P, 2, S], c=c4)
            top = sb("top", [P, 2, 4, H], c=c4)
            MAX, NEG_MAX, SUM, INV_SUM = range(4)
            p_t = [ps(f"b_p_t{u}", [P, C], c4) for u in range(2)]
            p_l = [ps(f"p_l{u}", [P, S], c4) for u in range(2)]
            p_s = [ps(f"p_s{u}", [P, S], c4) for u in range(2)]
            p_1 = [ps(f"p_1{b}", [P, S], c4) for b in range(2)]
            norm = Norm("second")
            xn_done, xt_done, xt_copied = sem("b_xn_done"), sem("b_xt_done"), sem("b_xt_copied")
            logit_done, shifted, ex_done = sem("logit_done"), sem("shifted"), sem("ex_done")
            sw_done, t1_done, swt_done, swt_copied = sem("sw_done"), sem("t1_done"), sem("swt_done"), sem("swt_copied")
            swt_stored = [sem(f"swt_stored{u}") for u in range(2)]
            shift_steps, weight_steps = sem("shift_steps"), sem("weight_steps")
            sum_done, t1_copied = sem("sum_done"), sem("t1_copied")
            gate, exp_gate = sem("weights_gate"), sem("exp_gate")

            def by_head(ap):
                return ap.rearrange("p (h g) -> p h g", h=H)

            with nc.Block() as block:
                @block.vector
                def _(dve):
                    norm.first(dve)
                    shift_step, weight_step = Steps(dve, shift_steps), Steps(dve, weight_steps)

                    def normalise(tile, j, q):
                        wait(dve, t1_done, tile - 7)
                        norm.normalise(dve, xn[:, j, :], tile, q).then_inc(xn_done, 1)

                    def shift(tile, u):
                        step = shift_step
                        step.base, step.n = tile * 2, 0
                        dve.wait_ge(logit_done, tile + 1)
                        wait(dve, ex_done, tile - 1)
                        step(nc.vector.tensor_tensor(logit[:, u, :], p_l[u][:], bc[:], ALU.add))
                        step(nc.vector.tensor_reduce(top[:, u, MAX, :], by_head(logit[:, u, :]), AX.X, ALU.max))
                        nc.vector.tensor_scalar(top[:, u, NEG_MAX, :], top[:, u, MAX, :], -1.0, None, ALU.mult).then_inc(shifted, 1)

                    def weights(tile, u):
                        step = weight_step
                        step.base, step.n = tile, 0
                        dve.wait_ge(ex_done, tile + 1)
                        dve.sem_inc(gate, 1)
                        step(nc.vector.reciprocal(top[:, u, INV_SUM, :], top[:, u, SUM, :]))
                        wait(dve, t1_done, tile - 1)
                        wait(dve, sum_done, tile - 1)
                        nc.vector.tensor_tensor(by_head(sw[:, u, :]), by_head(ex[:, u, :]),
                                                top[:, u, INV_SUM, :].unsqueeze(2).broadcast_to([P, H, G]),
                                                ALU.mult).then_inc(sw_done, 1)

                    norm.invert(dve, 0)
                    for j in range(3):
                        normalise(j, j, 0)

                    def piece(q, last):
                        for j in range(TQ):
                            t = q * TQ + j
                            shift(t, j % 2)
                            if has(t - 1, NT):
                                weights(t - 1, (j - 1) % 2)
                            if not last:
                                norm.turn(dve, q + 1, j)
                            if has(t + 3, NT):
                                normalise(t + 3, (j + 3) % 8, q if j + 3 < TQ else q + 1)
                    by_piece(dve, XQ, piece)
                    weights(NT - 1, 1)
                    dve.wait_ge(t1_done, NT)
                    nc.vector.tensor_copy(t1[:, 0, :], p_1[0][:]).then_inc(t1_copied, 1)

                @block.scalar
                def _(act):
                    norm.root(act, 0)

                    def copy_rows(tile, j):
                        act.wait_ge(xt_done, tile + 1)
                        wait(act, logit_done, tile - 3)
                        nc.scalar.copy(xn_t[:, j % 4, :], p_t[j % 2][:]).then_inc(xt_copied, 1)

                    def exponentials(tile, u):
                        wait(act, sw_done, tile - 1)
                        act.wait_ge(shifted, tile + 1)
                        act.sem_inc(exp_gate, 1)
                        for h in range(H):
                            at = slice(h * G, (h + 1) * G)
                            ins = nc.scalar.activation(ex[:, u, at], logit[:, u, at], ACT.Exp, bias=top[:, u, NEG_MAX, h:h + 1],
                                                       accum_out=top[:, u, SUM, h:h + 1])
                        ins.then_inc(ex_done, 1)

                    def copy_weights(tile, u):
                        wait(act, swt_stored[u], (tile - u) * 8)
                        act.wait_ge(swt_done, tile + 1)
                        nc.scalar.copy(sw_t[:, u, :], p_s[u][:]).then_inc(swt_copied, 1)

                    for j in range(3):
                        copy_rows(j, j)

                    def piece(q, last):
                        for j in range(TQ):
                            t = q * TQ + j
                            exponentials(t, j % 2)
                            if has(t - 1, NT):
                                copy_weights(t - 1, (j - 1) % 2)
                            if has(t + 3, NT):
                                copy_rows(t + 3, j + 3)
                            if j == TQ // 2 and not last:
                                norm.root(act, q + 1)
                    by_piece(act, XQ, piece)
                    copy_weights(NT - 1, 1)
                    act.wait_ge(t1_done, NT)
                    nc.scalar.copy(t1[:, 1, :], p_1[1][:]).then_inc(t1_copied, 1)

                @block.tensor
                def _(pe):
                    def turn(tile, j):
                        pe.wait_ge(xn_done, tile + 1)
                        wait(pe, xt_copied, tile - 1)
                        for b in range(2):
                            mm = pe.transpose(p_t[j % 2][:, b * P:(b + 1) * P], xn[:, j % 8, b * P:(b + 1) * P], ident[:])
                        mm.then_inc(xt_done, 1)

                    def logits(tile, j):
                        pe.wait_ge(xt_copied, tile + 1)
                        wait(pe, shifted, tile - 1)
                        for b in range(2):
                            mm = pe.matmul(p_l[j % 2][:], xn_t[:, j % 4, b * P:(b + 1) * P], wct[:, b, :],
                                           start=b == 0, stop=b == 1)
                        mm.then_inc(logit_done, 1)

                    def sums(tile, j):
                        u = j % 2
                        first, last = isinstance(tile, int) and tile == 0, isinstance(tile, int) and tile == NT - 1
                        pe.wait_ge(sw_done, tile + 1)
                        wait(pe, swt_copied, tile - 1)
                        for q in range(4):
                            mm = pe.transpose(p_s[u][:, q * P:(q + 1) * P], sw[:, u, q * P:(q + 1) * P], ident[:])
                        mm.then_inc(swt_done, 1)
                        for b in range(2):
                            mm = pe.matmul(p_1[b][:], xn[:, j % 8, b * P:(b + 1) * P], sw[:, u, :], start=first, stop=last)
                        mm.then_inc(t1_done, 1)

                    for j in range(3):
                        turn(j, j)
                    for j in range(2):
                        logits(j, j)

                    def piece(q, last):
                        for j in range(TQ):
                            t = q * TQ + j
                            if has(t - 1, NT):
                                sums(t - 1, j + 7)
                            if has(t + 2, NT):
                                logits(t + 2, j + 2)
                            if has(t + 3, NT):
                                turn(t + 3, j + 3)
                    by_piece(pe, XQ, piece)
                    sums(NT - 1, 7)

                @block.gpsimd
                def _(pool):
                    pool.wait_ge(sw_done, 1)
                    nc.gpsimd.tensor_copy(slice_sum[:], sw[:, 0, :]).then_inc(sum_done, 1)

                    def add(tile, u):
                        pool.wait_ge(sw_done, tile + 1)
                        pool.wait_ge(sum_done, tile)
                        nc.gpsimd.tensor_tensor(slice_sum[:], slice_sum[:], sw[:, u, :], ALU.add).then_inc(sum_done, 1)
                    add(1, 1)
                    with pool.Fori(1, NT // 2) as i:
                        for u in range(2):
                            add(i * 2 + u, u)

                @block.sync
                def _(sp):
                    for dst, src in loads5:
                        sp.dma_start(dst, src).then_inc(h_in, 16)

                    def pair(i):
                        for u in range(2):
                            tile = i * 2 + u
                            if not isinstance(tile, int):
                                tile = sp.snap(tile)
                            sp.wait_ge(swt_copied, tile + 1)
                            sp.dma_start(weights_t[ds(tile, 1), :, :].rearrange("a p s -> p (a s)"), sw_t[:, u, :]).then_inc(swt_stored[u], 16)
                    loop(sp, NT // 2, pair)
                    for u in range(2):
                        sp.wait_ge(swt_stored[u], 16 * (NT // 2))

        z_out = sb("z_out", [P, 4, C])
        with ExitStack() as c5:
            def w5(name, shape):
                return sb(name, shape, c=c5)
            sum_row = w5("sum_row", [1, S])
            rsum, u_sb, u_t = w5("rsum", [L, H]), w5("u_sb", [L, S]), w5("u_t", [P, 4, L])
            pad_x, pad_bc = w5("pad_x", [P, 4, L + KC - 1]), w5("pad_bc", [NS, 2, L + KC - 1])
            conv_x, conv_bc = w5("conv_x", [P, 4, L]), w5("conv_bc", [NS, 2, L])
            tap_x, tap_bc = w5("tap_x", [P, 4, L]), w5("tap_bc", [NS, 2, L])
            act_x, act_bc = w5("act_x", [P, 4, L]), w5("act_bc", [NS, 2, L])
            dt, dt_abs, dt_exp, dt_one, dt_log = [w5(f"dt{i}", [L, 2 * H]) for i in range(5)]
            da, da_wide = w5("da", [L, 2 * H]), w5("da_wide", [L, 2 * H, L])
            cum, decay = w5("cum", [L, 2 * H]), w5("decay", [L, 2 * H, L])
            cb, mix, x_row = w5("cb", [L, L]), w5("mix", [L, H, L]), w5("x_row", [L, S])
            gain, y_sb, gate, sq = w5("gain", [L, H]), w5("y_sb", [L, S]), w5("gate", [L, S]), w5("sq", [L, S])
            ms, y_t, pairs = w5("ms", [L, 4]), w5("y_t", [P, 4, L]), w5("pairs", [P, 4, P])
            bank = [ps(f"bank{i}", [P, 512], c5) for i in range(8)]

            hp, ha, hv = sem("hydra_pe"), sem("hydra_act"), sem("hydra_dve")
            h3 = lambda ap: ap.rearrange("p (h g) -> p h g", h=H)
            b4 = lambda ap: ap.rearrange("p (b l) -> p b l", b=4)
            mid = lambda ap, n, m: ap.unsqueeze(1).broadcast_to([m, n, ap.shape[1]])
            last = lambda ap, n: ap.unsqueeze(2).broadcast_to([ap.shape[0], ap.shape[1], n])

            with nc.Block() as block:
                @block.sync
                def _(sp):
                    for u in range(4):
                        sp.dma_start(wt[:, u, :], weights_t[u, :, :]).then_inc(wt_in[u], 16)

                @block.tensor
                def _(pe):
                    pe.wait_ge(h_in, 16 * len(loads5))
                    for h in range(H):
                        pe.matmul(bank[0][0:L, h:h + 1], slice_sum[:, h * G:(h + 1) * G], ones[:, 0:1], start=True, stop=True)
                    pe.matmul(bank[1][0:1, :], ones[:, 0:1], slice_sum[:], start=True, stop=True).then_inc(hp, 1)
                    pe.wait_ge(t1_copied, 2)
                    pe.wait_ge(ha, 1)
                    for h in range(H):
                        g = slice(h * G, (h + 1) * G)
                        for b in range(2):
                            pe.matmul(bank[2][0:L, g], t1[:, b, g], wfx_t[:, b, g], start=b == 0, stop=False)
                        mm = pe.matmul(bank[2][0:L, g], sum_row[0:1, g], b_fx[0:1, g], start=False, stop=True)
                    mm.then_inc(hp, 1)
                    pe.wait_ge(hv, 3)
                    for b in range(4):
                        mm = pe.transpose(bank[3][:, b * L:(b + 1) * L], u_sb[:, b * P:(b + 1) * P], ident[0:L, 0:L])
                    mm.then_inc(hp, 1)
                    pe.wait_ge(ha, 2)
                    for b in range(4):
                        pe.matmul(bank[4][0:L, :], u_t[:, b, :], in_wt[:, b, 0:S], start=b == 0, stop=b == 3)
                    for b in range(4):
                        pe.matmul(bank[5][0:L, 0:2 * H], u_t[:, b, :], in_wt[:, b, DT0:IN], start=b == 0, stop=b == 3)
                    for q in range(4):
                        for b in range(4):
                            pe.matmul(bank[6][:, q * L:(q + 1) * L], in_wt[:, b, X0 + q * P:X0 + (q + 1) * P], u_t[:, b, :],
                                      start=b == 0, stop=b == 3)
                    for q in range(2):
                        for b in range(4):
                            mm = pe.matmul(bank[7][0:NS, q * L:(q + 1) * L], in_wt[:, b, B0 + q * NS:B0 + (q + 1) * NS],
                                           u_t[:, b, :], start=b == 0, stop=b == 3)
                    mm.then_inc(hp, 1)
                    pe.wait_ge(hv, NV_DA)
                    pe.matmul(bank[0][0:L, 0:H], upto[:], da[:, 0:H], start=True, stop=True)
                    pe.matmul(bank[0][0:L, H:2 * H], onward[:], da[:, H:2 * H], start=True, stop=True)
                    for h in range(H):
                        pe.matmul(bank[1][0:L, h * L:(h + 1) * L], da_wide[:, h, :], upto[:], start=True, stop=True)
                        mm = pe.matmul(bank[2][0:L, h * L:(h + 1) * L], da_wide[:, H + h, :], onward[:], start=True, stop=True)
                    mm.then_inc(hp, 1)
                    pe.wait_ge(hv, NV_ACT)
                    pe.matmul(bank[3][0:L, 0:L], act_bc[:, 0, :], act_bc[:, 1, :], start=True, stop=True)
                    for b in range(4):
                        pe.transpose(bank[6][0:L, b * P:(b + 1) * P], act_x[:, b, :], ident[:])
                    for b in range(4):
                        mm = pe.matmul(bank[7][0:L, 0:H], act_x[:, b, :], fcd_t[:, b, :], start=b == 0, stop=b == 3)
                    mm.then_inc(hp, 1)
                    pe.wait_ge(hv, NV_MIX)
                    for h in range(H):
                        mm = pe.matmul(bank[5][0:L, h * G:(h + 1) * G], mix[:, h, :], x_row[:, h * G:(h + 1) * G],
                                       start=True, stop=True)
                    mm.then_inc(hp, 1)
                    pe.wait_ge(hv, NV_Y)
                    for b in range(4):
                        mm = pe.transpose(bank[3][:, b * L:(b + 1) * L], y_sb[:, b * P:(b + 1) * P], ident[0:L, 0:L])
                    mm.then_inc(hp, 1)
                    pe.wait_ge(ha, NA_YT)
                    for q in range(4):
                        for b in range(4):
                            mm = pe.matmul(bank[0][:, q * L:(q + 1) * L], how_t[:, b, q * P:(q + 1) * P], y_t[:, b, :],
                                           start=b == 0, stop=b == 3)
                    mm.then_inc(hp, 1)
                    pe.wait_ge(hv, NV_Y + 1)
                    for q in range(4):
                        mm = pe.matmul(bank[1 + q // 2][:, (q % 2) * C:(q % 2 + 1) * C], pairs[:, q, :], ow_t[:, q, :],
                                       start=True, stop=True)
                    mm.then_inc(hp, 1)

                @block.scalar
                def _(act):
                    step = Steps(act, ha)
                    act.wait_ge(h_in, 16 * len(loads5))
                    act.wait_ge(hp, 1)
                    step(nc.scalar.copy(sum_row[:], bank[1][0:1, :]))
                    act.wait_ge(hp, 3)
                    step(nc.scalar.copy(u_t[:].rearrange("p b l -> p (b l)"), bank[3][:, 0:4 * L]))
                    step(nc.scalar.activation(a_log[:], a_log[:], ACT.Exp))
                    act.wait_ge(hv, NV_ABS)
                    step(nc.scalar.activation(dt_exp[:], dt_abs[:], ACT.Exp, scale=-1.0))
                    act.wait_ge(hv, NV_ABS + 1)
                    step(nc.scalar.activation(dt_log[:], dt_one[:], ACT.Ln))
                    act.wait_ge(hv, NV_CONV)
                    nc.scalar.activation(tap_x[:], conv_x[:], ACT.Exp, scale=-1.0)
                    step(nc.scalar.activation(tap_bc[:], conv_bc[:], ACT.Exp, scale=-1.0))
                    step(nc.scalar.activation(gate[:], bank[4][0:L, :], ACT.Exp, scale=-1.0))
                    act.wait_ge(hp, 6)
                    step(nc.scalar.copy(x_row[:], bank[6][0:L, :]))
                    act.wait_ge(hv, NV_DECAY)
                    step(nc.scalar.activation(decay[:], decay[:], ACT.Exp))
                    act.wait_ge(hv, NV_MS)
                    step(nc.scalar.activation(ms[:, 2:3], ms[:, 1:2], ACT.Sqrt))
                    act.wait_ge(hp, 8)
                    step(nc.scalar.copy(y_t[:].rearrange("p b l -> p (b l)"), bank[3][:, 0:4 * L]))
                    act.wait_ge(hp, 10)
                    for q in range(2):
                        step(nc.scalar.copy(z_out[:, 2 * q:2 * q + 2, :].rearrange("p a c -> p (a c)"), bank[1 + q][:]))

                @block.vector
                def _(dve):
                    step = Steps(dve, hv)
                    v = nc.vector
                    dve.wait_ge(h_in, 16 * len(loads5))
                    dve.wait_ge(hp, 1)
                    step(v.tensor_scalar(rsum[:], bank[0][0:L, 0:H], 1e-5, None, ALU.add))
                    step(v.reciprocal(rsum[:], rsum[:]))
                    dve.wait_ge(hp, 2)
                    step(v.tensor_tensor(h3(u_sb[:]), h3(bank[2][0:L, :]), last(rsum[:], G), ALU.mult))
                    assert step.n == 3
                    step(v.memset(pad_x[:], 0.0))
                    step(v.memset(pad_bc[:], 0.0))
                    dve.wait_ge(hp, 4)
                    step(v.tensor_tensor(dt[:], bank[5][0:L, 0:2 * H], dt_bias[:], ALU.add))
                    step(v.scalar_tensor_tensor(dt_abs[:], dt[:], -1.0, dt[:], ALU.mult, ALU.max))
                    assert step.n == NV_ABS
                    dve.wait_ge(ha, 4)
                    step(v.tensor_scalar(dt_one[:], dt_exp[:], 1.0, None, ALU.add))
                    step(v.tensor_scalar(dt_abs[:], dt_one[:], -1.0, None, ALU.add))
                    step(v.tensor_tensor(dt_exp[:], dt_exp[:], dt_abs[:], ALU.subtract))
                    step(v.reciprocal(dt_abs[:], dt_one[:]))
                    step(v.tensor_tensor(dt_exp[:], dt_exp[:], dt_abs[:], ALU.mult))
                    step(v.scalar_tensor_tensor(dt[:], dt[:], 0.0, dt_exp[:], ALU.max, ALU.add))
                    dve.wait_ge(ha, 5)
                    step(v.tensor_tensor(dt[:], dt[:], dt_log[:], ALU.add))
                    step(v.scalar_tensor_tensor(da[:].rearrange("p (a h) -> p a h", a=2), dt[:].rearrange("p (a h) -> p a h", a=2),
                                                -1.0, mid(a_log[:], 2, L), ALU.mult, ALU.mult))
                    step(v.tensor_copy(da_wide[:], last(da[:], L)))
                    assert step.n == NV_DA, step.n
                    step(v.tensor_copy(pad_x[:, :, KC - 1:], b4(bank[6][:, 0:4 * L])))
                    step(v.tensor_copy(pad_bc[:, :, KC - 1:], bank[7][0:NS, 0:2 * L].rearrange("p (b l) -> p b l", b=2)))
                    for pad, cw, bias, conv, tap in ((pad_x, cw_x, cb_x, conv_x, tap_x), (pad_bc, cw_bc, cb_bc, conv_bc, tap_bc)):
                        step(v.tensor_tensor(conv[:], pad[:, :, 0:L], last(cw[:, :, 0], L), ALU.mult))
                        for k in range(1, KC):
                            step(v.tensor_tensor(tap[:], pad[:, :, k:k + L], last(cw[:, :, k], L), ALU.mult))
                            step(v.tensor_tensor(conv[:], conv[:], tap[:], ALU.add))
                        step(v.tensor_tensor(conv[:], conv[:], last(bias[:], L), ALU.add))
                    assert step.n == NV_CONV, step.n
                    dve.wait_ge(ha, 6)
                    for conv, tap, out in ((conv_x, tap_x, act_x), (conv_bc, tap_bc, act_bc)):
                        step(v.tensor_scalar(tap[:], tap[:], 1.0, None, ALU.add))
                        step(v.reciprocal(tap[:], tap[:]))
                        step(v.tensor_tensor(out[:], conv[:], tap[:], ALU.mult))
                    assert step.n == NV_ACT, step.n
                    dve.wait_ge(hp, 5)
                    step(v.tensor_copy(cum[:], bank[0][0:L, 0:2 * H]))
                    for a in range(2):
                        step(v.tensor_tensor(decay[:, a * H:(a + 1) * H, :], bank[1 + a][0:L, :].rearrange("p (h l) -> p h l", h=H),
                                             last(cum[:, a * H:(a + 1) * H], L), ALU.subtract))
                    step(v.tensor_scalar(decay[:], decay[:], 0.0, None, ALU.min))
                    assert step.n == NV_DECAY, step.n
                    dve.wait_ge(ha, 9)
                    dve.wait_ge(hp, 6)
                    step(v.tensor_copy(cb[:], bank[3][0:L, 0:L]))
                    for a, mask in ((0, upto), (1, onward)):
                        part = decay[:, a * H:(a + 1) * H, :]
                        step(v.tensor_tensor(part, part, mid(mask[:], H, L), ALU.mult))
                        step(v.tensor_tensor(part, part, mid(cb[:], H, L), ALU.mult))
                        step(v.tensor_tensor(part, part, last(dt[:, a * H:(a + 1) * H], L), ALU.mult))
                    step(v.memset(mix[:], 0.0))
                    step(v.tensor_copy(mix[:, :, 1:L], decay[:, 0:H, 0:L - 1]))
                    step(v.tensor_tensor(mix[:, :, 0:L - 1], mix[:, :, 0:L - 1], decay[:, H:2 * H, 1:L], ALU.add))
                    assert step.n == NV_MIX, step.n
                    step(v.tensor_tensor(gain[:], bank[7][0:L, 0:H], d_skip[:], ALU.add))
                    step(v.tensor_tensor(h3(sq[:]), h3(x_row[:]), last(gain[:], G), ALU.mult))
                    step(v.tensor_scalar(gate[:], gate[:], 1.0, None, ALU.add))
                    step(v.reciprocal(gate[:], gate[:]))
                    step(v.tensor_tensor(gate[:], gate[:], bank[4][0:L, :], ALU.mult))
                    dve.wait_ge(hp, 7)
                    step(v.tensor_tensor(y_sb[:], sq[:], bank[5][0:L, :], ALU.add))
                    step(v.tensor_tensor(y_sb[:], y_sb[:], gate[:], ALU.mult))
                    step(v.tensor_tensor(sq[:], y_sb[:], y_sb[:], ALU.mult))
                    step(v.tensor_reduce(ms[:, 0:1], sq[:], AX.X, ALU.add))
                    step(v.tensor_scalar(ms[:, 1:2], ms[:, 0:1], 1.0 / S, EPS, ALU.mult, ALU.add))
                    assert step.n == NV_MS, step.n
                    dve.wait_ge(ha, 10)
                    step(v.reciprocal(ms[:, 3:4], ms[:, 2:3]))
                    step(v.tensor_scalar(y_sb[:], y_sb[:], ms[:, 3:4], None, ALU.mult))
                    step(v.tensor_tensor(y_sb[:], y_sb[:], norm_w[:], ALU.mult))
                    step(v.memset(pairs[:], 0.0))
                    assert step.n == NV_Y, step.n
                    dve.wait_ge(hp, 9)
                    for a in range(2):
                        ins = v.tensor_copy(pairs[a * L:(a + 1) * L, :, a * L:(a + 1) * L],
                                            b4(bank[0][a * L:(a + 1) * L, 0:4 * L]))
                    step(ins)

        with ExitStack() as c6:
            ob = sb("ob", [P, 2, C], c=c6)
            p_y = [ps(f"p_y{u}", [P, C], c6) for u in range(2)]
            biased = sem("biased")
            y_done, y_added = sem("y_done"), sem("y_added")
            y_stored = [sem(f"y_stored{u}") for u in range(2)]
            with nc.Block() as block:
                @block.sync
                def _(sp):
                    with sp.Fori(1, NT // 4) as i:
                        for u in range(4):
                            at = sp.snap(i * 4 + u)
                            sp.wait_ge(y_done, i * 4 + u - 3)
                            sp.dma_start(wt[:, u, :], weights_t[ds(at, 1), :, :].rearrange("a p s -> p (a s)")).then_inc(wt_in[u], 16)

                @block.tensor
                def _(pe):
                    def four(i):
                        for u in range(4):
                            tile = i * 4 + u
                            pe.wait_ge(wt_in[u], (i + 1) * 16)
                            wait(pe, y_added, tile - 1)
                            for q in range(4):
                                mm = pe.matmul(p_y[u % 2][:], wt[:, u, q * P:(q + 1) * P], z_out[:, q, :],
                                               start=q == 0, stop=q == 3)
                            mm.then_inc(y_done, 1)
                    loop(pe, NT // 4, four)

                @block.vector
                def _(dve):
                    def pair(i):
                        for u in range(2):
                            tile = i * 2 + u
                            wait(dve, y_stored[u], i * 16)
                            dve.wait_ge(y_done, tile + 1)
                            dve.wait_ge(biased, tile + 1)
                            nc.vector.tensor_tensor(ob[:, u, :], flat(x_sb[:, ds(tile, 1), :]), p_y[u][:],
                                                    ALU.add).then_inc(y_added, 1)
                    loop(dve, NT // 2, pair)

                @block.gpsimd
                def _(pool):
                    pool.wait_ge(h_in, 16 * len(loads5))
                    with pool.Fori(0, NT) as tile:
                        xt = flat(x_sb[:, ds(tile, 1), :])
                        nc.gpsimd.tensor_tensor(xt, xt, out_b[:], ALU.add).then_inc(biased, 1)

                @block.scalar
                def _(act):
                    def pair(i):
                        for u in range(2):
                            tile = i * 2 + u
                            rows = tile * P
                            rows = rows if isinstance(rows, int) else act.snap(rows)
                            act.wait_ge(y_added, tile + 1)
                            act.dma_start(t["out"][ds(rows, P), :], ob[:, u, :]).then_inc(y_stored[u], 16)
                    loop(act, NT // 2, pair)
                    for u in range(2):
                        act.wait_ge(y_stored[u], 16 * (NT // 2))


def pick(inputs):
    g = {k: np.asarray(v) for k, v in inputs.items()}
    n = g["x"].shape[0]

    def rows(v, m=P):
        return np.broadcast_to(v.reshape(1, -1), (m, v.size))

    a_bd = np.zeros((H * D, 2 * H), g["x"].dtype)
    for h in range(H):
        a_bd[h * D:(h + 1) * D, h] = g["L0_gnn_a_dst"][h]
        a_bd[h * D:(h + 1) * D, H + h] = g["L0_gnn_a_src"][h]
    f = "L0_ffn_"
    b = chunk_bounds(n)
    t = {
        "x": g["x"], "adj": g["adj"],
        "ident": np.eye(P, dtype=np.float32), "ones": np.ones((P, P), np.float32),
        "cand_base": rows(np.repeat(np.asarray(b[:-1], np.float32) + 1, 8)),
        "upto": np.triu(np.ones((G, G), np.float32)), "onward": np.tril(np.ones((G, G), np.float32)),
        "W": g["L0_gnn_W"], "W_t": g["L0_gnn_W"].T, "Wr_t": g["L0_gnn_Wr"].T, "a_bd": a_bd,
        "br": rows(g["L0_gnn_br"]), "be": rows(g["L0_gnn_be"]), "We": rows(g["L0_gnn_We"]),
        "W_x": g[f + "W_x"], "W_slice_t": g[f + "W_slice"].T, "b_x_t": g[f + "b_x"].reshape(H, G).T,
        "b_slice": rows(g[f + "b_slice"]), "temp": rows(g[f + "temperature"]),
        "W_fx_t": g[f + "W_fx"].T, "b_fx": g[f + "b_fx"].reshape(1, S),
        "hy_in_t": g[f + "hy_in_w"].T, "hy_out_t": g[f + "hy_out_w"].T, "out_w_t": g[f + "out_w"].T,
        "fcD_t": g[f + "hy_fcD_w"].T, "conv_w": g[f + "hy_conv_w"], "conv_b_x": g[f + "hy_conv_b"][:S].reshape(4, P).T,
        "conv_b_bc": g[f + "hy_conv_b"][S:].reshape(2, NS).T,
        "dt_bias": rows(np.concatenate([g[f + "hy_dt_bias"]] * 2), G), "A_log": rows(g[f + "hy_A_log"], G),
        "hy_D": rows(g[f + "hy_D"], G), "norm_w": rows(g[f + "hy_norm_w"], G), "out_b": rows(g[f + "out_b"]),
    }
    return {k: np.ascontiguousarray(v) for k, v in t.items()}


def kernel(**inputs):
    import concourse.bacc as bacc
    from concourse.bass_utils import run_bass_kernel_spmd

    arrays = pick(inputs)
    nc = bacc.Bacc("TRN2", target_bir_lowering=False, num_devices=1)
    t = {k: nc.dram_tensor(f"in_{k}", v.shape, mybir.dt.from_np(v.dtype), kind="ExternalInput").ap() for k, v in arrays.items()}
    t["out"] = nc.dram_tensor("out", arrays["x"].shape, F32, kind="ExternalOutput").ap()
    build(nc, t)
    r = run_bass_kernel_spmd(nc, [{f"in_{k}": v for k, v in arrays.items()}], core_ids=[0])
    return r.results[0]["out"]
```
